# Optimizing a Trainium2 kernel written in Bass

```python
import numpy as np
import jax
import jax.numpy as jnp

def _softmax(x, axis=-1):
    return jax.nn.softmax(x, axis=axis)
def _gelu(x):
    return jax.nn.gelu(x, approximate=True)
def _silu(x):
    return jax.nn.silu(x)
def _sigmoid(x):
    return jax.nn.sigmoid(x)
def _layernorm(x, axis=-1, eps=1e-5):
    m = jnp.mean(x, axis=axis, keepdims=True)
    v = jnp.var(x, axis=axis, keepdims=True)
    return (x - m) / jnp.sqrt(v + eps)
def _scatter_add(tgt, idx, src, axis=0):
    return tgt.at[idx].add(src)
def _segment_sum(src, seg, n):
    return jax.ops.segment_sum(src, seg, n)

kernel_name = 'mk_conv_seq_d4_conv_nhwc128_d1afa3'

def setup_inputs(seed: int = 0):
    np.random.seed(seed)
    _w = jnp.asarray
    def _rec_inputs():
        import jax
        import jax.numpy as jnp
        _gk = jax.random.key(seed)
        x = -0.0005207 + 1.001 * jax.random.normal(jax.random.fold_in(_gk, 1), (4, 64, 64, 128), jnp.float32)
        return x
    x = _rec_inputs()
    def _L0_conv_setup():
        import jax, jax.numpy as jnp
        import numpy as np
        DIM = 128
        KS = 7
        HEADS = 4
        HEAD_DIM = DIM // HEADS

        def _neighborhood_attention(x, qkv_w, qkv_b, proj_w, proj_b, rpb):
            B, H, W, C = x.shape
            k = KS
            qkv = (x @ qkv_w + qkv_b).reshape(B, H, W, 3, HEADS, HEAD_DIM)
            q = qkv[..., 0, :, :] * HEAD_DIM ** (-0.5)
            kk = qkv[..., 1, :, :]
            v = qkv[..., 2, :, :]
            sh = jnp.clip(jnp.arange(H) - k // 2, 0, H - k)
            sw = jnp.clip(jnp.arange(W) - k // 2, 0, W - k)
            idx_h = sh[:, None] + jnp.arange(k)[None, :]
            idx_w = sw[:, None] + jnp.arange(k)[None, :]
            kwin = kk[:, idx_h[:, None, :, None], idx_w[None, :, None, :]]
            vwin = v[:, idx_h[:, None, :, None], idx_w[None, :, None, :]]
            bih = idx_h - jnp.arange(H)[:, None] + (k - 1)
            biw = idx_w - jnp.arange(W)[:, None] + (k - 1)
            bias = rpb[:, bih[:, None, :, None], biw[None, :, None, :]]
            bias = jnp.transpose(bias, (1, 2, 0, 3, 4))
            scores = jnp.einsum('bxyhd,bxyklhd->bxyhkl', q, kwin) + bias[None]
            attn = jax.nn.softmax(scores.reshape(B, H, W, HEADS, k * k), axis=-1)
            attn = attn.reshape(B, H, W, HEADS, k, k)
            out = jnp.einsum('bxyhkl,bxyklhd->bxyhd', attn, vwin).reshape(B, H, W, C)
            return out @ proj_w + proj_b
        key = jax.random.key(seed)
        ks = jax.random.split(key, 10)
        B, H, W, C = (4, 64, 64, DIM)
        s = 0.02
        return {'x': jax.random.normal(ks[0], (B, H, W, C), jnp.float32), 'qkv_w': jax.random.normal(ks[1], (C, 3 * C), jnp.float32) * s, 'qkv_b': jnp.zeros((3 * C,), jnp.float32), 'proj_w': jax.random.normal(ks[2], (C, C), jnp.float32) * s, 'proj_b': jnp.zeros((C,), jnp.float32), 'rpb': jax.random.normal(ks[3], (HEADS, 2 * KS - 1, 2 * KS - 1), jnp.float32) * s, 'g1_w': jax.random.normal(ks[4], (C, C // 2), jnp.float32) * s, 'g1_b': jnp.zeros((C // 2,), jnp.float32), 'g2_w': jax.random.normal(ks[5], (C // 2, 1), jnp.float32) * s, 'g2_b': jnp.zeros((1,), jnp.float32)}
    _L0_conv_all = _L0_conv_setup()
    _L0_conv_in = {k: v for k, v in _L0_conv_all.items() if k in ('qkv_w', 'qkv_b', 'proj_w', 'proj_b', 'rpb', 'g1_w', 'g1_b', 'g2_w', 'g2_b', )}
    del _L0_conv_all

    def _L1_conv_setup():
        import jax, jax.numpy as jnp
        import numpy as np
        GROUPS = 32
        EPS = 1e-06

        def group_norm(x, scale, bias):
            B, H, W, C = x.shape
            xg = x.reshape(B, H, W, GROUPS, C // GROUPS)
            mean = jnp.mean(xg, axis=(1, 2, 4), keepdims=True)
            var = jnp.var(xg, axis=(1, 2, 4), keepdims=True)
            xn = (xg - mean) * jax.lax.rsqrt(var + EPS)
            return xn.reshape(B, H, W, C) * scale + bias
        key = jax.random.key(seed)
        ks = jax.random.split(key, 8)
        B, H, W, C = (8, 64, 64, 128)
        s = C ** (-0.5)
        return {'x': jax.random.normal(ks[0], (B, H, W, C), dtype=jnp.float32), 'gn_scale': jnp.ones((C,), dtype=jnp.float32), 'gn_bias': jnp.zeros((C,), dtype=jnp.float32), 'wq': jax.random.normal(ks[1], (C, C), dtype=jnp.float32) * s, 'bq': jnp.zeros((C,), dtype=jnp.float32), 'wk': jax.random.normal(ks[2], (C, C), dtype=jnp.float32) * s, 'bk': jnp.zeros((C,), dtype=jnp.float32), 'wv': jax.random.normal(ks[3], (C, C), dtype=jnp.float32) * s, 'bv': jnp.zeros((C,), dtype=jnp.float32), 'wo': jax.random.normal(ks[4], (C, C), dtype=jnp.float32) * s, 'bo': jnp.zeros((C,), dtype=jnp.float32)}
    _L1_conv_all = _L1_conv_setup()
    _L1_conv_in = {k: v for k, v in _L1_conv_all.items() if k in ('gn_scale', 'gn_bias', 'wq', 'bq', 'wk', 'bk', 'wv', 'bv', 'wo', 'bo', )}
    del _L1_conv_all

    def _L2_conv_setup():
        import jax, jax.numpy as jnp
        import numpy as np
        LN_EPS = 1e-05

        def _layer_norm(x, scale, bias):
            mu = jnp.mean(x, axis=-1, keepdims=True)
            var = jnp.mean(jnp.square(x - mu), axis=-1, keepdims=True)
            return (x - mu) * jax.lax.rsqrt(var + LN_EPS) * scale + bias
        key = jax.random.key(seed)
        ks = jax.random.split(key, 8)
        B, N, C, H = (1, 384, 128, 128)
        s_in = 1.0 / np.sqrt(C)
        s_h = 1.0 / np.sqrt(H)
        return {'pair': jax.random.normal(ks[0], (B, N, N, C), jnp.float32), 'W_left': jax.random.normal(ks[1], (C, H), jnp.float32) * s_in, 'b_left': jnp.zeros((H,), jnp.float32), 'W_right': jax.random.normal(ks[2], (C, H), jnp.float32) * s_in, 'b_right': jnp.zeros((H,), jnp.float32), 'W_gate': jax.random.normal(ks[3], (C, H), jnp.float32) * s_in, 'b_gate': jnp.zeros((H,), jnp.float32), 'W_eq': jax.random.normal(ks[4], (C, H), jnp.float32) * s_in, 'b_eq': jnp.zeros((H,), jnp.float32), 'W_out': jax.random.normal(ks[5], (H, C), jnp.float32) * s_h, 'b_out': jnp.zeros((C,), jnp.float32), 'ln_scale': jnp.ones((C,), jnp.float32), 'ln_bias': jnp.zeros((C,), jnp.float32)}
    _L2_conv_all = _L2_conv_setup()
    _L2_conv_in = {k: v for k, v in _L2_conv_all.items() if k in ('W_left', 'b_left', 'W_right', 'b_right', 'W_gate', 'b_gate', 'W_eq', 'b_eq', 'W_out', 'b_out', 'ln_scale', 'ln_bias', )}
    del _L2_conv_all

    def _L3_conv_setup():
        import jax, jax.numpy as jnp
        import numpy as np
        D_MODEL = 128
        D_STATE = 1
        D_INNER = 256
        DT_RANK = 8
        K = 4
        B_SZ, H_SZ, W_SZ = (4, 128, 128)

        def _selective_scan(u, delta, A, Bm, Cm, Dv, dbias):
            delta = jax.nn.softplus(delta + dbias[:, None, :, None])
            du = delta * u
            d_l = jnp.moveaxis(delta, -1, 0)
            du_l = jnp.moveaxis(du, -1, 0)
            B_l = jnp.moveaxis(Bm, -1, 0)
            C_l = jnp.moveaxis(Cm, -1, 0)
            x0 = jnp.zeros(delta.shape[:3] + (A.shape[-1],), delta.dtype)

            def step(xc, inp):
                dlt, dut, Bt, Ct = inp
                dA = jnp.exp(dlt[..., None] * A[:, None])
                xc = dA * xc + dut[..., None] * Bt[:, :, None, :]
                y = jnp.einsum('kbcn,kbn->kbc', xc, Ct)
                return (xc, y)
            _, ys = jax.lax.scan(step, x0, (d_l, du_l, B_l, C_l))
            y = jnp.moveaxis(ys, 0, -1)
            return y + u * Dv[:, None, :, None]
        key = jax.random.key(seed)
        ks = jax.random.split(key, 6)
        x = jax.random.normal(ks[0], (B_SZ, H_SZ, W_SZ, D_MODEL), jnp.float32)
        Win = jax.random.normal(ks[1], (D_MODEL, 2 * D_INNER), jnp.float32) / np.sqrt(D_MODEL).astype(np.float32)
        conv_w = jax.random.normal(ks[2], (D_INNER, 1, 3, 3), jnp.float32) / 3.0
        conv_b = jnp.zeros((D_INNER,), jnp.float32)
        Wxproj = jax.random.normal(ks[3], (D_INNER, DT_RANK + 2 * D_STATE), jnp.float32) / np.sqrt(D_INNER).astype(np.float32)
        dt_weight = jax.random.normal(ks[4], (K, D_INNER, DT_RANK), jnp.float32) / np.sqrt(DT_RANK).astype(np.float32)
        A_log = jnp.tile(jnp.log(jnp.arange(1, D_STATE + 1, dtype=jnp.float32))[None, :], (K * D_INNER, 1))
        D_param = jnp.ones((K * D_INNER,), jnp.float32)
        dt_bias = jnp.zeros((K * D_INNER,), jnp.float32)
        gamma = jnp.ones((D_INNER,), jnp.float32)
        beta = jnp.zeros((D_INNER,), jnp.float32)
        Wout = jax.random.normal(ks[5], (D_INNER, D_MODEL), jnp.float32) / np.sqrt(D_INNER).astype(np.float32)
        return dict(x=x, Win=Win, conv_w=conv_w, conv_b=conv_b, Wxproj=Wxproj, dt_weight=dt_weight, A_log=A_log, D_param=D_param, dt_bias=dt_bias, gamma=gamma, beta=beta, Wout=Wout)
    _L3_conv_all = _L3_conv_setup()
    _L3_conv_in = {k: v for k, v in _L3_conv_all.items() if k in ('Win', 'conv_w', 'conv_b', 'Wxproj', 'dt_weight', 'A_log', 'D_param', 'dt_bias', 'gamma', 'beta', 'Wout', )}
    del _L3_conv_all

    return {
        "x": x,
        "L0_conv_qkv_w": _L0_conv_in["qkv_w"],
        "L0_conv_qkv_b": _L0_conv_in["qkv_b"],
        "L0_conv_proj_w": _L0_conv_in["proj_w"],
        "L0_conv_proj_b": _L0_conv_in["proj_b"],
        "L0_conv_rpb": _L0_conv_in["rpb"],
        "L0_conv_g1_w": _L0_conv_in["g1_w"],
        "L0_conv_g1_b": _L0_conv_in["g1_b"],
        "L0_conv_g2_w": _L0_conv_in["g2_w"],
        "L0_conv_g2_b": _L0_conv_in["g2_b"],
        "L1_conv_gn_scale": _L1_conv_in["gn_scale"],
        "L1_conv_gn_bias": _L1_conv_in["gn_bias"],
        "L1_conv_wq": _L1_conv_in["wq"],
        "L1_conv_bq": _L1_conv_in["bq"],
        "L1_conv_wk": _L1_conv_in["wk"],
        "L1_conv_bk": _L1_conv_in["bk"],
        "L1_conv_wv": _L1_conv_in["wv"],
        "L1_conv_bv": _L1_conv_in["bv"],
        "L1_conv_wo": _L1_conv_in["wo"],
        "L1_conv_bo": _L1_conv_in["bo"],
        "L2_conv_W_left": _L2_conv_in["W_left"],
        "L2_conv_b_left": _L2_conv_in["b_left"],
        "L2_conv_W_right": _L2_conv_in["W_right"],
        "L2_conv_b_right": _L2_conv_in["b_right"],
        "L2_conv_W_gate": _L2_conv_in["W_gate"],
        "L2_conv_b_gate": _L2_conv_in["b_gate"],
        "L2_conv_W_eq": _L2_conv_in["W_eq"],
        "L2_conv_b_eq": _L2_conv_in["b_eq"],
        "L2_conv_W_out": _L2_conv_in["W_out"],
        "L2_conv_b_out": _L2_conv_in["b_out"],
        "L2_conv_ln_scale": _L2_conv_in["ln_scale"],
        "L2_conv_ln_bias": _L2_conv_in["ln_bias"],
        "L3_conv_Win": _L3_conv_in["Win"],
        "L3_conv_conv_w": _L3_conv_in["conv_w"],
        "L3_conv_conv_b": _L3_conv_in["conv_b"],
        "L3_conv_Wxproj": _L3_conv_in["Wxproj"],
        "L3_conv_dt_weight": _L3_conv_in["dt_weight"],
        "L3_conv_A_log": _L3_conv_in["A_log"],
        "L3_conv_D_param": _L3_conv_in["D_param"],
        "L3_conv_dt_bias": _L3_conv_in["dt_bias"],
        "L3_conv_gamma": _L3_conv_in["gamma"],
        "L3_conv_beta": _L3_conv_in["beta"],
        "L3_conv_Wout": _L3_conv_in["Wout"],
    }

def reference(x, L0_conv_qkv_w, L0_conv_qkv_b, L0_conv_proj_w, L0_conv_proj_b, L0_conv_rpb, L0_conv_g1_w, L0_conv_g1_b, L0_conv_g2_w, L0_conv_g2_b, L1_conv_gn_scale, L1_conv_gn_bias, L1_conv_wq, L1_conv_bq, L1_conv_wk, L1_conv_bk, L1_conv_wv, L1_conv_bv, L1_conv_wo, L1_conv_bo, L2_conv_W_left, L2_conv_b_left, L2_conv_W_right, L2_conv_b_right, L2_conv_W_gate, L2_conv_b_gate, L2_conv_W_eq, L2_conv_b_eq, L2_conv_W_out, L2_conv_b_out, L2_conv_ln_scale, L2_conv_ln_bias, L3_conv_Win, L3_conv_conv_w, L3_conv_conv_b, L3_conv_Wxproj, L3_conv_dt_weight, L3_conv_A_log, L3_conv_D_param, L3_conv_dt_bias, L3_conv_gamma, L3_conv_beta, L3_conv_Wout):
    import jax
    import jax.numpy as jnp
    def _L0_conv_ref(x, qkv_w, qkv_b, proj_w, proj_b, rpb, g1_w, g1_b, g2_w, g2_b):
        import jax, jax.numpy as jnp
        import numpy as np
        DIM = 128
        KS = 7
        HEADS = 4
        HEAD_DIM = DIM // HEADS

        def _neighborhood_attention(x, qkv_w, qkv_b, proj_w, proj_b, rpb):
            B, H, W, C = x.shape
            k = KS
            qkv = (x @ qkv_w + qkv_b).reshape(B, H, W, 3, HEADS, HEAD_DIM)
            q = qkv[..., 0, :, :] * HEAD_DIM ** (-0.5)
            kk = qkv[..., 1, :, :]
            v = qkv[..., 2, :, :]
            sh = jnp.clip(jnp.arange(H) - k // 2, 0, H - k)
            sw = jnp.clip(jnp.arange(W) - k // 2, 0, W - k)
            idx_h = sh[:, None] + jnp.arange(k)[None, :]
            idx_w = sw[:, None] + jnp.arange(k)[None, :]
            kwin = kk[:, idx_h[:, None, :, None], idx_w[None, :, None, :]]
            vwin = v[:, idx_h[:, None, :, None], idx_w[None, :, None, :]]
            bih = idx_h - jnp.arange(H)[:, None] + (k - 1)
            biw = idx_w - jnp.arange(W)[:, None] + (k - 1)
            bias = rpb[:, bih[:, None, :, None], biw[None, :, None, :]]
            bias = jnp.transpose(bias, (1, 2, 0, 3, 4))
            scores = jnp.einsum('bxyhd,bxyklhd->bxyhkl', q, kwin) + bias[None]
            attn = jax.nn.softmax(scores.reshape(B, H, W, HEADS, k * k), axis=-1)
            attn = attn.reshape(B, H, W, HEADS, k, k)
            out = jnp.einsum('bxyhkl,bxyklhd->bxyhd', attn, vwin).reshape(B, H, W, C)
            return out @ proj_w + proj_b
        attn_out = _neighborhood_attention(x, qkv_w, qkv_b, proj_w, proj_b, rpb)
        gate = jax.nn.sigmoid(jax.nn.relu(x @ g1_w + g1_b) @ g2_w + g2_b)
        return attn_out * gate + x

    def _L1_conv_ref(x, gn_scale, gn_bias, wq, bq, wk, bk, wv, bv, wo, bo):
        import jax, jax.numpy as jnp
        import numpy as np
        GROUPS = 32
        EPS = 1e-06

        def group_norm(x, scale, bias):
            B, H, W, C = x.shape
            xg = x.reshape(B, H, W, GROUPS, C // GROUPS)
            mean = jnp.mean(xg, axis=(1, 2, 4), keepdims=True)
            var = jnp.var(xg, axis=(1, 2, 4), keepdims=True)
            xn = (xg - mean) * jax.lax.rsqrt(var + EPS)
            return xn.reshape(B, H, W, C) * scale + bias
        B, H, W, C = x.shape
        N = H * W
        h = group_norm(x, gn_scale, gn_bias)
        hf = h.reshape(B, N, C)
        q = hf @ wq + bq
        k = hf @ wk + bk
        v = hf @ wv + bv
        w_ = jnp.einsum('bqd,bkd->bqk', q, k) * C ** (-0.5)
        w_ = jax.nn.softmax(w_, axis=2)
        o = jnp.einsum('bqk,bkd->bqd', w_, v)
        o = o @ wo + bo
        return x + o.reshape(B, H, W, C)

    def _L2_conv_ref(pair, W_left, b_left, W_right, b_right, W_gate, b_gate, W_eq, b_eq, W_out, b_out, ln_scale, ln_bias):
        import jax, jax.numpy as jnp
        import numpy as np
        LN_EPS = 1e-05

        def _layer_norm(x, scale, bias):
            mu = jnp.mean(x, axis=-1, keepdims=True)
            var = jnp.mean(jnp.square(x - mu), axis=-1, keepdims=True)
            return (x - mu) * jax.lax.rsqrt(var + LN_EPS) * scale + bias
        left = pair @ W_left + b_left
        right = pair @ W_right + b_right
        gate = jax.nn.sigmoid(pair @ W_gate + b_gate)
        left = left + (pair @ W_eq + b_eq)
        right_sum = jnp.sum(right, axis=2, keepdims=True)
        out = left * right_sum
        out = out * gate
        out = out @ W_out + b_out
        return _layer_norm(out + pair, ln_scale, ln_bias)

    def _L3_conv_ref(x, Win, conv_w, conv_b, Wxproj, dt_weight, A_log, D_param, dt_bias, gamma, beta, Wout):
        import jax, jax.numpy as jnp
        import numpy as np
        D_MODEL = 128
        D_STATE = 1
        D_INNER = 256
        DT_RANK = 8
        K = 4
        B_SZ, H_SZ, W_SZ = (4, 128, 128)

        def _selective_scan(u, delta, A, Bm, Cm, Dv, dbias):
            delta = jax.nn.softplus(delta + dbias[:, None, :, None])
            du = delta * u
            d_l = jnp.moveaxis(delta, -1, 0)
            du_l = jnp.moveaxis(du, -1, 0)
            B_l = jnp.moveaxis(Bm, -1, 0)
            C_l = jnp.moveaxis(Cm, -1, 0)
            x0 = jnp.zeros(delta.shape[:3] + (A.shape[-1],), delta.dtype)

            def step(xc, inp):
                dlt, dut, Bt, Ct = inp
                dA = jnp.exp(dlt[..., None] * A[:, None])
                xc = dA * xc + dut[..., None] * Bt[:, :, None, :]
                y = jnp.einsum('kbcn,kbn->kbc', xc, Ct)
                return (xc, y)
            _, ys = jax.lax.scan(step, x0, (d_l, du_l, B_l, C_l))
            y = jnp.moveaxis(ys, 0, -1)
            return y + u * Dv[:, None, :, None]
        Bb, H, W, _ = x.shape
        L = H * W
        Cd, r, N = (D_INNER, DT_RANK, D_STATE)
        xz = x @ Win
        xb, z = jnp.split(xz, 2, axis=-1)
        xb = jnp.transpose(xb, (0, 3, 1, 2))
        xb = jax.lax.conv_general_dilated(xb, conv_w, (1, 1), ((1, 1), (1, 1)), dimension_numbers=('NCHW', 'OIHW', 'NCHW'), feature_group_count=Cd)
        xb = jax.nn.silu(xb + conv_b[None, :, None, None])
        xf = xb.reshape(Bb, Cd, L)
        xt = jnp.transpose(xb, (0, 1, 3, 2)).reshape(Bb, Cd, L)
        xs = jnp.stack([xf, xf[..., ::-1], xt, xt[..., ::-1]], axis=1)
        xs_flat = xs.reshape(Bb * K, Cd, L)
        x_dbl = jnp.einsum('bcl,cd->bdl', xs_flat, Wxproj)
        dt = x_dbl[:, :r]
        Bs = x_dbl[:, r:r + N]
        Cs = x_dbl[:, r + N:]
        dt_kb = dt.reshape(K, Bb, r, L)
        dt_out = jnp.einsum('kdr,kbrl->bkdl', dt_weight, dt_kb)
        delta_kb = dt_out.reshape(Bb * K, Cd, L).reshape(K, Bb, Cd, L)
        u_kb = xs_flat.reshape(K, Bb, Cd, L)
        B_kb = Bs.reshape(K, Bb, N, L)
        C_kb = Cs.reshape(K, Bb, N, L)
        A = -jnp.exp(A_log).reshape(K, Cd, N)
        y_kb = _selective_scan(u_kb, delta_kb, A, B_kb, C_kb, D_param.reshape(K, Cd), dt_bias.reshape(K, Cd))
        ys = jnp.transpose(y_kb, (1, 0, 2, 3))
        y0 = ys[:, 0]
        y1 = ys[:, 1][..., ::-1]
        y2 = jnp.transpose(ys[:, 2].reshape(Bb, Cd, W, H), (0, 1, 3, 2)).reshape(Bb, Cd, L)
        y3 = jnp.transpose(ys[:, 3][..., ::-1].reshape(Bb, Cd, W, H), (0, 1, 3, 2)).reshape(Bb, Cd, L)
        y = (y0 + y1 + y2 + y3).transpose(0, 2, 1)
        zf = jax.nn.silu(z.reshape(Bb, L, Cd))
        yz = y * zf
        mu = yz.mean(-1, keepdims=True)
        xc = yz - mu
        var = (xc * xc).mean(-1, keepdims=True)
        yn = gamma * xc / jnp.sqrt(var + 1e-05) + beta
        out = yn @ Wout
        return out.reshape(Bb, H, W, -1)

    def _gn(v, G=32, eps=1e-5):
        B_, H_, W_, C_ = v.shape
        g = v.reshape(B_, H_, W_, G, C_ // G)
        m = jnp.mean(g, axis=(1, 2, 4), keepdims=True)
        s = jnp.var(g, axis=(1, 2, 4), keepdims=True)
        return ((g - m) / jnp.sqrt(s + eps)).reshape(v.shape)

    def _ln_c(v, eps=1e-6):
        m = jnp.mean(v, axis=-1, keepdims=True)
        s = jnp.var(v, axis=-1, keepdims=True)
        return (v - m) / jnp.sqrt(s + eps)

    def _ln_t(v, eps=1e-5):
        m = jnp.mean(v, axis=-1, keepdims=True)
        s = jnp.var(v, axis=-1, keepdims=True)
        return (v - m) / jnp.sqrt(s + eps)

    def _to_tokens(v):
        B_, H_, W_, C_ = v.shape
        return v.reshape(B_, H_ * W_, C_)
    def _from_tokens(t, like):
        return t.reshape(like.shape)

    x = _L0_conv_ref(x, L0_conv_qkv_w, L0_conv_qkv_b, L0_conv_proj_w, L0_conv_proj_b, L0_conv_rpb, L0_conv_g1_w, L0_conv_g1_b, L0_conv_g2_w, L0_conv_g2_b)
    x = _L1_conv_ref(x, L1_conv_gn_scale, L1_conv_gn_bias, L1_conv_wq, L1_conv_bq, L1_conv_wk, L1_conv_bk, L1_conv_wv, L1_conv_bv, L1_conv_wo, L1_conv_bo)
    x = _L2_conv_ref(x, L2_conv_W_left, L2_conv_b_left, L2_conv_W_right, L2_conv_b_right, L2_conv_W_gate, L2_conv_b_gate, L2_conv_W_eq, L2_conv_b_eq, L2_conv_W_out, L2_conv_b_out, L2_conv_ln_scale, L2_conv_ln_bias)
    x = _L3_conv_ref(x, L3_conv_Win, L3_conv_conv_w, L3_conv_conv_b, L3_conv_Wxproj, L3_conv_dt_weight, L3_conv_A_log, L3_conv_D_param, L3_conv_dt_bias, L3_conv_gamma, L3_conv_beta, L3_conv_Wout)
    return x


_drawn_inputs = setup_inputs


def setup_inputs(seed=0):
    import zlib

    import numpy as np

    out = dict(_drawn_inputs(seed))
    spreads = {'L0_conv_qkv_b': (0.0, 0.1),
     'L0_conv_proj_b': (0.0, 0.1),
     'L0_conv_g1_b': (0.0, 0.8),
     'L1_conv_gn_scale': (1.0, 0.2),
     'L1_conv_gn_bias': (0.0, 0.1),
     'L1_conv_bq': (0.0, 0.1),
     'L1_conv_bk': (0.0, 2.0),
     'L1_conv_bv': (0.0, 0.1),
     'L1_conv_bo': (0.0, 0.1),
     'L2_conv_b_left': (0.0, 0.1),
     'L2_conv_b_right': (0.0, 0.1),
     'L2_conv_b_gate': (0.0, 0.1),
     'L2_conv_b_eq': (0.0, 0.1),
     'L2_conv_b_out': (0.0, 0.505),
     'L2_conv_ln_scale': (1.0, 0.2),
     'L2_conv_ln_bias': (0.0, 0.1),
     'L3_conv_conv_b': (0.0, 0.1),
     'L3_conv_A_log': (0.0, 0.452),
     'L3_conv_D_param': (1.0, 0.2),
     'L3_conv_dt_bias': (0.0, 0.416),
     'L3_conv_gamma': (1.0, 0.2),
     'L3_conv_beta': (0.0, 0.1)}
    factors = {'L0_conv_qkv_w': 5.348, 'L0_conv_rpb': 30.485, 'L0_conv_g1_w': 8.0, 'L0_conv_g2_w': 8.0}
    for name, (base, spread) in spreads.items():
        noise = np.random.default_rng([zlib.crc32(name.encode()), seed]).standard_normal(out[name].shape)
        drawn = base * np.exp(spread * noise) if base else spread * noise
        out[name] = jnp.asarray(drawn.astype(out[name].dtype))
    for name, factor in factors.items():
        out[name] = (out[name] * factor).astype(out[name].dtype)
    return out
```

```python
from contextlib import ExitStack

import numpy as np
import concourse.bass as bass
from concourse import mybir

F32 = mybir.dt.float32
F32R = mybir.dt.float32r
ALU = mybir.AluOpType
ACT = mybir.ActivationFunctionType
AX = mybir.AxisListType

NI = 4
HW = 64
TOK = HW * HW
C = 128
SEMS = None


class Lane:

    def __init__(self, sem):
        self.sem, self.n, self.ops, self.seen = sem, 0, [], {}

    def wait(self, *tokens):
        for token in tokens:
            if token is None:
                continue
            sem, value = token
            if self.seen.get(id(sem), 0) < value:
                self.seen[id(sem)] = value
                self.ops.append(lambda e, s=sem, v=value: e.wait_ge(s, v))

    def do(self, f, *tokens):
        self.wait(*tokens)
        self.ops.append(f)

    def sig(self, f, *tokens):
        self.wait(*tokens)
        self.n += 1
        self.ops.append(lambda e: f(e).then_inc(self.sem, 1))
        return self.sem, self.n

    def play(self, e):
        for f in self.ops:
            f(e)


class Load:

    def __init__(self, sem):
        self.sem, self.n = sem, 0

    def dma(self, lane, dst, src, *tokens, slow=False):
        lane.wait(*tokens)
        self.n += 16
        lane.ops.append(lambda e: e.dma_start(dst, src, allow_slow_non_contiguous=slow).then_inc(self.sem, 16))
        return self.sem, self.n


class Phase:

    def __init__(self, nc, ctx, name):
        self.nc, self.ctx, self.name, self.k = nc, ctx, name, 0
        self.pe, self.act, self.dve, self.pool, self.sp = (Lane(self.sem(x)) for x in ("pe", "act", "dve", "pool", "sp"))

    def sem(self, what):
        self.k += 1
        return SEMS.enter_context(self.nc.semaphore(f"{self.name}_{what}_{self.k}"))

    def load(self, what):
        return Load(self.sem(what))

    def sb(self, name, shape, dt=F32):
        return self.ctx.enter_context(self.nc.sbuf_tensor(f"{self.name}_{name}", shape, dt))

    def ps(self, name, shape, dt=F32):
        return self.ctx.enter_context(self.nc.psum_tensor(f"{self.name}_{name}", shape, dt))

    def run(self):
        with self.nc.Block() as block:
            block.sync(lambda e: self.sp.play(e))
            block.tensor(lambda e: self.pe.play(e))
            block.scalar(lambda e: self.act.play(e))
            block.vector(lambda e: self.dve.play(e))
            block.gpsimd(lambda e: self.pool.play(e))


def layer0(nc, P, io, x1):
    pe, act, dve, pool, sp = P.pe, P.act, P.dve, P.pool, P.sp
    S32 = 32.0 ** -0.5

    ident = P.sb("ident", [128, 128])
    wqkv = P.sb("wqkv", [128, 384])
    wp = P.sb("wp", [128, 128])
    g1w = P.sb("g1w", [128, 64])
    g2w = P.sb("g2w", [64, 1])
    cols = P.sb("cols", [128, 6])
    bvb = P.sb("bvb", [128, 128])
    pbb = P.sb("pbb", [128, 128])
    bm = P.sb("bm", [128, 36, 308])
    msk = P.sb("msk", [128, 9, 308])
    xt = P.sb("xt", [128, 2, TOK])
    qt = P.sb("qt", [128, TOK])
    kt = P.sb("kt", [128, TOK])
    gt = P.sb("gt", [64, TOK])
    gate = P.sb("gate", [128, NI, 3, 32])
    xw = P.sb("xw", [128, 2, 308])
    vg = P.sb("vg", [128, 2, 3, 128])
    pr = P.sb("pr", [128, 2, 4, 308])
    st = P.sb("st", [128, 2, 16])
    ptb = P.sb("ptb", [128, 4, 384])
    on = P.sb("on", [128, 2, 128])
    ot = P.sb("ot", [128, 2, 128])
    tm = P.sb("tm", [128, 2, 128])
    xs = P.sb("xs", [128, 3, 128])
    ys = P.sb("ys", [128, 3, 128])

    psS = P.ps("S", [128, 3, 512])
    psT = P.ps("T", [128, 2, 512])
    psV = P.ps("V", [128, 512])
    psO = P.ps("O", [128, 512])
    psF = P.ps("F", [128, 512])

    lw = P.load("w")
    for dst, src in ((ident[:], io["ident"]), (wqkv[:], io["L0_conv_qkv_w"]), (wp[:], io["L0_conv_proj_w"]),
                     (g1w[:], io["L0_conv_g1_w"]), (g2w[:], io["L0_conv_g2_w"]),
                     (cols[:, 0:3], io["L0_conv_qkv_b"].rearrange("(t p) -> p t", p=128)),
                     (cols[0:64, 3:4], io["L0_conv_g1_b"].rearrange("(p a) -> p a", a=1)),
                     (cols[:, 4:5], io["L0_conv_g2_b"].rearrange("(a p) -> a p", a=1).broadcast_to([128, 1])),
                     (bvb[:], io["L0_conv_qkv_b"].rearrange("(a p) -> a p", a=1)[:, 256:384].broadcast_to([128, 128])),
                     (pbb[:], io["L0_conv_proj_b"].rearrange("(a p) -> a p", a=1).broadcast_to([128, 128]))):
        w = lw.dma(sp, dst, src, slow=True)
    lx = [P.load("x0"), P.load("x1")]
    lb = P.load("b")
    lt = [P.load("t") for _ in range(3)]
    lo = [P.load("o") for _ in range(3)]
    xin = [lx[0].dma(sp, xt[:, 0, :], io["xT"][0]), None]
    b1 = lb.dma(sp, msk[:], io["mask"].rearrange("k p n -> p k n"))
    b1 = lb.dma(sp, bm[:], io["rpbx"].rearrange("k p n -> p k n"))

    z1 = dve.sig(lambda e: e.memset(psT[:], 0.0))
    z2 = dve.sig(lambda e: e.memset(psV[:], 0.0))
    d0 = dve.sig(lambda e: e.tensor_scalar(cols[:, 0:1], cols[:, 0:1], S32, None, ALU.mult), w)
    d0 = dve.sig(lambda e: e.tensor_scalar(cols[:, 4:5], cols[:, 4:5], -1.0, None, ALU.mult), w)
    for k in range(9):
        db = dve.sig(lambda e, k=k: e.tensor_tensor(bm[:, 4 * k:4 * k + 4, :], bm[:, 4 * k:4 * k + 4, :],
                     msk[:, k:k + 1, :].broadcast_to([128, 4, 308]), ALU.add), b1)

    def img(t, b=None):
        v = t[:] if b is None else t[:, b, :]
        return v.rearrange("p (h w) -> p h w", w=HW)

    def tiled(t, sl):
        return t[:, sl].rearrange("p (t r c) -> p r t c", t=4, r=8)

    sfree = [None] * 3
    sn = [0]
    tfree = [z1, z1]
    tn = [0]
    vfree = z2
    ofree = None
    ffree = None

    def bank():
        i = sn[0] % 3
        sn[0] += 1
        return i

    prfree = [None, None]
    ptfree = [None] * 4
    vgfree = [None, None]
    xtfree = [None, None]
    outdone = [None] * 3
    qkfree = None
    lastpe = None
    onfree = [None, None]
    otfree = [None, None]
    tmtok = [None, None]
    N = NI * 32
    info = {}

    def project(b):
        nonlocal vfree
        X = xt[:, b % 2, :]
        xtok = xin[b % 2]
        ready = []
        for ch in range(8):
            sl = slice(512 * ch, 512 * ch + 512)
            for which in range(3):
                i = bank()
                if which < 2:
                    t = pe.sig(lambda e, i=i, sl=sl, k=which: e.matmul(psS[:, i, :], wqkv[:, 128 * k:128 * k + 128], X[:, sl], start=True, stop=True), w, xtok, sfree[i])
                    if which == 0:
                        sfree[i] = act.sig(lambda e, i=i, sl=sl: e.activation(tiled(qt, sl), psS[:, i, :].rearrange("p (r t c) -> p r t c", r=8, t=4), ACT.Identity, bias=cols[:, 0:1], scale=S32), t, d0, qkfree)
                    else:
                        sfree[i] = dve.sig(lambda e, i=i, sl=sl: e.tensor_scalar(kt[:, sl], psS[:, i, :], cols[:, 1:2], None, ALU.add), t, qkfree)
                else:
                    t = pe.sig(lambda e, i=i, sl=sl: e.matmul(psS[0:64, i, :], g1w[:], X[:, sl], start=True, stop=True), w, xtok, sfree[i])
                    sfree[i] = act.sig(lambda e, i=i, sl=sl: e.activation(tiled(gt, sl), psS[0:64, i, :].rearrange("p (r t c) -> p r t c", r=8, t=4), ACT.Relu, bias=cols[0:64, 3:4]), t, qkfree)
                ready.append(sfree[i])
        i = bank()
        for k in range(32):
            t = pe.sig(lambda e, k=k, i=i: e.matmul(psS[:, i, k:k + 1], gt[:, 128 * k:128 * k + 128], g2w[:], start=True, stop=True), sfree[i], ready[-1])
        a = sfree[i] = act.sig(lambda e, i=i: e.activation(gate[:, b, 0, :], psS[:, i, 0:32], ACT.Exp, bias=cols[:, 4:5], scale=-1.0), t)
        a = dve.sig(lambda e: e.tensor_scalar(gate[:, b, 1, :], gate[:, b, 0, :], 1.0, None, ALU.add), a)
        a = dve.sig(lambda e: e.reciprocal(gate[:, b, 2, :], gate[:, b, 1, :]), a)
        return ready[-3:] + [a]

    rdy = None

    def score(n):
        nonlocal vfree, rdy, qkfree
        b, k = divmod(n, 32)
        if k == 0:
            qkfree = lastpe
            rdy = project(b)
            if b + 1 < NI:
                xin[(b + 1) % 2] = lx[(b + 1) % 2].dma(sp, xt[:, (b + 1) % 2, :], io["xT"][b + 1], xtfree[(b + 1) % 2])
        r0, c0 = 8 * (k // 4), 16 * (k % 4)
        kr, kc = min(max(r0 - 3, 0), 50), min(max(c0 - 3, 0), 42)
        cls = 3 * {0: 0, 3: 1, 6: 2}[r0 - kr] + {0: 0, 3: 1, 6: 2}[c0 - kc]
        info["x", n] = lt[n % 3].dma(sp, xs[:, n % 3, :], io["x"][b, r0:r0 + 8, c0:c0 + 16, :], outdone[n % 3])
        s = n % 2
        mm = []
        dd = []
        for h in range(4):
            i = bank()
            p = slice(32 * h, 32 * h + 32)
            t = pe.sig(lambda e, i=i, p=p: e.matmul(psS[:, i, 0:308], qt[p, 128 * k:128 * k + 128], img(kt)[p, kr:kr + 14, kc:kc + 22],
                                                    start=True, stop=True), sfree[i], *rdy)
            sfree[i] = d = dve.sig(lambda e, i=i, h=h: e.tensor_tensor_reduce(pr[:, s, h, :], psS[:, i, 0:308], bm[:, 4 * cls + h, :], 1.0, -3.0e38,
                                                                           ALU.add, ALU.max, st[:, s, h:h + 1]), t, db, prfree[s])
            dd.append(d)
        d = dve.sig(lambda e: e.tensor_scalar(st[:, s, 4:8], st[:, s, 0:4], -1.0, None, ALU.mult), dd[-1])
        for h in range(4):
            a = act.sig(lambda e, h=h: e.activation(pr[:, s, h, :], pr[:, s, h, :], ACT.Exp, bias=st[:, s, 4 + h:5 + h], accum_out=st[:, s, 8 + h:9 + h]), d)
        info["e", n] = a
        info["w", n] = wtok = pool.sig(lambda e: e.tensor_copy(xw[:, s, :].rearrange("p (r c) -> p r c", c=22), img(xt, b % 2)[:, kr:kr + 14, kc:kc + 22]),
                                       xin[b % 2], info.get(("vm", n - 2)))
        for j, (o, m) in enumerate(((0, 5), (5, 5), (10, 4))):
            t = pe.sig(lambda e, j=j, o=o, m=m: e.matmul(psV[0:22 * m, 128 * j:128 * j + 128], xw[:, s, 22 * o:22 * o + 22 * m], wqkv[:, 256:384],
                                                         start=True, stop=True), vfree, wtok)
        info["vm", n] = t
        vfree = info["v", n] = dve.sig(lambda e: e.tensor_tensor(vg[0:110, s, :, :], psV[0:110, 0:384].rearrange("p (j c) -> p j c", j=3),
                                                                 bvb[0:110, :].rearrange("p (a c) -> p a c", a=1).broadcast_to([110, 3, 128]), ALU.add),
                                       t, vgfree[s], w)
        if k == 31:
            xtfree[b % 2] = wtok

    def attend(n):
        nonlocal ofree, lastpe
        s = n % 2
        ev = []
        for h in range(4):
            i = tn[0] % 2
            tn[0] += 1
            for j, (o, m) in enumerate(((0, 110), (110, 110), (220, 88))):
                t = pe.sig(lambda e, i=i, j=j, o=o, m=m, h=h: e.transpose(psT[0:m, i, 128 * j:128 * j + 128], pr[:, s, h, o:o + m], ident[:]),
                           tfree[i], info["e", n], w)
            lane = act if h % 2 == 0 else dve
            if h % 2 == 0:
                tfree[i] = act.sig(lambda e, i=i, h=h: e.activation(ptb[0:110, h, :], psT[0:110, i, 0:384], ACT.Copy), t, ptfree[h])
            else:
                tfree[i] = dve.sig(lambda e, i=i, h=h: e.tensor_copy(ptb[0:110, h, :], psT[0:110, i, 0:384]), t, ptfree[h])
            ev.append(tfree[i])
        prfree[s] = t
        for h in range(4):
            for j, m in enumerate((110, 110, 88)):
                t = pe.sig(lambda e, h=h, j=j, m=m: e.matmul(psO[:, 32 * h:32 * h + 32], ptb[0:m, h, 128 * j:128 * j + 128], vg[0:m, s, j, 32 * h:32 * h + 32],
                                                             start=(j == 0), stop=(j == 2)), ev[h], info["v", n], ofree)
            ptfree[h] = t
        vgfree[s] = t
        lastpe = t
        d = dve.sig(lambda e: e.reciprocal(st[:, s, 12:16], st[:, s, 8:12]), info["e", n])
        ofree = info["n", n] = dve.sig(lambda e: e.tensor_tensor(on[:, s, :].rearrange("p (h d) -> p h d", h=4), psO[:, 0:128].rearrange("p (h d) -> p h d", h=4),
                                                   st[:, s, 12:16].rearrange("p (h a) -> p h a", a=1).broadcast_to([128, 4, 32]), ALU.mult), t, d, onfree[s])

    def finish(n):
        nonlocal ffree
        b, k = divmod(n, 32)
        r0, c0 = 8 * (k // 4), 16 * (k % 4)
        s = n % 2
        t = pe.sig(lambda e: e.transpose(psF[:, 0:128], on[:, s, :], ident[:]), info["n", n], ffree)
        onfree[s] = t
        a = act.sig(lambda e: e.activation(ot[:, s, :], psF[:, 0:128], ACT.Copy), t, otfree[s])
        t = pe.sig(lambda e: e.matmul(psF[:, 128:256], ot[:, s, :], wp[:], start=True, stop=True), a)
        otfree[s] = t
        ffree = d = dve.sig(lambda e: e.tensor_tensor(tm[:, s, :], psF[:, 128:256], pbb[:], ALU.add), t, w)
        info["g"] = d = dve.sig(lambda e: e.scalar_tensor_tensor(ys[:, n % 3, :], tm[:, s, :], gate[:, b, 2, k:k + 1], xs[:, n % 3, :], ALU.mult, ALU.add),
                    d, info["x", n], info["s", n - 3] if n >= 3 else None)
        outdone[n % 3] = d
        info["s", n] = lo[n % 3].dma(sp, x1[b, r0:r0 + 8, c0:c0 + 16, :], ys[:, n % 3, :], d)

    for n in range(N + 2):
        if n < N:
            score(n)
        if 1 <= n <= N:
            attend(n - 1)
        if n >= 2:
            finish(n - 2)
    sp.wait(*[info["s", N - 1 - i] for i in range(3)])
    P.run()


def layer1(nc, P, io, x1, x2):
    pe, act, dve, pool, sp = P.pe, P.act, P.dve, P.pool, P.sp
    SC = float(C) ** -0.5
    R = lambda t: t.bitcast(F32)

    ident = P.sb("ident", [128, 128])
    wraw = P.sb("wraw", [128, 4, 128])
    wh = P.sb("wh", [128, 3, 128], F32R)
    wl = P.sb("wl", [128, 3, 128], F32R)
    cols = P.sb("cols", [128, 8])
    bvb = P.sb("bvb", [128, 128])
    bob = P.sb("bob", [128, 128])
    grp = P.sb("grp", [128, 128])
    zero = P.sb("zero", [128, 1])
    pr = P.sb("pr", [128, 5, TOK])
    qh, ql = P.sb("qh", [128, TOK], F32R), P.sb("ql", [128, TOK], F32R)
    kh, kl = P.sb("kh", [128, TOK], F32R), P.sb("kl", [128, TOK], F32R)
    vh, vl = P.sb("vh", [128, 32, 128], F32R), P.sb("vl", [128, 32, 128], F32R)
    ph, pl = P.sb("ph", [128, 2, 512], F32R), P.sb("pl", [128, 2, 512], F32R)
    hc = P.sb("hc", [128, 512])
    st = P.sb("st", [128, 5, 16])
    bn = P.sb("bn", [128, 8, 6])
    gs = P.sb("gs", [128, 16])
    ots = P.sb("ots", [128, 256])
    xs = P.sb("xs", [128, 2, 128])
    ys = P.sb("ys", [128, 2, 128])

    psS = P.ps("S", [128, 3, 512])
    psT = P.ps("T", [128, 2, 512])
    psO = P.ps("O", [128, 2, 512])
    psF = P.ps("F", [128, 512])

    def row(name):
        return io[name].rearrange("(a p) -> a p", a=1).broadcast_to([128, 128])

    def col(name):
        return io[name].rearrange("(p a) -> p a", a=1)

    lw = P.load("w")
    for dst, src in ((ident[:], io["ident"]), (grp[:], io["group"]), (wraw[:, 0, :], io["L1_conv_wq"]), (wraw[:, 1, :], io["L1_conv_wk"]),
                     (wraw[:, 2, :], io["L1_conv_wv"]), (wraw[:, 3, :], io["L1_conv_wo"]),
                     (cols[:, 0:1], col("L1_conv_bq")), (cols[:, 1:2], col("L1_conv_bk")), (cols[:, 2:3], col("L1_conv_gn_scale")),
                     (cols[:, 3:4], col("L1_conv_gn_bias")), (bvb[:], row("L1_conv_bv")), (bob[:], row("L1_conv_bo"))):
        w = lw.dma(sp, dst, src, slow=True)
    li = [P.load("i0"), P.load("i1")]
    lt = [P.load("t0"), P.load("t1")]
    lo = [P.load("o0"), P.load("o1")]

    dve.sig(lambda e: e.memset(zero[:], 0.0))
    a = dve.sig(lambda e: e.tensor_copy(wh[:], wraw[:, 0:3, :]), w)
    wt = dve.sig(lambda e: e.tensor_tensor(wl[:], wraw[:, 0:3, :], R(wh[:]), ALU.subtract), a)

    sfree, sn = [None] * 3, [0]
    tfree, pfree = [None] * 2, [None] * 2
    ofree, ffree = [None, None], None
    slot = [None] * 5
    xsfree, ysfree = [None, None], [None, None]
    otsfree = None
    info = {}
    pvlast = qklast = None

    def bank():
        i = sn[0] % 3
        sn[0] += 1
        return i

    def three(out, lh, ll, rh, rl, *waits):
        pe.do(lambda e: e.matmul(out, lh, rh, start=True, stop=False), *waits)
        pe.do(lambda e: e.matmul(out, ll, rh, start=False, stop=False))
        return pe.sig(lambda e: e.matmul(out, lh, rl, start=False, stop=True))

    def prepare(b):
        nonlocal hcfree
        raw, X = pr[:, 3, :].rearrange("p (t c) -> p t c", c=128), pr[:, 4, :]
        ld = []
        for hf in range(2):
            ld.append(li[hf].dma(sp, raw[:, 16 * hf:16 * hf + 16, :], x1[b, 32 * hf:32 * hf + 32].rearrange("(t r) c d -> (r c) t d", r=2), slot[3]))
        for ch in range(8):
            i = bank()
            for k in range(4):
                t = pe.sig(lambda e, i=i, k=k, ch=ch: e.transpose(psS[:, i, 128 * k:128 * k + 128], raw[:, 4 * ch + k, :], ident[:]), sfree[i], ld[ch // 4], w)
            sfree[i] = act.sig(lambda e, i=i, ch=ch: e.activation(X[:, 512 * ch:512 * ch + 512], psS[:, i, :], ACT.Copy), t, slot[4])
            s = dve.sig(lambda e, ch=ch: e.bn_stats(bn[:, ch, :], X[:, 512 * ch:512 * ch + 512]), sfree[i])
        s = dve.sig(lambda e: e.bn_aggr(gs[:, 0:2], bn[:].rearrange("p a b -> p (a b)")), s)
        i = bank()
        t = pe.sig(lambda e: e.matmul(psS[:, i, 0:2], grp[:], gs[:, 0:2], start=True, stop=True), s, sfree[i])
        s = dve.sig(lambda e: e.tensor_copy(gs[:, 2:4], psS[:, i, 0:2]), t)
        s = dve.sig(lambda e: e.tensor_tensor(gs[:, 4:5], gs[:, 0:1], gs[:, 2:3], ALU.subtract), s)
        s = dve.sig(lambda e: e.tensor_tensor(gs[:, 5:6], gs[:, 4:5], gs[:, 4:5], ALU.mult), s)
        t = pe.sig(lambda e: e.matmul(psS[:, i, 2:3], grp[:], gs[:, 5:6], start=True, stop=True), s)
        s = sfree[i] = dve.sig(lambda e: e.tensor_tensor(gs[:, 6:7], psS[:, i, 2:3], gs[:, 3:4], ALU.add), t)
        s = dve.sig(lambda e: e.tensor_scalar(gs[:, 11:12], gs[:, 6:7], 1.0e-6, None, ALU.add), s)
        s = act.sig(lambda e: e.activation(gs[:, 12:13], gs[:, 11:12], ACT.Sqrt), s)
        s = dve.sig(lambda e: e.reciprocal(gs[:, 9:10], gs[:, 12:13]), s)
        s = dve.sig(lambda e: e.tensor_tensor(gs[:, 7:8], gs[:, 9:10], cols[:, 2:3], ALU.mult), s, w)
        s = dve.sig(lambda e: e.tensor_tensor(gs[:, 10:11], gs[:, 2:3], gs[:, 7:8], ALU.mult), s)
        s = dve.sig(lambda e: e.tensor_tensor(gs[:, 8:9], cols[:, 3:4], gs[:, 10:11], ALU.subtract), s)
        for ch in range(8):
            z = ch % 2
            sl = slice(512 * ch, 512 * ch + 512)
            s1 = act.sig(lambda e, sl=sl: e.activation(hc[:], X[:, sl], ACT.Identity, bias=gs[:, 8:9], scale=gs[:, 7:8]), s, hcfree)
            s2 = pool.sig(lambda e, z=z: e.tensor_copy(ph[:, z, :], hc[:]), s1, pfree[z])
            s3 = hcfree = dve.sig(lambda e, z=z: e.tensor_tensor(pl[:, z, :], hc[:], R(ph[:, z, :]), ALU.subtract), s2)
            for k, (dh, dl, bias) in enumerate(((qh, ql, 0), (kh, kl, 1))):
                i = bank()
                t = three(psS[:, i, :], wh[:, k, :], wl[:, k, :], ph[:, z, :], pl[:, z, :], s3, wt, sfree[i])
                u = act.sig(lambda e, i=i, dh=dh, k=k, sl=sl: e.activation(dh[:, sl], psS[:, i, :], ACT.Identity, bias=cols[:, k:k + 1]), t, qklast)
                sfree[i] = dve.sig(lambda e, i=i, dh=dh, dl=dl, k=k, sl=sl: e.scalar_tensor_tensor(dl[:, sl], psS[:, i, :], cols[:, k:k + 1], R(dh[:, sl]),
                                                                                               ALU.add, ALU.subtract), u)
            i = bank()
            pe.wait(sfree[i])
            for k in range(4):
                tk = slice(128 * k, 128 * k + 128)
                t = three(psS[:, i, tk], ph[:, z, tk], pl[:, z, tk], wh[:, 2, :], wl[:, 2, :])
            pfree[z] = t
            v = psS[:, i, :].rearrange("p (t c) -> p t c", c=128)
            sl4 = slice(4 * ch, 4 * ch + 4)
            bvx = bvb[:].rearrange("p (a c) -> p a c", a=1).broadcast_to([128, 4, 128])
            u = sfree[i] = dve.sig(lambda e, v=v, bvx=bvx: e.tensor_tensor(hc[:].rearrange("p (t c) -> p t c", c=128), v, bvx, ALU.add), t, w)
            u2 = act.sig(lambda e, sl4=sl4: e.activation(vh[:, sl4, :], hc[:].rearrange("p (t c) -> p t c", c=128), ACT.Copy), u, pvlast)
            hcfree = u2 = dve.sig(lambda e, sl4=sl4: e.tensor_tensor(vl[:, sl4, :], hc[:].rearrange("p (t c) -> p t c", c=128), R(vh[:, sl4, :]), ALU.subtract), u2)
        slot[3] = t
        slot[4] = s1
        info["v"] = u2
        info["qk"] = sfree[(sn[0] - 2) % 3]

    hcfree = None
    pending = []

    def qk(b, u):
        nonlocal qklast
        q, kc = divmod(u, 8)
        s = q % 5
        i = bank()
        qs, ks = slice(128 * q, 128 * q + 128), slice(512 * kc, 512 * kc + 512)
        t = qklast = three(psS[:, i, :], qh[:, qs], ql[:, qs], kh[:, ks], kl[:, ks], info["v"], info["qk"], sfree[i])
        d = sfree[i] = dve.sig(lambda e: e.tensor_tensor_reduce(pr[:, s, ks], psS[:, i, :], zero[:].broadcast_to([128, 512]), 1.0, -3.0e38,
                                                                ALU.add, ALU.max, st[:, s, kc:kc + 1]), t, slot[s])
        if kc == 7:
            d = dve.sig(lambda e: e.tensor_reduce(st[:, s, 8:9], st[:, s, 0:8], AX.X, ALU.max), d)
            d = dve.sig(lambda e: e.tensor_scalar(st[:, s, 9:10], st[:, s, 8:9], -SC, None, ALU.mult), d)
            for k in range(4):
                pending.append((q, s, k, d))

    def exps():
        if pending:
            q, s, k, d = pending.pop(0)
            es = slice(1024 * k, 1024 * k + 1024)
            info["e", q] = act.sig(lambda e: e.activation(pr[:, s, es], pr[:, s, es], ACT.Exp, bias=st[:, s, 9:10], scale=SC,
                                                         accum_out=st[:, s, 10 + k:11 + k]), d)

    def turn(v):
        g, j = divmod(v, 16)
        i = v % 2
        for q in range(2):
            s = (2 * g + q) % 5
            for k in range(2):
                kt = 2 * j + k
                t = pe.sig(lambda e, k=k, q=q, s=s, kt=kt: e.transpose(psT[:, i, 256 * k + 128 * q:256 * k + 128 * q + 128], pr[:, s, 128 * kt:128 * kt + 128], ident[:]),
                           info["e", 2 * g + q], tfree[i])
        if j == 15:
            slot[2 * g % 5] = slot[(2 * g + 1) % 5] = t
        a = act.sig(lambda e: e.activation(ph[:, i, :], psT[:, i, :], ACT.Copy), t, pfree[i])
        tfree[i] = info["p", v] = dve.sig(lambda e: e.tensor_tensor(pl[:, i, :], psT[:, i, :], R(ph[:, i, :]), ALU.subtract), a)

    def pv(b, v):
        nonlocal pvlast
        g, j = divmod(v, 16)
        i, o = v % 2, g % 2
        out = psO[:, o, 0:256]
        for k in range(2):
            kt = 2 * j + k
            ks = slice(256 * k, 256 * k + 256)
            pe.do(lambda e, kt=kt, ks=ks, f=(j == 0 and k == 0): e.matmul(out, vh[:, kt, :], ph[:, i, ks], start=f, stop=False), info["p", v], ofree[o])
            pe.do(lambda e, kt=kt, ks=ks: e.matmul(out, vl[:, kt, :], ph[:, i, ks], start=False, stop=False))
            t = pe.sig(lambda e, kt=kt, ks=ks, f=(j == 15 and k == 1): e.matmul(out, vh[:, kt, :], pl[:, i, ks], start=False, stop=f))
        pfree[i] = pvlast = t
        if j == 15:
            for q in range(2):
                n = 2 * g + q
                info["x", n] = lt[q].dma(sp, xs[:, q, :], x1[b, 2 * n:2 * n + 2].rearrange("r c d -> (r c) d"), xsfree[q])
            info["o"] = (b, g, t)

    def out1():
        nonlocal otsfree
        b, g, t = info["o"]
        o = g % 2
        a = ofree[o] = act.sig(lambda e: e.activation(ots[:], psO[:, o, 0:256], ACT.Copy), t, otsfree)
        info["a"] = a

    def out2():
        nonlocal ffree, otsfree
        b, g, _ = info.pop("o")
        for q in range(2):
            n = 2 * g + q
            s = n % 5
            t = pe.sig(lambda e, q=q: e.matmul(psF[:, 128 * q:128 * q + 128], ots[:, 128 * q:128 * q + 128], wraw[:, 3, :], start=True, stop=True), info["a"], ffree)
        otsfree = t
        for q in range(2):
            n = 2 * g + q
            s = n % 5
            r = dve.sig(lambda e, s=s: e.tensor_reduce(st[:, s, 14:15], st[:, s, 10:14], AX.X, ALU.add), info["e", n])
            r = dve.sig(lambda e, s=s: e.reciprocal(st[:, s, 15:16], st[:, s, 14:15]), r)
            x = pool.sig(lambda e, q=q: e.tensor_tensor(xs[:, q, :], xs[:, q, :], bob[:], ALU.add), info["x", n], w)
            d = xsfree[q] = ffree = dve.sig(lambda e, q=q, s=s: e.scalar_tensor_tensor(ys[:, q, :], psF[:, 128 * q:128 * q + 128], st[:, s, 15:16], xs[:, q, :],
                                                                           ALU.mult, ALU.add), t, r, x, ysfree[q])
            ysfree[q] = lo[q].dma(sp, x2[b, 2 * n:2 * n + 2].rearrange("r c d -> (r c) d"), ys[:, q, :], d)

    for b in range(NI):
        prepare(b)
        for v in range(-24, 259):
            if 0 <= v + 24 < 256:
                qk(b, v + 24)
            exps()
            if 0 <= v + 1 < 256:
                turn(v + 1)
            if 0 <= v < 256:
                pv(b, v)
            if "o" in info and v % 16 == 0:
                out1()
            elif "o" in info and v % 16 == 2:
                out2()
    sp.wait(*ysfree)
    P.run()


def layer2(nc, P, io, x2, x3t):
    pe, act, dve, pool, sp = P.pe, P.act, P.dve, P.pool, P.sp
    ident = P.sb("ident", [128, 128])
    wts = P.sb("wts", [128, 5, 128])
    cols = P.sb("cols", [128, 8])
    bob = P.sb("bob", [128, 128])
    x = P.sb("x", [128, 2, 32, 128])
    xt = P.sb("xt", [128, 2, TOK])
    rs = P.sb("rs", [128, 3, 64])
    ee = P.sb("ee", [128, 2, 512])
    ll = P.sb("ll", [128, 2, 512])
    bn = P.sb("bn", [128, 32, 6])
    mv = P.sb("mv", [128, 2, 32, 2])
    rstd = P.sb("rstd", [128, 3, 32])
    o3 = P.sb("o3", [128, 2, 512])
    psA = P.ps("A", [128, 2, 512])
    psG = P.ps("G", [128, 2, 512])
    psO = P.ps("O", [128, 2, 512])
    psX = P.ps("X", [128, 2, 512])

    def col(name):
        return io[name].rearrange("(p a) -> p a", a=1)

    lw = P.load("w")
    for dst, src in ((ident[:], io["ident"]), (wts[:, 0, :], io["L2_conv_W_left"]), (wts[:, 1, :], io["L2_conv_W_eq"]),
                     (wts[:, 2, :], io["L2_conv_W_right"]), (wts[:, 3, :], io["L2_conv_W_gate"]), (wts[:, 4, :], io["L2_conv_W_out"]),
                     (cols[:, 0:1], col("L2_conv_b_left")), (cols[:, 1:2], col("L2_conv_b_eq")), (cols[:, 2:3], col("L2_conv_b_right")),
                     (cols[:, 3:4], col("L2_conv_b_gate")), (cols[:, 4:5], col("L2_conv_ln_scale")), (cols[:, 5:6], col("L2_conv_ln_bias")),
                     (bob[:], io["L2_conv_b_out"].rearrange("(a p) -> a p", a=1).broadcast_to([128, 128]))):
        w = lw.dma(sp, dst, src, slow=True)
    li = [P.load("i0"), P.load("i1")]
    lo = [P.load("o0"), P.load("o1")]
    dve.sig(lambda e: e.tensor_tensor(wts[:, 0, :], wts[:, 0, :], wts[:, 1, :], ALU.add), w)
    dve.sig(lambda e: e.tensor_tensor(cols[:, 0:1], cols[:, 0:1], cols[:, 1:2], ALU.add), w)
    dve.sig(lambda e: e.tensor_scalar(cols[:, 2:3], cols[:, 2:3], 64.0, None, ALU.mult), w)
    wk = dve.sig(lambda e: e.tensor_scalar(cols[:, 3:4], cols[:, 3:4], -1.0, None, ALU.mult), w)

    bx, nx = [None] * 2, [0]
    bo, no = [None] * 2, [0]
    ba, bg = [None] * 2, [None] * 2
    eef, llf, o3f = [None] * 2, [None] * 2, [None] * 2
    xfree, xtfree, mvfree = [None] * 2, [None] * 2, None
    pend = []

    def chunk(b, ch, rsok, xok, xtok):
        s = ch % 2
        sl = slice(512 * ch, 512 * ch + 512)
        X = xt[:, b % 2, sl]
        t1 = pe.sig(lambda e: e.matmul(psG[:, s, :], wts[:, 3, :], X, start=True, stop=True), xtok, bg[s])
        t2 = pe.sig(lambda e: e.matmul(psA[:, s, :], wts[:, 0, :], X, start=True, stop=True), ba[s], wk)
        a = bg[s] = act.sig(lambda e: e.activation(ee[:, s, :], psG[:, s, :], ACT.Exp, bias=cols[:, 3:4], scale=-1.0), t1, wk, eef[s])
        a = pool.sig(lambda e: e.tensor_scalar(ee[:, s, :], ee[:, s, :], 1.0, None, ALU.add), a)
        d = dve.sig(lambda e: e.reciprocal(ee[:, s, :], ee[:, s, :]), a)
        d2 = ba[s] = dve.sig(lambda e: e.scalar_tensor_tensor(ll[:, s, :].rearrange("p (r c) -> p r c", c=64), psA[:, s, :].rearrange("p (r c) -> p r c", c=64),
                                                             cols[:, 0:1], rs[:, 2, 8 * ch:8 * ch + 8].rearrange("p (r a) -> p r a", a=1).broadcast_to([128, 8, 64]),
                                                             ALU.add, ALU.mult), t2, rsok, llf[s])
        d2 = eef[s] = dve.sig(lambda e: e.tensor_tensor(ll[:, s, :], ll[:, s, :], ee[:, s, :], ALU.mult), d2, d)
        v = x[:, b % 2, 4 * ch:4 * ch + 4, :]
        xb = pool.sig(lambda e: e.tensor_tensor(v, v, bob[:].rearrange("p (a c) -> p a c", a=1).broadcast_to([128, 4, 128]), ALU.add), xok, xtok, w)
        return lambda: tail(b, ch, s, d2, xb)

    def tail(b, ch, s, d2, xb):
        i = ch % 2
        v = x[:, b % 2, 4 * ch:4 * ch + 4, :]
        for k in range(4):
            t = pe.sig(lambda e, k=k: e.matmul(psO[:, i, 128 * k:128 * k + 128], ll[:, s, 128 * k:128 * k + 128], wts[:, 4, :], start=True, stop=True), d2, bo[i], w)
        llf[s] = t
        y = bo[i] = dve.sig(lambda e: e.tensor_tensor(v, psO[:, i, :].rearrange("p (k c) -> p k c", k=4), v, ALU.add), t, xb)
        for k in range(4):
            q = dve.sig(lambda e, k=k: e.bn_stats(bn[:, 4 * ch + k, :], v[:, k, :]), y)
        for k in range(4):
            q = dve.sig(lambda e, k=k: e.bn_aggr(mv[:, b % 2, 4 * ch + k, :], bn[:, 4 * ch + k, :]), q)
        return q

    for b in range(NI + 1):
        if b < NI:
            ld = []
            for hf in range(2):
                ld.append(li[hf].dma(sp, x[:, b % 2, 16 * hf:16 * hf + 16, :], x2[b, 32 * hf:32 * hf + 32].rearrange("(t r) c d -> (r c) t d", r=2), xfree[b % 2]))
            for ch in range(8):
                i = nx[0] % 2
                nx[0] += 1
                for k in range(4):
                    t = pe.sig(lambda e, i=i, k=k, ch=ch, b=b: e.transpose(psX[:, i, 128 * k:128 * k + 128], x[:, b % 2, 4 * ch + k, :], ident[:]), bx[i], ld[ch // 4], w)
                bx[i] = a = act.sig(lambda e, i=i, ch=ch, b=b: e.activation(xt[:, b % 2, 512 * ch:512 * ch + 512], psX[:, i, :], ACT.Copy), t, xtfree[b % 2])
                r = dve.sig(lambda e, ch=ch, b=b: e.tensor_reduce(rs[:, 0, 8 * ch:8 * ch + 8], xt[:, b % 2, 512 * ch:512 * ch + 512].rearrange("p (r c) -> p r c", c=64),
                                                                 AX.X, ALU.add), a)
            i = nx[0] % 2
            nx[0] += 1
            t = pe.sig(lambda e, i=i: e.matmul(psX[:, i, 0:64], wts[:, 2, :], rs[:, 0, :], start=True, stop=True), r, bx[i], w)
            rsok = bx[i] = dve.sig(lambda e, i=i: e.tensor_scalar(rs[:, 2, :], psX[:, i, 0:64], cols[:, 2:3], None, ALU.add), t, wk)
            prev = None
            for ch in range(8):
                nxt = chunk(b, ch, rsok, ld[ch // 4], a)
                if prev:
                    prev()
                prev = nxt
            q = prev()
            xtfree[b % 2] = llf[1]
            pend.append((b, q))
        if b >= 1 or b == NI:
            pass
        if b < NI:
            q = dve.sig(lambda e, b=b: e.tensor_scalar(rstd[:, 0, :], mv[:, b % 2, :, 1], 1.0e-5, None, ALU.add), q)
            q = act.sig(lambda e: e.activation(rstd[:, 1, :], rstd[:, 0, :], ACT.Sqrt), q)
            q = dve.sig(lambda e: e.reciprocal(rstd[:, 2, :], rstd[:, 1, :]), q)
            for ch in range(8):
                for k in range(4):
                    n = 4 * ch + k
                    z = dve.sig(lambda e, n=n, b=b: e.tensor_scalar(x[:, b % 2, n, :], x[:, b % 2, n, :], mv[:, b % 2, n, 0:1], rstd[:, 2, n:n + 1],
                                                                   ALU.subtract, ALU.mult), q)
                i = nx[0] % 2
                nx[0] += 1
                for k in range(4):
                    t = pe.sig(lambda e, i=i, k=k, ch=ch, b=b: e.transpose(psX[:, i, 128 * k:128 * k + 128], x[:, b % 2, 4 * ch + k, :], ident[:]), bx[i], z)
                s = ch % 2
                bx[i] = a = act.sig(lambda e, i=i, s=s: e.activation(o3[:, s, :], psX[:, i, :], ACT.Identity, bias=cols[:, 5:6], scale=cols[:, 4:5]), t, o3f[s])
                o3f[s] = lo[s].dma(sp, x3t[b, :, 512 * ch:512 * ch + 512], o3[:, s, :], a)
            xfree[b % 2] = t
    sp.wait(*o3f)
    P.run()


def directed(t, d):
    if d == 0:
        return t.rearrange("p (k l) -> p k l", k=8)
    if d == 1:
        return t[:, ::-1].rearrange("p (k l) -> p k l", k=8)
    v = t.rearrange("p (h w) -> p h w", w=HW)
    if d == 3:
        v = v[:, ::-1, ::-1]
    return v.rearrange("p h (k w) -> p k w h", k=8)


def part(t, d, c):
    v = directed(t, d)
    return v[:, c] if d >= 2 else v[:, c, :]


def layer3(nc, ctx, io, x3t, dbl, out):
    U = ctx.enter_context(nc.sbuf_tensor("l3_u", [128, 2 * NI, TOK], F32))
    with ExitStack() as inner:
        convolve(nc, Phase(nc, inner, "l3a"), io, x3t, dbl, U)
    with ExitStack() as inner:
        scan(nc, Phase(nc, inner, "l3b"), io, x3t, dbl, out, U)


def convolve(nc, P, io, x3t, dbl, U):
    pe, act, dve, pool, sp = P.pe, P.act, P.dve, P.pool, P.sp
    R = lambda t: t.bitcast(F32)
    win = P.sb("win", [128, 256])
    taps = P.sb("taps", [128, 9, 256])
    th, tl = P.sb("th", [128, 9, 256], F32R), P.sb("tl", [128, 9, 256], F32R)
    xh, xl = P.sb("xh", [128, 66, 66], F32R), P.sb("xl", [128, 66, 66], F32R)
    xr = P.sb("xr", [128, 512])
    wx = P.sb("wx", [128, 2, 10])
    cb = P.sb("cb", [128, 2])
    ds = P.sb("ds", [10, 2, 512])
    ps = P.ps("c", [128, 4, 512])
    psD = P.ps("d", [128, 2, 512])
    lw = P.load("w")
    for dst, src in ((win[:], io["L3_conv_Win"][:, 0:256]), (taps[:], io["taps"].rearrange("(a t) c -> a t c", a=1).broadcast_to([128, 9, 256])),
                     (wx[:], io["L3_conv_Wxproj"].rearrange("(h p) d -> p h d", p=128)), (cb[:], io["L3_conv_conv_b"].rearrange("(h p) -> p h", p=128))):
        w = lw.dma(sp, dst, src, slow=True)
    lx = P.load("x")
    ld = [P.load("d0"), P.load("d1")]
    dve.sig(lambda e: e.memset(R(xh[:]), 0.0))
    z = dve.sig(lambda e: e.memset(R(xl[:]), 0.0))
    a = dve.sig(lambda e: e.tensor_tensor(taps[:], taps[:], win[:].rearrange("p (a c) -> p a c", a=1).broadcast_to([128, 9, 256]), ALU.mult), w)
    a = dve.sig(lambda e: e.tensor_copy(th[:], taps[:]), a)
    wt = dve.sig(lambda e: e.tensor_tensor(tl[:], taps[:], R(th[:]), ALU.subtract), a)
    free, df = [None] * 4, [None] * 2
    n = 0
    xrf = padf = None
    dsf = [None, None]
    for b in range(NI):
        for ch in range(8):
            t = lx.dma(sp, xr[:], x3t[b, :, 512 * ch:512 * ch + 512], xrf)
            r = slice(8 * ch + 1, 8 * ch + 9)
            v = xr[:].rearrange("p (r c) -> p r c", c=64)
            a = act.sig(lambda e, r=r, v=v: e.activation(xh[:, r, 1:65], v, ACT.Copy), t, z, padf)
            xrf = px = dve.sig(lambda e, r=r, v=v: e.tensor_tensor(xl[:, r, 1:65], v, R(xh[:, r, 1:65]), ALU.subtract), a)
        for ch in range(8):
            last = []
            for h in range(2):
                i = n % 4
                n += 1
                hs = slice(128 * h, 128 * h + 128)
                pe.wait(px, wt, free[i])
                for t9 in range(9):
                    dy, dx = divmod(t9, 3)
                    rr, cc = slice(8 * ch + dy, 8 * ch + dy + 8), slice(dx, dx + 64)
                    o = ps[:, i, :].rearrange("p (r c) -> p r c", c=64)
                    for k, (wv, xv) in enumerate(((th, xh), (tl, xh), (th, xl))):
                        first, end = t9 == 0 and k == 0, t9 == 8 and k == 2
                        f = lambda e, o=o, wv=wv, xv=xv, t9=t9, hs=hs, rr=rr, cc=cc, first=first, end=end: e.matmul(o, wv[:, t9, hs], xv[:, rr, cc], start=first, stop=end)
                        if end:
                            padf = t = pe.sig(f)
                        else:
                            pe.do(f)
                free[i] = act.sig(lambda e, i=i, b=b, h=h, ch=ch: e.activation(U[:, 2 * b + h, 512 * ch:512 * ch + 512], ps[:, i, :], ACT.Silu, bias=cb[:, h:h + 1]), t, w)
                last.append(free[i])
            j = ch % 2
            pe.do(lambda e, j=j, b=b, ch=ch: e.matmul(psD[0:10, j, :], wx[:, 0, :], U[:, 2 * b, 512 * ch:512 * ch + 512], start=True, stop=False), *last, df[j])
            t = pe.sig(lambda e, j=j, b=b, ch=ch: e.matmul(psD[0:10, j, :], wx[:, 1, :], U[:, 2 * b + 1, 512 * ch:512 * ch + 512], start=False, stop=True))
            df[j] = d = dve.sig(lambda e, j=j: e.tensor_copy(ds[:, j, :], psD[0:10, j, :]), t, dsf[j])
            dsf[j] = ld[j].dma(sp, dbl[b, :, 512 * ch:512 * ch + 512], ds[:, j, :], d)
    sp.wait(*dsf)
    P.run()


def scan(nc, P, io, x3t, dbl, out, U):
    pe, act, dve, pool, sp = P.pe, P.act, P.dve, P.pool, P.sp
    D = P.sb("D", [128, TOK])
    acc = P.sb("acc", [128, 2, TOK])
    dtw = P.sb("dtw", [32, NI, 256])
    sel = P.sb("sel", [128, NI, 128])
    cA, cD, cB = P.sb("cA", [128, 8]), P.sb("cD", [128, 8]), P.sb("cB", [128, 8])
    cg = P.sb("cg", [128, 4])
    wz = P.sb("wz", [128, 256])
    wo = P.sb("wo", [128, 2, 128])
    gw = P.sb("gw", [128, 2, 128])
    bw = P.sb("bw", [128, 128])
    ones = P.sb("ones", [128, 128])
    rstd = P.sb("rstd", [128, 2, 32])
    E = P.sb("E", [128, 2, 512])
    dl = P.sb("dl", [128, 2, 512])
    du = P.sb("du", [128, 2, 512])
    hh = P.sb("hh", [128, 4, 512])
    psd = P.ps("d", [128, 2, 512])
    psB = P.ps("B", [128, 2, 512])
    psC = P.ps("C", [128, 2, 512])
    psX = P.ps("X", [128, 2, 512])

    lw = P.load("w")
    dve0 = dve.sig(lambda e: e.memset(dtw[:], 0.0))
    loads = [(sel[:], io["sel"]), (cA[:], io["L3_conv_A_log"].rearrange("(k p) -> p k", p=128) if len(io["L3_conv_A_log"].shape) == 1 else io["L3_conv_A_log"].rearrange("(k p) a -> p (k a)", p=128)),
             (cD[:], io["L3_conv_D_param"].rearrange("(k p) -> p k", p=128)), (cB[:], io["L3_conv_dt_bias"].rearrange("(k p) -> p k", p=128)),
             (cg[:, 0:2], io["L3_conv_gamma"].rearrange("(h p) -> p h", p=128)), (cg[:, 2:4], io["L3_conv_beta"].rearrange("(h p) -> p h", p=128)),
             (wz[:], io["L3_conv_Win"][:, 256:512]), (wo[:], io["L3_conv_Wout"].rearrange("(h p) d -> p h d", p=128)),
             (D[32:36, :], dbl[:, 8, :]), (D[64:68, :], dbl[:, 9, :])]
    loads += [(D[8 * b:8 * b + 8, :], dbl[b, 0:8, :]) for b in range(NI)]
    loads += [(dtw[8 * b:8 * b + 8, b, :], io["dtw"][b]) for b in range(NI)]
    for dst, src in loads:
        w = lw.dma(sp, dst, src, dve0, slow=True)
    a = act.sig(lambda e: e.activation(cA[:], cA[:], ACT.Exp), w)
    wA = dve.sig(lambda e: e.tensor_scalar(cA[:], cA[:], -1.0, None, ALU.mult), a)
    for h in range(2):
        g = dve.sig(lambda e, h=h: e.tensor_scalar(gw[:, h, :], wo[:, h, :], cg[:, h:h + 1], None, ALU.mult), w)
    dve.sig(lambda e: e.memset(ones[:], 1.0))
    for h in range(2):
        g = dve.sig(lambda e, h=h: e.tensor_scalar(E[:, 0, 128 * h:128 * h + 128], ones[:], cg[:, 2 + h:3 + h], None, ALU.mult), (dve.sem, dve.n))
    pe.do(lambda e: e.matmul(psX[:, 0, 0:128], E[:, 0, 0:128], wo[:, 0, :], start=True, stop=False), g, w)
    t = pe.sig(lambda e: e.matmul(psX[:, 0, 0:128], E[:, 0, 128:256], wo[:, 1, :], start=False, stop=True))
    g = dve.sig(lambda e: e.tensor_copy(bw[:], psX[:, 0, 0:128]), t)
    won = dve.sig(lambda e: e.memset(ones[:], 1.0 / 256), g)

    df, bf, cf = [None] * 2, [None] * 2, [None] * 2
    Ef, dlf, duf, hf = [won, None], [None] * 2, [None] * 2, [None] * 4
    accw = [None, None]
    xf = [won, None]
    lx = [P.load("x0"), P.load("x1")]
    lo = [P.load("o0"), P.load("o1")]
    xfree = None
    of = [None, None]
    m = 0
    mb = 0
    for n in range(NI):
        for a4 in range(4):
            for c in range(8):
                ib = mb % 2
                mb += 1
                tB = pe.sig(lambda e, ib=ib, a4=a4, n=n, c=c: e.matmul(psB[:, ib, :], sel[32:36, a4, :], part(D[32:36, :], n, c), start=True, stop=True), w, bf[ib])
                tC = pe.sig(lambda e, ib=ib, a4=a4, n=n, c=c: e.matmul(psC[:, ib, :], sel[64:68, a4, :], part(D[64:68, :], n, c), start=True, stop=True), w, cf[ib])
                for h in range(2):
                    i = m % 2
                    m += 1
                    k = 2 * a4 + h
                    hi = 2 * h + c % 2
                    shape = (lambda t: t) if n < 2 else (lambda t: t.rearrange("p (w h) -> p w h", h=64))
                    shapea = (lambda t: t) if a4 < 2 else (lambda t: t.rearrange("p (w h) -> p w h", h=64))
                    u = part(U[:, 2 * a4 + h, :], n, c)
                    t = pe.sig(lambda e, i=i, n=n, h=h, a4=a4, c=c: e.matmul(psd[:, i, :], dtw[:, n, 128 * h:128 * h + 128], part(D[0:32, :], a4, c),
                                                                         start=True, stop=True), w, df[i])
                    a = act.sig(lambda e, i=i, k=k: e.activation(E[:, i, :], psd[:, i, :], ACT.Exp, bias=cB[:, k:k + 1]), t, Ef[i])
                    a = dve.sig(lambda e, i=i: e.tensor_scalar(E[:, i, :], E[:, i, :], 2.0 ** 60, None, ALU.min), a)
                    a = act.sig(lambda e, i=i: e.activation(E[:, i, :], E[:, i, :], ACT.Ln, bias=1.0), a)
                    d = df[i] = dve.sig(lambda e, i=i, k=k: e.scalar_tensor_tensor(dl[:, i, :], psd[:, i, :], cB[:, k:k + 1], E[:, i, :], ALU.add, ALU.max), a, dlf[i])
                    a = act.sig(lambda e, i=i, k=k: e.activation(E[:, i, :], dl[:, i, :], ACT.Exp, scale=cA[:, k:k + 1]), d, wA)
                    p = dlf[i] = pool.sig(lambda e, i=i, u=u, shape=shape: e.tensor_tensor(shape(du[:, i, :]), shape(dl[:, i, :]), u, ALU.mult), d, duf[i])
                    dlf[i] = p
                    b_ = dve.sig(lambda e, i=i, ib=ib: e.tensor_tensor(du[:, i, :], psB[:, ib, :], du[:, i, :], ALU.mult), p)
                    bf[ib] = b_
                    init = 0.0 if c == 0 else hh[:, 2 * h + (c - 1) % 2, 511:512]
                    s = Ef[i] = dve.sig(lambda e, i=i, hi=hi, init=init: e.tensor_tensor_scan(hh[:, hi, :], E[:, i, :], du[:, i, :], init, ALU.mult, ALU.add), a, b_,
                                hf[2 * h + (c - 1) % 2], hf[hi])
                    hf[hi] = s
                    y = cf[ib] = dve.sig(lambda e, i=i, hi=hi, ib=ib: e.tensor_tensor(du[:, i, :], psC[:, ib, :], hh[:, hi, :], ALU.mult), s, tC)
                    hf[hi] = y
                    y = dve.sig(lambda e, i=i, k=k, u=u, shape=shape: e.scalar_tensor_tensor(shape(du[:, i, :]), u, cD[:, k:k + 1], shape(du[:, i, :]), ALU.mult, ALU.add), y)
                    o = part(acc[:, h, :], a4, c)
                    if a4 == 0:
                        p = pool.sig(lambda e, i=i, o=o, shapea=shapea: e.tensor_copy(o, shapea(du[:, i, :])), y, accw[h])
                    else:
                        p = pool.sig(lambda e, i=i, o=o, shapea=shapea: e.tensor_tensor(o, o, shapea(du[:, i, :]), ALU.add), y, accw[h])
                    duf[i] = p
                    if c == 7:
                        accw[h] = p
        xfree = None
        for c in range(8):
            sl = slice(512 * c, 512 * c + 512)
            i = c % 2
            ld = lx[i].dma(sp, dl[:, i, :], x3t[n, :, sl], dlf[i], Ef[i] if c < 2 else None)
            for h in range(2):
                t = pe.sig(lambda e, h=h, i=i: e.matmul(psd[:, h, :], wz[:, 128 * h:128 * h + 128], dl[:, i, :], start=True, stop=True), ld, df[h])
                dlf[i] = t
                a = df[h] = act.sig(lambda e, h=h: e.activation(E[:, h, :], psd[:, h, :], ACT.Silu), t, Ef[h])
                y = Ef[h] = dve.sig(lambda e, h=h, sl=sl: e.tensor_tensor(acc[:, h, sl], acc[:, h, sl], E[:, h, :], ALU.mult), a, accw[h])
            pe.do(lambda e, i=i, sl=sl: e.matmul(psB[:, i, :], ones[:], acc[:, 0, sl], start=True, stop=False), y, bf[i], won)
            t = pe.sig(lambda e, i=i, sl=sl: e.matmul(psB[:, i, :], ones[:], acc[:, 1, sl], start=False, stop=True))
            for h in range(2):
                y = bf[i] = dve.sig(lambda e, h=h, i=i, sl=sl: e.tensor_tensor(acc[:, h, sl], acc[:, h, sl], psB[:, i, :], ALU.subtract), t)
                q = act.sig(lambda e, h=h, sl=sl: e.activation(du[:, h, :], acc[:, h, sl], ACT.Square), y, duf[h])
            for k in range(4):
                for h in range(2):
                    f = lambda e, k=k, h=h, c=c: e.matmul(psX[:, 0, 4 * c + k:4 * c + k + 1], du[:, h, 128 * k:128 * k + 128], ones[:, 0:1], start=(h == 0), stop=(h == 1))
                    if h:
                        t = pe.sig(f)
                    else:
                        pe.do(f, q, xf[0])
            duf = [t, t]
        v = xf[0] = dve.sig(lambda e: e.tensor_scalar(rstd[:, 0, :], psX[:, 0, 0:32], 1.0e-5, None, ALU.add), t)
        v = act.sig(lambda e: e.activation(rstd[:, 1, :], rstd[:, 0, :], ACT.Sqrt), v)
        v = dve.sig(lambda e: e.reciprocal(rstd[:, 0, :], rstd[:, 1, :]), v)
        for c in range(8):
            i = c % 2
            for k in range(4):
                tk = slice(512 * c + 128 * k, 512 * c + 128 * k + 128)
                for h in range(2):
                    f = lambda e, k=k, h=h, tk=tk: e.matmul(psX[:, 1, 128 * k:128 * k + 128], acc[:, h, tk], gw[:, h, :], start=(h == 0), stop=(h == 1))
                    if h:
                        t = pe.sig(f)
                    else:
                        pe.do(f, xf[1], y)
            for k in range(4):
                y2 = dve.sig(lambda e, k=k, c=c, i=i: e.scalar_tensor_tensor(E[:, i, 128 * k:128 * k + 128], psX[:, 1, 128 * k:128 * k + 128],
                                                                            rstd[:, 0, 4 * c + k:4 * c + k + 1], bw[:], ALU.mult, ALU.add), t, v, Ef[i])
            xf[1] = y2
            Ef[i] = lo[i].dma(sp, out[n, 8 * c:8 * c + 8].rearrange("(t r) c d -> (r c) t d", r=2), E[:, i, :].rearrange("p (t c) -> p t c", t=4), y2)
        accw = [t, t]
    sp.wait(*Ef)
    P.run()


USED = ["x", "xT", "ident", "rpbx", "mask", "group", "taps", "dtw", "sel"]
USED += ["L0_conv_" + k for k in ("qkv_w", "qkv_b", "proj_w", "proj_b", "g1_w", "g1_b", "g2_w", "g2_b")]
USED += ["L1_conv_" + k for k in ("gn_scale", "gn_bias", "wq", "bq", "wk", "bk", "wv", "bv", "wo", "bo")]
USED += ["L2_conv_" + k for k in ("W_left", "b_left", "W_right", "b_right", "W_gate", "b_gate", "W_eq", "b_eq", "W_out", "b_out", "ln_scale", "ln_bias")]
USED += ["L3_conv_" + k for k in ("Win", "conv_b", "Wxproj", "A_log", "D_param", "dt_bias", "gamma", "beta", "Wout")]


def layout(inputs):
    a = {k: np.asarray(v) for k, v in inputs.items()}
    a["xT"] = np.ascontiguousarray(a["x"].reshape(NI, TOK, C).transpose(0, 2, 1))
    rpb = a["L0_conv_rpb"]
    q = np.arange(128)
    key = np.arange(308)
    rp, mask = [], []
    for dr in (0, 3, 6):
        for dc in (0, 3, 6):
            def axis(d, n, size):
                i = np.arange(n) + d
                start = {0: np.maximum(i - 3, 0), 3: i - 3, 6: np.minimum(i - 3, size - 7)}[d]
                return i, start
            ri, rs = axis(dr, 8, 14)
            ci, cs = axis(dc, 16, 22)
            qi, qs, pi, ps = ri[q // 16], rs[q // 16], ci[q % 16], cs[q % 16]
            kr, kc = key // 22, key % 22
            inside = ((kr >= qs[:, None]) & (kr < qs[:, None] + 7) & (kc >= ps[:, None]) & (kc < ps[:, None] + 7))
            br = np.clip(kr[None] - qi[:, None] + 6, 0, 12)
            bc = np.clip(kc[None] - pi[:, None] + 6, 0, 12)
            mask.append(np.where(inside, 0.0, -1.0e30).astype(np.float32))
            rp.append(rpb[:, br, bc])
    a["rpbx"] = np.ascontiguousarray(np.concatenate(rp))
    a["mask"] = np.stack(mask)
    a["group"] = (np.kron(np.eye(32), np.ones((4, 4))) / 4).astype(np.float32)
    a["taps"] = a["L3_conv_conv_w"].reshape(256, 9).T
    a["dtw"] = a["L3_conv_dt_weight"].transpose(0, 2, 1)
    sel = np.zeros((128, NI, 128), np.float32)
    for k in range(NI):
        sel[32 + k, k] = sel[64 + k, k] = 1.0
    a["sel"] = sel
    a["ident"] = np.eye(128, dtype=np.float32)
    return a


def program(nc, io, out):
    global SEMS
    x1 = nc.dram_tensor("x1", [NI, HW, HW, C], F32).ap()
    x2 = nc.dram_tensor("x2", [NI, HW, HW, C], F32).ap()
    x3t = nc.dram_tensor("x3t", [NI, C, TOK], F32).ap()
    dbl = nc.dram_tensor("dbl", [NI, 10, TOK], F32).ap()
    with ExitStack() as SEMS:
        with ExitStack() as ctx:
            layer0(nc, Phase(nc, ctx, "l0"), io, x1)
        with ExitStack() as ctx:
            layer1(nc, Phase(nc, ctx, "l1"), io, x1, x2)
        with ExitStack() as ctx:
            layer2(nc, Phase(nc, ctx, "l2"), io, x2, x3t)
        with ExitStack() as ctx:
            layer3(nc, ctx, io, x3t, dbl, out)


def kernel(**inputs):
    import concourse.bacc as bacc
    from concourse.bass_utils import run_bass_kernel_spmd

    a = layout(inputs)
    nc = bacc.Bacc("TRN2", target_bir_lowering=False, num_devices=1)
    arrays, io = {}, {}
    for name in USED:
        v = np.ascontiguousarray(a[name])
        arrays[f"in_{name}"] = v
        io[name] = nc.dram_tensor(f"in_{name}", v.shape, mybir.dt.from_np(v.dtype), kind="ExternalInput").ap()
    out = nc.dram_tensor("out_0", (NI, HW, HW, C), F32, kind="ExternalOutput").ap()
    program(nc, io, out)
    r = run_bass_kernel_spmd(nc, [arrays], core_ids=[0])
    return r.results[0]["out_0"]
```

```python
from contextlib import ExitStack

import numpy as np
import concourse.bass as bass
from concourse import mybir

F32 = mybir.dt.float32
F32R = mybir.dt.float32r
ALU = mybir.AluOpType
ACT = mybir.ActivationFunctionType
AX = mybir.AxisListType

NI = 4
HW = 64
TOK = HW * HW
C = 128
SEMS = None


class Lane:

    def __init__(self, sem):
        self.sem, self.n, self.ops, self.seen = sem, 0, [], {}

    def wait(self, *tokens):
        for token in tokens:
            if token is None:
                continue
            if isinstance(token, list):
                self.wait(*token)
                continue
            sem, value = token
            if self.seen.get(id(sem), 0) < value:
                self.seen[id(sem)] = value
                self.ops.append(lambda e, s=sem, v=value: e.wait_ge(s, v))

    def do(self, f, *tokens):
        self.wait(*tokens)
        self.ops.append(f)

    def sig(self, f, *tokens):
        self.wait(*tokens)
        self.n += 1
        self.ops.append(lambda e: f(e).then_inc(self.sem, 1))
        return self.sem, self.n

    def play(self, e):
        for f in self.ops:
            f(e)


class Load:

    def __init__(self, sem):
        self.sem, self.n = sem, 0

    def dma(self, lane, dst, src, *tokens, slow=False):
        lane.wait(*tokens)
        self.n += 16
        lane.ops.append(lambda e: e.dma_start(dst, src, allow_slow_non_contiguous=slow).then_inc(self.sem, 16))
        return self.sem, self.n


class Phase:

    def __init__(self, nc, ctx, name):
        self.nc, self.ctx, self.name, self.k = nc, ctx, name, 0
        self.pe, self.act, self.dve, self.pool, self.sp = (Lane(self.sem(x)) for x in ("pe", "act", "dve", "pool", "sp"))

    def sem(self, what):
        self.k += 1
        return SEMS.enter_context(self.nc.semaphore(f"{self.name}_{what}_{self.k}"))

    def load(self, what):
        return Load(self.sem(what))

    def sb(self, name, shape, dt=F32):
        return self.ctx.enter_context(self.nc.sbuf_tensor(f"{self.name}_{name}", shape, dt))

    def ps(self, name, shape, dt=F32):
        return self.ctx.enter_context(self.nc.psum_tensor(f"{self.name}_{name}", shape, dt))

    def run(self):
        with self.nc.Block() as block:
            block.sync(lambda e: self.sp.play(e))
            block.tensor(lambda e: self.pe.play(e))
            block.scalar(lambda e: self.act.play(e))
            block.vector(lambda e: self.dve.play(e))
            block.gpsimd(lambda e: self.pool.play(e))


class Ring:

    def __init__(self, tile, n, first=None):
        self.tile, self.n, self.k, self.free = tile, n, 0, [first] * n

    def take(self):
        i = self.k % self.n
        self.k += 1
        return i, self.tile[:, i], self.free[i]


def layer0(nc, P, io, vs, hls, x1):
    pe, act, dve, pool, sp = P.pe, P.act, P.dve, P.pool, P.sp
    R = lambda t: t.bitcast(F32)
    S32 = 32.0 ** -0.5
    NB = NI * 8
    N = NB * 4

    ident = P.sb("ident", [128, 128])
    wqkv = P.sb("wqkv", [128, 384])
    wp = P.sb("wp", [128, 128])
    g1w = P.sb("g1w", [128, 64])
    g2w = P.sb("g2w", [64, 1])
    cols = P.sb("cols", [128, 8])
    bvb = P.sb("bvb", [128, 128])
    pbb = P.sb("pbb", [128, 128])
    bm = P.sb("bm", [128, 36, 308])
    ks = P.sb("ks", [96, 4, TOK], F32R)
    qs = P.sb("qs", [96, 3, 4, 512], F32R)
    hl = P.sb("hl", [128, 2, 2, 512], F32R)
    xn = P.sb("xn", [128, 2, 512])
    xq = P.sb("xq", [128, 2, 512])
    vst = P.sb("vst", [128, 2, 512])
    gt = P.sb("gt", [64, 512])
    gate = P.sb("gate", [128, 3, 4 * NB])
    pr = P.sb("pr", [128, 3, 4, 308])
    vg = P.sb("vg", [128, 5, 3, 128])
    st = P.sb("st", [128, 4, 16])
    ptb = P.sb("ptb", [128, 2, 4, 384])
    on = P.sb("on", [128, 2, 128])
    ot = P.sb("ot", [128, 2, 128])
    tm = P.sb("tm", [128, 128])
    xs = P.sb("xs", [128, 7, 128])
    ys = P.sb("ys", [128, 3, 128])

    psS = P.ps("S", [128, 3, 512])
    psT = P.ps("T", [128, 2, 512])
    psO = P.ps("O", [128, 512])
    psF = P.ps("F", [128, 512])
    psP = P.ps("P", [128, 512])

    lw = P.load("w")
    lb = P.load("b")
    for dst, src in ((wqkv[:], io["L0_conv_qkv_w"]), (ident[:], io["ident"]), (wp[:], io["L0_conv_proj_w"]),
                     (g1w[:], io["L0_conv_g1_w"]), (g2w[:], io["L0_conv_g2_w"]),
                     (cols[:, 0:3], io["L0_conv_qkv_b"].rearrange("(t p) -> p t", p=128)),
                     (cols[0:64, 3:4], io["L0_conv_g1_b"].rearrange("(p a) -> p a", a=1)),
                     (cols[:, 4:5], io["L0_conv_g2_b"].rearrange("(a p) -> a p", a=1).broadcast_to([128, 1])),
                     (bvb[:], io["L0_conv_qkv_b"].rearrange("(a p) -> a p", a=1)[:, 256:384].broadcast_to([128, 128])),
                     (pbb[:], io["L0_conv_proj_b"].rearrange("(a p) -> a p", a=1).broadcast_to([128, 128]))):
        w = lw.dma(sp, dst, src, slow=True)
    b1 = lb.dma(act, pr[:].rearrange("p a b n -> p (a b) n")[:, 0:9, :], io["mask"].rearrange("k p n -> p k n"))
    for k in range(9):
        b1 = lb.dma(act, bm[:, 4 * k:4 * k + 4, :], io["rpbx"][4 * k:4 * k + 4].rearrange("k p n -> p k n"))
    ln, lq = [P.load("xn") for _ in range(2)], [P.load("xq") for _ in range(2)]
    lh = [[P.load("h") for _ in range(2)] for _ in range(4)]
    lk, lqs, lv = [P.load("k") for _ in range(4)], [P.load("q") for _ in range(3)], [P.load("v") for _ in range(4)]
    lg, lt, lo = [P.load("g") for _ in range(5)], [P.load("t") for _ in range(7)], [P.load("o") for _ in range(3)]

    z1 = dve.sig(lambda e: e.memset(psT[:], 0.0))
    dve.sig(lambda e: e.tensor_scalar(cols[:, 0:1], cols[:, 0:1], S32, None, ALU.mult), w)
    dve.sig(lambda e: e.tensor_scalar(wqkv[:, 0:128], wqkv[:, 0:128], S32, None, ALU.mult), w)
    d0 = dve.sig(lambda e: e.tensor_scalar(cols[:, 4:5], cols[:, 4:5], -1.0, None, ALU.mult), w)

    xin, xnf, xqf = {}, [None] * 2, [None] * 2
    hif = [None, None]
    vstf = [None, None]
    scored, stack, vdone = {}, {}, {}
    qsf = [None] * 3
    pfree = [None]
    gtf = [None]
    gates, hidden = {}, {}

    def fetch(G):
        b, rb = divmod(G, 8)
        s = G % 2
        sl = slice(512 * rb, 512 * rb + 512)
        xin[G] = (ln[s].dma(sp, xn[:, s, :], io["xT"][b, :, sl], xnf[s]), lq[s].dma(sp, xq[:, s, :], io["xqT"][b, :, sl], xqf[s]))

    def split(G, which):
        b, rb = divmod(G, 8)
        s = G % 2
        X, t = (xq, xin[G][1]) if which == 0 else (xn, xin[G][0])
        t = pe.sig(lambda e: e.matmul(psP[:], wqkv[:, 128 * which:128 * which + 128], X[:, s, :], start=True, stop=True), t, d0, pfree[0])
        u = which
        a = act.sig(lambda e: e.activation(hl[:, u, 0, :], psP[:], ACT.Identity, bias=cols[:, which:which + 1]), t, hif[u])
        d = pfree[0] = dve.sig(lambda e: e.scalar_tensor_tensor(hl[:, u, 1, :], psP[:], cols[:, which:which + 1], R(hl[:, u, 0, :]), ALU.add, ALU.subtract), a)
        if which == 0:
            dst, ld, wait = qs[:, G % 3], lqs[G % 3], qsf[G % 3]
            order = (0, 1, 0)
        else:
            dst, ld, wait = ks[:, :, 512 * rb:512 * rb + 512], lk[G % 4], scored.get(min(G - 7, 8 * b - 1))
            order = (0, 0, 1)
        slot = hls[2 * (G % 4) + which]
        d2 = hif[u] = lh[G % 4][which].dma(sp, slot.rearrange("s c n -> c s n"), R(hl[:, u]), a, d)
        for k, j in enumerate(order):
            d3 = ld.dma(sp, R(dst[32 * k:32 * k + 32]), slot[j].rearrange("(h p) n -> p h n", h=4), d2, wait)
        stack[G, which] = d3

    def values(G):
        b, rb = divmod(G, 8)
        s = G % 2
        for k in range(4):
            t = pe.sig(lambda e, k=k: e.matmul(psP[:, 128 * k:128 * k + 128], xn[:, s, 128 * k:128 * k + 128], wqkv[:, 256:384], start=True, stop=True), xin[G][0], pfree[0], w)
        xnf[s] = t
        d = pfree[0] = dve.sig(lambda e: e.tensor_tensor(vst[:, s, :].rearrange("p (k c) -> p k c", k=4), psP[:].rearrange("p (k c) -> p k c", k=4),
                                                         bvb[:].rearrange("p (a c) -> p a c", a=1).broadcast_to([128, 4, 128]), ALU.add), t, w, vstf[s])
        vdone[G] = vstf[s] = lv[G % 4].dma(sp, vs[b, 8 * rb:8 * rb + 8].rearrange("(t r) c d -> (r c) t d", r=2), vst[:, s, :].rearrange("p (t c) -> p t c", t=4), d)

    def gating(G):
        s = G % 2
        t = pe.sig(lambda e: e.matmul(psP[0:64, :], g1w[:], xq[:, s, :], start=True, stop=True), xin[G][1], pfree[0], w)
        xqf[s] = t
        a = act.sig(lambda e: e.activation(gt[:], psP[0:64, :], ACT.Relu, bias=cols[0:64, 3:4]), t, gtf[0], d0)
        hidden[G] = pfree[0] = a

    def opening(G):
        a = hidden[G]
        for k in range(4):
            t = pe.sig(lambda e, k=k: e.matmul(psP[:, k:k + 1], gt[:, 128 * k:128 * k + 128], g2w[:], start=True, stop=True), a, pfree[0])
        gtf[0] = t
        sl = slice(4 * G, 4 * G + 4)
        a = pfree[0] = act.sig(lambda e: e.activation(gate[:, 0, sl], psP[:, 0:4], ACT.Exp, bias=cols[:, 4:5], scale=-1.0), t)
        a = dve.sig(lambda e: e.tensor_scalar(gate[:, 1, sl], gate[:, 0, sl], 1.0, None, ALU.add), a)
        gates[G] = dve.sig(lambda e: e.reciprocal(gate[:, 2, sl], gate[:, 1, sl]), a)

    for G in range(2):
        fetch(G)
    for G in range(2):
        split(G, 0)
        split(G, 1)
        values(G)
        gating(G)
        opening(G)
        fetch(G + 2)
    for k in range(9):
        db = dve.sig(lambda e, k=k: e.tensor_tensor(bm[:, 4 * k:4 * k + 4, :], bm[:, 4 * k:4 * k + 4, :],
                     pr[:, k // 4, k % 4:k % 4 + 1, :].broadcast_to([128, 4, 308]), ALU.add), b1)

    kimg = ks[:].rearrange("p a (h w) -> p a h w", w=HW)
    rS, rT = Ring(psS, 3), Ring(psT, 2, z1)
    prf, ptf, vgf = [db] * 3, [[None] * 4 for _ in range(2)], [None] * 5
    sumd = {}
    onf, otf, xsf = [None] * 2, [None] * 2, [None] * 7
    ofree, ffree, tmf = [None], [None], [None]
    info = {}

    def where(n):
        G, i = divmod(n, 4)
        b, rb = divmod(G, 8)
        r0, c0 = 8 * rb, 16 * i
        return b, r0, c0, min(max(r0 - 3, 0), 50), min(max(c0 - 3, 0), 42)

    def bring(n):
        b, r0, c0, kr, kc = where(n)
        G = n // 4
        for j, (o, m) in enumerate(((0, 5), (5, 5), (10, 4))):
            info["v", n] = lg[n % 5].dma(sp, vg[0:22 * m, n % 5, j, :], vs[b, kr + o:kr + o + m, kc:kc + 22, :],
                                         *[vdone[x] for x in (G - 1, G, G + 1) if x // 8 == b and x in vdone], vgf[n % 5])
        info["x", n] = lt[n % 7].dma(pool, xs[:, n % 7, :], io["x"][b, r0:r0 + 8, c0:c0 + 16, :], xsf[n % 7])

    def score(n, h):
        b, r0, c0, kr, kc = where(n)
        G, i4 = divmod(n, 4)
        cls = 3 * {0: 0, 3: 1, 6: 2}[r0 - kr] + {0: 0, 3: 1, 6: 2}[c0 - kc]
        s = n % 3
        i, X, f = rS.take()
        need = [stack[x, 1] for x in (G - 1, G, G + 1) if x // 8 == b and (x, 1) in stack] + [stack[G, 0]]
        t = pe.sig(lambda e: e.matmul(X[:, 0:308], qs[:, G % 3, h, 128 * i4:128 * i4 + 128], kimg[:, h, kr:kr + 14, kc:kc + 22],
                                      start=True, stop=True), f, *need)
        if h == 3 and i4 == 3:
            scored[G] = qsf[G % 3] = t
        rS.free[i] = d = dve.sig(lambda e: e.tensor_tensor_reduce(pr[:, s, h, :], X[:, 0:308], bm[:, 4 * cls + h, :], 1.0, -3.0e38,
                                                                  ALU.add, ALU.max, st[:, n % 4, h:h + 1]), t, db, prf[s], sumd.get(n - 4))
        if h == 3:
            info["m", n] = dve.sig(lambda e: e.tensor_scalar(st[:, n % 4, 4:8], st[:, n % 4, 0:4], -1.0, None, ALU.mult), d)

    def expo(n, h):
        s = n % 3
        info["e", n, h] = act.sig(lambda e: e.activation(pr[:, s, h, :], pr[:, s, h, :], ACT.Exp, bias=st[:, n % 4, 4 + h:5 + h],
                                                         accum_out=st[:, n % 4, 8 + h:9 + h]), info["m", n])

    def turn(n, h):
        i, X, f = rT.take()
        s = n % 3
        for j, (o, m) in enumerate(((0, 110), (110, 110), (220, 88))):
            t = pe.sig(lambda e, j=j, o=o, m=m: e.transpose(X[0:m, 128 * j:128 * j + 128], pr[:, s, h, o:o + m], ident[:]), f, info["e", n, h], w)
        if h == 3:
            prf[s] = t
        v = ptb[0:110, n % 2, h, :]
        if h % 2 == 0:
            rT.free[i] = act.sig(lambda e: e.activation(v, X[0:110, 0:384], ACT.Copy), t, ptf[n % 2][h])
        else:
            rT.free[i] = dve.sig(lambda e: e.tensor_copy(v, X[0:110, 0:384]), t, ptf[n % 2][h])
        info["p", n, h] = rT.free[i]

    def attend(n, h):
        for j, m in enumerate((110, 110, 88)):
            t = pe.sig(lambda e, j=j, m=m: e.matmul(psO[:, 32 * h:32 * h + 32], ptb[0:m, n % 2, h, 128 * j:128 * j + 128], vg[0:m, n % 5, j, 32 * h:32 * h + 32],
                                                    start=(j == 0), stop=(j == 2)), info["p", n, h], info["v", n], ofree[0])
        ptf[n % 2][h] = t
        if h == 3:
            vgf[n % 5] = t
            s = n % 4
            d = sumd[n] = dve.sig(lambda e: e.reciprocal(st[:, s, 12:16], st[:, s, 8:12]), info["e", n, 3])
            ofree[0] = info["n", n] = sumd[n] = dve.sig(lambda e: e.tensor_tensor(on[:, n % 2, :].rearrange("p (h d) -> p h d", h=4), psO[:, 0:128].rearrange("p (h d) -> p h d", h=4),
                                                                st[:, s, 12:16].rearrange("p (h a) -> p h a", a=1).broadcast_to([128, 4, 32]), ALU.mult), t, d, onf[n % 2])

    def flip(n):
        s = n % 2
        t = onf[s] = pe.sig(lambda e: e.transpose(psF[:, 0:128], on[:, s, :], ident[:]), info["n", n], ffree[0])
        ffree[0] = info["f", n] = act.sig(lambda e: e.activation(ot[:, s, :], psF[:, 0:128], ACT.Copy), t, otf[s])

    def finish(n):
        b, r0, c0, _, _ = where(n)
        s = n % 2
        t = otf[s] = pe.sig(lambda e: e.matmul(psF[:, 128:256], ot[:, s, :], wp[:], start=True, stop=True), info["f", n], ffree[0])
        ffree[0] = d = dve.sig(lambda e: e.tensor_tensor(tm[:], psF[:, 128:256], pbb[:], ALU.add), t, w, tmf[0])
        xsf[n % 7] = tmf[0] = d = dve.sig(lambda e: e.scalar_tensor_tensor(ys[:, n % 3, :], tm[:], gate[:, 2, n:n + 1], xs[:, n % 7, :], ALU.mult, ALU.add),
                                          d, info["x", n], gates[n // 4], info.get(("s", n - 3)))
        info["s", n] = lo[n % 3].dma(pool, x1[b, r0:r0 + 8, c0:c0 + 16, :], ys[:, n % 3, :], d)

    bring(0)
    for n in range(N + 6):
        G = n // 4 + 2
        if n % 4 == 0:
            if 2 < G <= NB:
                opening(G - 1)
            if G < NB:
                split(G, 1)
        elif G < NB and n % 4 == 1:
            split(G, 0)
        elif G < NB and n % 4 == 2:
            values(G)
        elif G < NB:
            gating(G)
            if G + 2 < NB:
                fetch(G + 2)
        if 0 <= n - 4 < N:
            flip(n - 4)
        for h in range(4):
            if n < N:
                score(n, h)
            if 0 <= n - 1 < N:
                expo(n - 1, h)
            if 0 <= n - 2 < N:
                turn(n - 2, h)
            if 0 <= n - 3 < N:
                attend(n - 3, h)
            if h == 1 and 0 <= n - 5 < N:
                finish(n - 5)
        if n + 1 < N:
            bring(n + 1)
    pool.wait(*[info["s", N - 1 - i] for i in range(3)])
    P.run()


def layer1(nc, P, io, x1, x1t, x2):
    pe, act, dve, pool, sp = P.pe, P.act, P.dve, P.pool, P.sp
    SC = float(C) ** -0.5
    R = lambda t: t.bitcast(F32)

    ident = P.sb("ident", [128, 128])
    wraw = P.sb("wraw", [128, 4, 128])
    wh = P.sb("wh", [128, 3, 128], F32R)
    wl = P.sb("wl", [128, 3, 128], F32R)
    cols = P.sb("cols", [128, 8])
    bob = P.sb("bob", [128, 128])
    grp = P.sb("grp", [128, 128])
    zero = P.sb("zero", [128, 1])
    pr = P.sb("pr", [128, 5, TOK])
    qh, ql = P.sb("qh", [128, TOK], F32R), P.sb("ql", [128, TOK], F32R)
    kh, kl = P.sb("kh", [128, TOK], F32R), P.sb("kl", [128, TOK], F32R)
    vh, vl = P.sb("vh", [128, 32, 128], F32R), P.sb("vl", [128, 32, 128], F32R)
    ph, pl = P.sb("ph", [128, 2, 512], F32R), P.sb("pl", [128, 2, 512], F32R)
    xc = P.sb("xc", [128, 2, 512])
    nh, nl = P.sb("nh", [128, 2, 512], F32R), P.sb("nl", [128, 2, 512], F32R)
    st = P.sb("st", [128, 5, 20])
    bn = P.sb("bn", [128, 8, 6])
    gs = P.sb("gs", [128, 2, 16])
    ots = P.sb("ots", [128, 256])
    xs = P.sb("xs", [128, 2, 128])
    ys = P.sb("ys", [128, 2, 128])

    psS = P.ps("S", [128, 3, 512])
    psT = P.ps("T", [128, 2, 512])
    psO = P.ps("O", [128, 2, 512])
    psF = P.ps("F", [128, 512])

    def row(name):
        return io[name].rearrange("(a p) -> a p", a=1).broadcast_to([128, 128])

    def col(name):
        return io[name].rearrange("(p a) -> p a", a=1)

    lw = P.load("w")
    for dst, src in ((ident[:], io["ident"]), (grp[:], io["group"]), (wraw[:, 0, :], io["L1_conv_wq"]), (wraw[:, 1, :], io["L1_conv_wk"]),
                     (wraw[:, 2, :], io["L1_conv_wv"]), (wraw[:, 3, :], io["L1_conv_wo"]),
                     (cols[:, 0:1], col("L1_conv_bq")), (cols[:, 1:2], col("L1_conv_bk")), (cols[:, 2:3], col("L1_conv_gn_scale")),
                     (cols[:, 3:4], col("L1_conv_gn_bias")), (cols[:, 4:5], col("L1_conv_bv")), (bob[:], row("L1_conv_bo"))):
        w = lw.dma(sp, dst, src, slow=True)
    li = [P.load("i0"), P.load("i1")]
    lx = [P.load("x0"), P.load("x1")]
    lt = [P.load("t0"), P.load("t1")]
    lo = [P.load("o0"), P.load("o1")]

    dve.sig(lambda e: e.memset(zero[:], 0.0))
    a = dve.sig(lambda e: e.tensor_copy(wh[:], wraw[:, 0:3, :]), w)
    wt = dve.sig(lambda e: e.tensor_tensor(wl[:], wraw[:, 0:3, :], R(wh[:]), ALU.subtract), a)
    t = pe.sig(lambda e: e.matmul(psF[:, 0:128], cols[:, 4:5].broadcast_to([128, 128]), wraw[:, 3, :], start=True, stop=True), w)
    wb = dve.sig(lambda e: e.tensor_tensor(bob[:], bob[:], psF[:, 0:128], ALU.add), t)

    sfree, sn = [None] * 3, [0]
    tfree, pfree = [None] * 2, [None] * 2
    ofree, ffree = [None, None], None
    slot = [None] * 5
    xsfree, ysfree = [None, None], [None, None]
    otsfree = None
    info = {}

    def bank():
        i = sn[0] % 3
        sn[0] += 1
        return i

    def three(out, lh, ll, rh, rl, *waits):
        pe.do(lambda e: e.matmul(out, lh, rh, start=True, stop=False), *waits)
        pe.do(lambda e: e.matmul(out, ll, rh, start=False, stop=False))
        return pe.sig(lambda e: e.matmul(out, lh, rl, start=False, stop=True))

    xr = Ring(xc, 2)
    nfree, nn = [None] * 2, [0]
    ready = {}

    def fetch_raw(b, ch):
        i, x, f = xr.take()
        ready["raw"] = i, x, li[i].dma(sp, x.rearrange("p (t c) -> p t c", c=128), x1[b, 8 * ch:8 * ch + 8].rearrange("(t r) c d -> (r c) t d", r=2), f)

    def channels(b, ch):
        i0, raw, ld = ready.pop("raw")
        i = bank()
        for k in range(4):
            t = pe.sig(lambda e, k=k: e.transpose(psS[:, i, 128 * k:128 * k + 128], raw[:, 128 * k:128 * k + 128], ident[:]), ld, sfree[i], w)
        if i0 is None:
            slot[4] = t
        else:
            xr.free[i0] = t
        i1, x, f = xr.take()
        a = sfree[i] = act.sig(lambda e: e.activation(x, psS[:, i, :], ACT.Copy), t, f)
        d = ready["bn"] = dve.sig(lambda e: e.bn_stats(bn[:, ch, :], x), a)
        ready["t", b, ch] = lx[i1].dma(sp, x1t[b, :, 512 * ch:512 * ch + 512], x, a)
        xr.free[i1] = [d, ready["t", b, ch]]

    def moments(b, part_):
        g = gs[:, b % 2]
        if part_ == 0:
            ready["m"] = dve.sig(lambda e: e.bn_aggr(g[:, 0:2], bn[:].rearrange("p a b -> p (a b)")), ready["bn"], ready.get(("last", b - 2)))
        elif part_ == 1:
            i = bank()
            t = pe.sig(lambda e: e.matmul(psS[:, i, 0:2], grp[:], g[:, 0:2], start=True, stop=True), ready["m"], sfree[i])
            s = sfree[i] = dve.sig(lambda e: e.tensor_copy(g[:, 2:4], psS[:, i, 0:2]), t)
            s = dve.sig(lambda e: e.tensor_tensor(g[:, 4:5], g[:, 0:1], g[:, 2:3], ALU.subtract), s)
            ready["m"] = dve.sig(lambda e: e.tensor_tensor(g[:, 5:6], g[:, 4:5], g[:, 4:5], ALU.mult), s)
        else:
            i = bank()
            t = pe.sig(lambda e: e.matmul(psS[:, i, 0:1], grp[:], g[:, 5:6], start=True, stop=True), ready["m"], sfree[i])
            s = sfree[i] = dve.sig(lambda e: e.tensor_tensor(g[:, 6:7], psS[:, i, 0:1], g[:, 3:4], ALU.add), t)
            s = dve.sig(lambda e: e.tensor_scalar(g[:, 11:12], g[:, 6:7], 1.0e-6, None, ALU.add), s)
            s = act.sig(lambda e: e.activation(g[:, 12:13], g[:, 11:12], ACT.Sqrt), s)
            s = dve.sig(lambda e: e.reciprocal(g[:, 9:10], g[:, 12:13]), s)
            s = dve.sig(lambda e: e.tensor_tensor(g[:, 7:8], g[:, 9:10], cols[:, 2:3], ALU.mult), s, w)
            s = dve.sig(lambda e: e.tensor_tensor(g[:, 10:11], g[:, 2:3], g[:, 7:8], ALU.mult), s)
            ready["g", b] = dve.sig(lambda e: e.tensor_tensor(g[:, 8:9], cols[:, 3:4], g[:, 10:11], ALU.subtract), s)

    def fetch_norm(b, ch, kind):
        i, x, f = xr.take()
        ready["x", b, ch, kind] = i, x, li[i].dma(sp, x, x1t[b, :, 512 * ch:512 * ch + 512], ready["t", b, ch], f)

    def normal(b, ch, kind):
        i, x, ld = ready.pop(("x", b, ch, kind))
        g = gs[:, b % 2]
        z = nn[0] % 2
        nn[0] += 1
        a = act.sig(lambda e: e.activation(nh[:, z, :], x, ACT.Identity, bias=g[:, 8:9], scale=g[:, 7:8]), ld, ready["g", b], nfree[z])
        d = ready["last", b] = dve.sig(lambda e: e.tensor_scalar(x, x, g[:, 7:8], g[:, 8:9], ALU.mult, ALU.add), a)
        p = xr.free[i] = pool.sig(lambda e: e.tensor_tensor(nl[:, z, :], x, R(nh[:, z, :]), ALU.subtract), d)
        ready["n", b, ch, kind] = z, p

    def product(b, ch, kind):
        z, p = ready.pop(("n", b, ch, kind))
        sl = slice(512 * ch, 512 * ch + 512)
        if kind == 0:
            for k, (dh, dl) in enumerate(((kh, kl), (qh, ql))):
                k = 1 - k
                i = bank()
                t = three(psS[:, i, :], wh[:, k, :], wl[:, k, :], nh[:, z, :], nl[:, z, :], p, wt, sfree[i])
                u = act.sig(lambda e, i=i, dh=dh, k=k: e.activation(dh[:, sl], psS[:, i, :], ACT.Identity, bias=cols[:, k:k + 1]), t, ready.get(("qk", b - 1)), w)
                sfree[i] = dve.sig(lambda e, i=i, dh=dh, dl=dl, k=k: e.scalar_tensor_tensor(dl[:, sl], psS[:, i, :], cols[:, k:k + 1], R(dh[:, sl]),
                                                                                         ALU.add, ALU.subtract), u)
            ready["kq", b, ch] = sfree[i]
        else:
            i = bank()
            pe.wait(sfree[i], p)
            for k in range(4):
                tk = slice(128 * k, 128 * k + 128)
                t = three(psS[:, i, tk], nh[:, z, tk], nl[:, z, tk], wh[:, 2, :], wl[:, 2, :])
            v = psS[:, i, :].rearrange("p (t c) -> p t c", c=128)
            sl4 = slice(4 * ch, 4 * ch + 4)
            u = act.sig(lambda e: e.activation(vh[:, sl4, :], v, ACT.Copy), t, ready.get(("pv", b - 1, 2 * ch + 1)))
            sfree[i] = ready["v", b, ch] = dve.sig(lambda e: e.tensor_tensor(vl[:, sl4, :], v, R(vh[:, sl4, :]), ALU.subtract), u)
        nfree[z] = t

    pending = []

    def qk(b, u):
        q, kc = divmod(u, 8)
        s = (32 * b + q) % 5
        i = bank()
        qs, ks = slice(128 * q, 128 * q + 128), slice(512 * kc, 512 * kc + 512)
        t = ready["qk", b] = three(psS[:, i, :], qh[:, qs], ql[:, qs], kh[:, ks], kl[:, ks], ready["kq", b, kc], ready["kq", b, q // 4], sfree[i])
        d = sfree[i] = dve.sig(lambda e: e.tensor_tensor_reduce(pr[:, s, ks], psS[:, i, :], zero[:].broadcast_to([128, 512]), 1.0, -3.0e38,
                                                                ALU.add, ALU.max, st[:, s, kc:kc + 1]), t, slot[s])
        if kc == 7:
            d = dve.sig(lambda e: e.tensor_reduce(st[:, s, 8:9], st[:, s, 0:8], AX.X, ALU.max), d)
            d = dve.sig(lambda e: e.tensor_scalar(st[:, s, 9:10], st[:, s, 8:9], -SC, None, ALU.mult), d)
            for k in range(8):
                pending.append((32 * b + q, s, k, d, 256 * b + u - 24 + 1))

    def exps(step):
        if pending and pending[0][4] <= step:
            q, s, k, d, _ = pending.pop(0)
            es = slice(512 * k, 512 * k + 512)
            info["e", q, k] = act.sig(lambda e: e.activation(pr[:, s, es], pr[:, s, es], ACT.Exp, bias=st[:, s, 9:10], scale=SC,
                                                         accum_out=st[:, s, 10 + k:11 + k]), d)

    def turn(v):
        g, j = divmod(v, 16)
        i = v % 2
        for q in range(2):
            s = (2 * g + q) % 5
            for k in range(2):
                kt = 2 * j + k
                t = pe.sig(lambda e, k=k, q=q, s=s, kt=kt: e.transpose(psT[:, i, 256 * k + 128 * q:256 * k + 128 * q + 128], pr[:, s, 128 * kt:128 * kt + 128], ident[:]),
                           info["e", 2 * g + q, j // 2], tfree[i])
        if j == 15:
            slot[2 * g % 5] = slot[(2 * g + 1) % 5] = t
        a = act.sig(lambda e: e.activation(ph[:, i, :], psT[:, i, :], ACT.Copy), t, pfree[i])
        tfree[i] = info["p", v] = dve.sig(lambda e: e.tensor_tensor(pl[:, i, :], psT[:, i, :], R(ph[:, i, :]), ALU.subtract), a)

    def pv(b, v):
        g, j = divmod(v, 16)
        i, o = v % 2, g % 2
        out = psO[:, o, 0:256]
        for k in range(2):
            kt = 2 * j + k
            ks = slice(256 * k, 256 * k + 256)
            pe.do(lambda e, kt=kt, ks=ks, f=(j == 0 and k == 0): e.matmul(out, vh[:, kt, :], ph[:, i, ks], start=f, stop=False), info["p", 256 * b + v], ofree[o], ready["v", b, j // 2])
            pe.do(lambda e, kt=kt, ks=ks: e.matmul(out, vl[:, kt, :], ph[:, i, ks], start=False, stop=False))
            t = pe.sig(lambda e, kt=kt, ks=ks, f=(j == 15 and k == 1): e.matmul(out, vh[:, kt, :], pl[:, i, ks], start=False, stop=f))
        pfree[i] = t
        if v >= 240:
            ready["pv", b, j] = t
        if j == 15:
            for q in range(2):
                n = 2 * g + q
                info["x", n] = lt[q].dma(sp, xs[:, q, :], x1[b, 2 * n:2 * n + 2].rearrange("r c d -> (r c) d"), xsfree[q])
            info["o"] = (b, g, t)

    def out1():
        nonlocal otsfree
        b, g, t = info["o"]
        o = g % 2
        a = ofree[o] = act.sig(lambda e: e.activation(ots[:], psO[:, o, 0:256], ACT.Copy), t, otsfree)
        info["a"] = a

    def out2():
        nonlocal ffree, otsfree
        b, g, _ = info.pop("o")
        for q in range(2):
            n = 2 * g + q
            t = pe.sig(lambda e, q=q: e.matmul(psF[:, 128 * q:128 * q + 128], ots[:, 128 * q:128 * q + 128], wraw[:, 3, :], start=True, stop=True), info["a"], ffree)
        otsfree = t
        for q in range(2):
            n = 2 * g + q
            s = (32 * b + n) % 5
            r = dve.sig(lambda e, s=s: e.tensor_reduce(st[:, s, 18:19], st[:, s, 10:18], AX.X, ALU.add), info["e", 32 * b + n, 7])
            r = dve.sig(lambda e, s=s: e.reciprocal(st[:, s, 19:20], st[:, s, 18:19]), r)
            x = pool.sig(lambda e, q=q: e.tensor_tensor(xs[:, q, :], xs[:, q, :], bob[:], ALU.add), info["x", n], wb)
            d = xsfree[q] = ffree = dve.sig(lambda e, q=q, s=s: e.scalar_tensor_tensor(ys[:, q, :], psF[:, 128 * q:128 * q + 128], st[:, s, 19:20], xs[:, q, :],
                                                                           ALU.mult, ALU.add), t, r, x, ysfree[q])
            ysfree[q] = lo[q].dma(sp, x2[b, 2 * n:2 * n + 2].rearrange("r c d -> (r c) d"), ys[:, q, :], d)

    at = {}

    def plan(step, f, *args):
        at.setdefault(step, []).append((f, args))

    first = pr[:, 4, :]
    halves = []
    for hf in range(2):
        halves.append(li[hf].dma(sp, first[:, 2048 * hf:2048 * hf + 2048].rearrange("p (t c) -> p t c", c=128), x1[0, 32 * hf:32 * hf + 32].rearrange("(t r) c d -> (r c) t d", r=2)))
    for hf, ld in enumerate(halves):
        for ch in range(4 * hf, 4 * hf + 4):
            ready["raw"] = None, first[:, 512 * ch:512 * ch + 512], ld
            channels(0, ch)
    for k in range(3):
        moments(0, k)
    for b in range(NI):
        base = 256 * b
        if b + 1 < NI:
            for ch in range(8):
                plan(base + 12 + 22 * ch, fetch_raw, b + 1, ch)
                plan(base + 18 + 22 * ch, channels, b + 1, ch)
            for k in range(3):
                plan(base + 190 + 2 * k, moments, b + 1, k)
        for kind, first, every in ((0, -26, 1), (1, -14, 2)):
            for ch in range(8):
                t = base + first + every * ch
                plan(t, product, b, ch, kind)
                plan(t - 2, normal, b, ch, kind)
                plan(t - 4, fetch_norm, b, ch, kind)
    for jobs in at.values():
        jobs.sort(key=lambda j: (product, normal, channels, moments, fetch_norm, fetch_raw).index(j[0]))
    for step in range(-30, 256 * NI + 4):
        for f, args in at.get(step, ()):
            f(*args)
        if 0 <= step + 24 < 256 * NI:
            qk(*divmod(step + 24, 256))
        if 0 <= step + 1 < 256 * NI:
            turn(step + 1)
        exps(step)
        if 0 <= step < 256 * NI:
            pv(*divmod(step, 256))
        if "o" in info and step % 16 == 1:
            out1()
        elif "o" in info and step % 16 == 3:
            out2()
    sp.wait(*ysfree)
    P.run()


def layer2(nc, P, io, x2, x3t):
    pe, act, dve, pool, sp = P.pe, P.act, P.dve, P.pool, P.sp
    ident = P.sb("ident", [128, 128])
    wts = P.sb("wts", [128, 5, 128])
    cols = P.sb("cols", [128, 8])
    bob = P.sb("bob", [128, 128])
    x = P.sb("x", [128, 2, 32, 128])
    xt = P.sb("xt", [128, 2, TOK])
    rs = P.sb("rs", [128, 3, 64])
    ee = P.sb("ee", [128, 2, 512])
    ll = P.sb("ll", [128, 2, 512])
    bn = P.sb("bn", [128, 32, 6])
    mv = P.sb("mv", [128, 2, 32, 2])
    rstd = P.sb("rstd", [128, 3, 32])
    o3 = P.sb("o3", [128, 2, 512])
    psA = P.ps("A", [128, 2, 512])
    psG = P.ps("G", [128, 2, 512])
    psO = P.ps("O", [128, 2, 512])
    psX = P.ps("X", [128, 2, 512])

    def col(name):
        return io[name].rearrange("(p a) -> p a", a=1)

    lw = P.load("w")
    for dst, src in ((ident[:], io["ident"]), (wts[:, 0, :], io["L2_conv_W_left"]), (wts[:, 1, :], io["L2_conv_W_eq"]),
                     (wts[:, 2, :], io["L2_conv_W_right"]), (wts[:, 3, :], io["L2_conv_W_gate"]), (wts[:, 4, :], io["L2_conv_W_out"]),
                     (cols[:, 0:1], col("L2_conv_b_left")), (cols[:, 1:2], col("L2_conv_b_eq")), (cols[:, 2:3], col("L2_conv_b_right")),
                     (cols[:, 3:4], col("L2_conv_b_gate")), (cols[:, 4:5], col("L2_conv_ln_scale")), (cols[:, 5:6], col("L2_conv_ln_bias")),
                     (bob[:], io["L2_conv_b_out"].rearrange("(a p) -> a p", a=1).broadcast_to([128, 128]))):
        w = lw.dma(sp, dst, src, slow=True)
    li = [P.load("i0"), P.load("i1")]
    lo = [P.load("o0"), P.load("o1")]
    dve.sig(lambda e: e.tensor_tensor(wts[:, 0, :], wts[:, 0, :], wts[:, 1, :], ALU.add), w)
    dve.sig(lambda e: e.tensor_tensor(cols[:, 0:1], cols[:, 0:1], cols[:, 1:2], ALU.add), w)
    dve.sig(lambda e: e.tensor_scalar(cols[:, 2:3], cols[:, 2:3], 64.0, None, ALU.mult), w)
    wk = dve.sig(lambda e: e.tensor_scalar(cols[:, 3:4], cols[:, 3:4], -1.0, None, ALU.mult), w)

    bx, nx = [None] * 2, [0]
    bo, no = [None] * 2, [0]
    ba, bg = [None] * 2, [None] * 2
    eef, llf, o3f = [None] * 2, [None] * 2, [None] * 2
    xfree, xtfree, mvfree = [None] * 2, [None] * 2, None
    pend = []

    def chunk(b, ch, rsok, xok, xtok):
        s = ch % 2
        sl = slice(512 * ch, 512 * ch + 512)
        X = xt[:, b % 2, sl]
        t1 = pe.sig(lambda e: e.matmul(psG[:, s, :], wts[:, 3, :], X, start=True, stop=True), xtok, bg[s])
        t2 = pe.sig(lambda e: e.matmul(psA[:, s, :], wts[:, 0, :], X, start=True, stop=True), ba[s], wk)
        a = bg[s] = act.sig(lambda e: e.activation(ee[:, s, :], psG[:, s, :], ACT.Exp, bias=cols[:, 3:4], scale=-1.0), t1, wk, eef[s])
        a = pool.sig(lambda e: e.tensor_scalar(ee[:, s, :], ee[:, s, :], 1.0, None, ALU.add), a)
        d = dve.sig(lambda e: e.reciprocal(ee[:, s, :], ee[:, s, :]), a)
        d2 = ba[s] = dve.sig(lambda e: e.scalar_tensor_tensor(ll[:, s, :].rearrange("p (r c) -> p r c", c=64), psA[:, s, :].rearrange("p (r c) -> p r c", c=64),
                                                             cols[:, 0:1], rs[:, 2, 8 * ch:8 * ch + 8].rearrange("p (r a) -> p r a", a=1).broadcast_to([128, 8, 64]),
                                                             ALU.add, ALU.mult), t2, rsok, llf[s])
        d2 = eef[s] = dve.sig(lambda e: e.tensor_tensor(ll[:, s, :], ll[:, s, :], ee[:, s, :], ALU.mult), d2, d)
        v = x[:, b % 2, 4 * ch:4 * ch + 4, :]
        xb = pool.sig(lambda e: e.tensor_tensor(v, v, bob[:].rearrange("p (a c) -> p a c", a=1).broadcast_to([128, 4, 128]), ALU.add), xok, xtok, w)
        return lambda: tail(b, ch, s, d2, xb)

    def tail(b, ch, s, d2, xb):
        i = ch % 2
        v = x[:, b % 2, 4 * ch:4 * ch + 4, :]
        for k in range(4):
            t = pe.sig(lambda e, k=k: e.matmul(psO[:, i, 128 * k:128 * k + 128], ll[:, s, 128 * k:128 * k + 128], wts[:, 4, :], start=True, stop=True), d2, bo[i], w)
        llf[s] = t
        y = bo[i] = dve.sig(lambda e: e.tensor_tensor(v, psO[:, i, :].rearrange("p (k c) -> p k c", k=4), v, ALU.add), t, xb)
        for k in range(4):
            q = dve.sig(lambda e, k=k: e.bn_stats(bn[:, 4 * ch + k, :], v[:, k, :]), y)
        for k in range(4):
            q = dve.sig(lambda e, k=k: e.bn_aggr(mv[:, b % 2, 4 * ch + k, :], bn[:, 4 * ch + k, :]), q)
        return q

    for b in range(NI + 1):
        if b < NI:
            ld = []
            for hf in range(2):
                ld.append(li[hf].dma(sp, x[:, b % 2, 16 * hf:16 * hf + 16, :], x2[b, 32 * hf:32 * hf + 32].rearrange("(t r) c d -> (r c) t d", r=2), xfree[b % 2]))
            for ch in range(8):
                i = nx[0] % 2
                nx[0] += 1
                for k in range(4):
                    t = pe.sig(lambda e, i=i, k=k, ch=ch, b=b: e.transpose(psX[:, i, 128 * k:128 * k + 128], x[:, b % 2, 4 * ch + k, :], ident[:]), bx[i], ld[ch // 4], w)
                bx[i] = a = act.sig(lambda e, i=i, ch=ch, b=b: e.activation(xt[:, b % 2, 512 * ch:512 * ch + 512], psX[:, i, :], ACT.Copy), t, xtfree[b % 2])
                r = dve.sig(lambda e, ch=ch, b=b: e.tensor_reduce(rs[:, 0, 8 * ch:8 * ch + 8], xt[:, b % 2, 512 * ch:512 * ch + 512].rearrange("p (r c) -> p r c", c=64),
                                                                 AX.X, ALU.add), a)
            i = nx[0] % 2
            nx[0] += 1
            t = pe.sig(lambda e, i=i: e.matmul(psX[:, i, 0:64], wts[:, 2, :], rs[:, 0, :], start=True, stop=True), r, bx[i], w)
            rsok = bx[i] = dve.sig(lambda e, i=i: e.tensor_scalar(rs[:, 2, :], psX[:, i, 0:64], cols[:, 2:3], None, ALU.add), t, wk)
            prev = None
            for ch in range(8):
                nxt = chunk(b, ch, rsok, ld[ch // 4], a)
                if prev:
                    prev()
                prev = nxt
            q = prev()
            xtfree[b % 2] = llf[1]
            pend.append((b, q))
        if b >= 1 or b == NI:
            pass
        if b < NI:
            q = dve.sig(lambda e, b=b: e.tensor_scalar(rstd[:, 0, :], mv[:, b % 2, :, 1], 1.0e-5, None, ALU.add), q)
            q = act.sig(lambda e: e.activation(rstd[:, 1, :], rstd[:, 0, :], ACT.Sqrt), q)
            q = dve.sig(lambda e: e.reciprocal(rstd[:, 2, :], rstd[:, 1, :]), q)
            for ch in range(8):
                for k in range(4):
                    n = 4 * ch + k
                    z = dve.sig(lambda e, n=n, b=b: e.tensor_scalar(x[:, b % 2, n, :], x[:, b % 2, n, :], mv[:, b % 2, n, 0:1], rstd[:, 2, n:n + 1],
                                                                   ALU.subtract, ALU.mult), q)
                i = nx[0] % 2
                nx[0] += 1
                for k in range(4):
                    t = pe.sig(lambda e, i=i, k=k, ch=ch, b=b: e.transpose(psX[:, i, 128 * k:128 * k + 128], x[:, b % 2, 4 * ch + k, :], ident[:]), bx[i], z)
                s = ch % 2
                bx[i] = a = act.sig(lambda e, i=i, s=s: e.activation(o3[:, s, :], psX[:, i, :], ACT.Identity, bias=cols[:, 5:6], scale=cols[:, 4:5]), t, o3f[s])
                o3f[s] = lo[s].dma(sp, x3t[b, :, 512 * ch:512 * ch + 512], o3[:, s, :], a)
            xfree[b % 2] = t
    sp.wait(*o3f)
    P.run()


def directed(t, d):
    if d == 0:
        return t.rearrange("p (k l) -> p k l", k=8)
    if d == 1:
        return t[:, ::-1].rearrange("p (k l) -> p k l", k=8)
    v = t.rearrange("p (h w) -> p h w", w=HW)
    if d == 3:
        v = v[:, ::-1, ::-1]
    return v.rearrange("p h (k w) -> p k w h", k=8)


def part(t, d, c):
    v = directed(t, d)
    return v[:, c] if d >= 2 else v[:, c, :]


def layer3(nc, ctx, io, x3t, dbl, zs, yz):
    U = ctx.enter_context(nc.sbuf_tensor("l3_u", [128, 2 * NI, TOK], F32))
    with ExitStack() as inner:
        convolve(nc, Phase(nc, inner, "l3a"), io, x3t, dbl, zs, U)
    with ExitStack() as inner:
        scan(nc, Phase(nc, inner, "l3b"), io, dbl, zs, yz, U)


def convolve(nc, P, io, x3t, dbl, zs, U):
    pe, act, dve, pool, sp = P.pe, P.act, P.dve, P.pool, P.sp
    R = lambda t: t.bitcast(F32)
    win = P.sb("win", [128, 512])
    tmp = P.sb("tmp", [128, 9, 256])
    zst = tmp[:].rearrange("p a b -> p (a b)")[:, 0:2048].rearrange("p (s n) -> p s n", s=4)
    th, tl = P.sb("th", [128, 9, 256], F32R), P.sb("tl", [128, 9, 256], F32R)
    zh, zl = P.sb("zh", [128, 256], F32R), P.sb("zl", [128, 256], F32R)
    xh, xl = P.sb("xh", [128, 66, 66], F32R), P.sb("xl", [128, 66, 66], F32R)
    xr = P.sb("xr", [128, 2, 512])
    wx = P.sb("wx", [128, 2, 28])
    cb = P.sb("cb", [128, 2])
    mk = P.sb("mk", [28, 2])
    dh, dm = P.sb("dh", [28, 2, 512], F32R), P.sb("dm", [28, 2, 512])
    ps = P.ps("c", [128, 5, 512])
    psD = P.ps("d", [128, 2, 512])
    lw = P.load("w")
    for dst, src in ((win[:], io["L3_conv_Win"]), (tmp[:], io["taps"].rearrange("(a t) c -> a t c", a=1).broadcast_to([128, 9, 256])),
                     (wx[:], io["wx28"].rearrange("(h p) d -> p h d", p=128)), (cb[:], io["L3_conv_conv_b"].rearrange("(h p) -> p h", p=128)),
                     (mk[:], io["low"][0:28, 0:2])):
        w = lw.dma(sp, dst, src, slow=True)
    lx = [P.load("x0"), P.load("x1")]
    ld = [P.load("d0"), P.load("d1")]
    lz = [P.load("z") for _ in range(4)]
    dve.sig(lambda e: e.memset(R(xh[:]), 0.0))
    z = dve.sig(lambda e: e.memset(R(xl[:]), 0.0))
    a = dve.sig(lambda e: e.tensor_tensor(tmp[:], tmp[:], win[:, 0:256].rearrange("p (a c) -> p a c", a=1).broadcast_to([128, 9, 256]), ALU.mult), w)
    a = dve.sig(lambda e: e.tensor_copy(th[:], tmp[:]), a)
    dve.sig(lambda e: e.tensor_tensor(tl[:], tmp[:], R(th[:]), ALU.subtract), a)
    a = dve.sig(lambda e: e.tensor_copy(zh[:], win[:, 256:512]), w)
    wt = dve.sig(lambda e: e.tensor_tensor(zl[:], win[:, 256:512], R(zh[:]), ALU.subtract), a)
    free, df = [None] * 5, [None] * 2
    n = 0
    xrf, dsf = [None, None], [None, None]
    zf = [wt] * 4
    conv, pad = {}, {}
    nz = 0

    def load(b, ch):
        s = ch % 2
        t = lx[s].dma(sp, xr[:, s, :], x3t[b, :, 512 * ch:512 * ch + 512], xrf[s])
        r = slice(8 * ch + 1, 8 * ch + 9)
        v = xr[:, s, :].rearrange("p (r c) -> p r c", c=64)
        before = conv.get((b - 1, min(ch + 1, 7)))
        a = act.sig(lambda e: e.activation(xh[:, r, 1:65], v, ACT.Copy), t, z, before)
        xrf[s] = pad[b, ch] = dve.sig(lambda e: e.tensor_tensor(xl[:, r, 1:65], v, R(xh[:, r, 1:65]), ALU.subtract), a)

    for ch in range(8):
        load(0, ch)
    for b in range(NI):
        for ch in range(8):
            last = []
            for h in range(4):
                i = n % 5
                n += 1
                hs = slice(128 * (h % 2), 128 * (h % 2) + 128)
                pe.wait(pad[b, min(ch + 1, 7)], wt, free[i])
                o = ps[:, i, :].rearrange("p (r c) -> p r c", c=64)
                taps = range(9) if h < 2 else (4,)
                for t9 in taps:
                    dy, dx = divmod(t9, 3)
                    rr, cc = slice(8 * ch + dy, 8 * ch + dy + 8), slice(dx, dx + 64)
                    wh, wl = (th[:, t9, hs], tl[:, t9, hs]) if h < 2 else (zh[:, hs], zl[:, hs])
                    for k, (wv, xv) in enumerate(((wh, xh), (wl, xh), (wh, xl))):
                        first, end = t9 == taps[0] and k == 0, t9 == taps[-1] and k == 2
                        f = lambda e, o=o, wv=wv, xv=xv, rr=rr, cc=cc, first=first, end=end: e.matmul(o, wv, xv[:, rr, cc], start=first, stop=end)
                        if end:
                            conv[b, ch] = t = pe.sig(f)
                        else:
                            pe.do(f)
                if h < 2:
                    free[i] = act.sig(lambda e, i=i, b=b, h=h, ch=ch: e.activation(U[:, 2 * b + h, 512 * ch:512 * ch + 512], ps[:, i, :], ACT.Silu, bias=cb[:, h:h + 1]), t, w)
                    last.append(free[i])
                else:
                    q = nz % 4
                    nz += 1
                    free[i] = a = act.sig(lambda e, i=i, q=q: e.activation(zst[:, q, :], ps[:, i, :], ACT.Silu), t, zf[q])
                    zf[q] = lz[q].dma(sp, zs[b, h - 2, :, 512 * ch:512 * ch + 512], zst[:, q, :], a)
            j = ch % 2
            pe.do(lambda e, j=j, b=b, ch=ch: e.matmul(psD[0:28, j, :], wx[:, 0, :], U[:, 2 * b, 512 * ch:512 * ch + 512], start=True, stop=False), *last, df[j])
            t = pe.sig(lambda e, j=j, b=b, ch=ch: e.matmul(psD[0:28, j, :], wx[:, 1, :], U[:, 2 * b + 1, 512 * ch:512 * ch + 512], start=False, stop=True))
            d = dve.sig(lambda e, j=j: e.tensor_copy(dh[:, j, :], psD[0:28, j, :]), t)
            d = df[j] = dve.sig(lambda e, j=j: e.tensor_tensor(dm[:, j, :], psD[0:28, j, :], R(dh[:, j, :]), ALU.subtract), d, dsf[j])
            d = dve.sig(lambda e, j=j: e.tensor_scalar(dm[:, j, :], dm[:, j, :], mk[:, 0:1], None, ALU.mult), d, w)
            d = dve.sig(lambda e, j=j: e.scalar_tensor_tensor(dm[:, j, :], R(dh[:, j, :]), mk[:, 1:2], dm[:, j, :], ALU.mult, ALU.add), d)
            dsf[j] = ld[j].dma(sp, dbl[b, :, 512 * ch:512 * ch + 512], dm[:, j, :], d)
            if b + 1 < NI and ch >= 1:
                load(b + 1, ch - 1)
        if b + 1 < NI:
            load(b + 1, 7)
    sp.wait(*dsf, *zf)
    P.run()


def scan(nc, P, io, dbl, zs, yz, U):
    pe, act, dve, pool, sp = P.pe, P.act, P.dve, P.pool, P.sp
    R = lambda t: t.bitcast(F32)
    D = P.sb("D", [128, TOK], F32R)
    acc = P.sb("acc", [128, 2, TOK])
    dtw = P.sb("dtw", [128, 256], F32R)
    sel = P.sb("sel", [128, 2, 128], F32R)
    dg = P.sb("dg", [128, 8, 128])
    cc = P.sb("cc", [128, 32])
    tE, tL, tU, tZ = P.sb("E", [128, 4, 512]), P.sb("L", [128, 3, 512]), P.sb("du", [128, 3, 512]), P.sb("z", [128, 2, 512])
    psd = P.ps("d", [128, 2, 512])
    psB = P.ps("B", [128, 2, 512])
    psC = P.ps("C", [128, 2, 512])
    psX = P.ps("X", [128, 2, 512])
    cA, cD, cB, cm = cc[:, 0:8], cc[:, 8:16], cc[:, 16:24], cc[:, 28:30]

    lw = P.load("w")
    z0 = dve.sig(lambda e: e.memset(R(D[:]), 0.0))
    flat = lambda t: t.rearrange("p s n -> p (s n)")
    raw, selr, idn = flat(tE[:])[:, 0:256], flat(tE[:])[:, 256:512], flat(tE[:])[:, 768:896]
    loads = [(cA, io["L3_conv_A_log"].rearrange("(k p) a -> p (k a)", p=128)), (cD, io["L3_conv_D_param"].rearrange("(k p) -> p k", p=128)),
             (cB, io["L3_conv_dt_bias"].rearrange("(k p) -> p k", p=128)), (cm, io["low"][:, 2:4]),
             (raw, io["dtw"]), (selr, io["sel"].rearrange("p a b -> p (a b)")), (idn, io["ident"])]
    loads += [(R(D[32 * b:32 * b + 28, :]), dbl[b]) for b in range(NI)]
    for dst, src in loads:
        w = lw.dma(sp, dst, src, z0, slow=True)
    a = act.sig(lambda e: e.activation(cA, cA, ACT.Exp), w)
    wA = dve.sig(lambda e: e.tensor_scalar(cA, cA, -1.0, None, ALU.mult), a)
    t1, t2 = flat(tL[:])[:, 0:256], flat(tL[:])[:, 256:512]
    a = dve.sig(lambda e: e.tensor_copy(dtw[:], raw), w)
    a = dve.sig(lambda e: e.tensor_tensor(t1, raw, R(dtw[:]), ALU.subtract), a)
    a = dve.sig(lambda e: e.tensor_scalar(t1, t1, cm[:, 0:1], None, ALU.mult), a)
    a = dve.sig(lambda e: e.scalar_tensor_tensor(t2, R(dtw[:]), cm[:, 1:2], t1, ALU.mult, ALU.add), a)
    dve.sig(lambda e: e.tensor_copy(dtw[:], t2), a)
    dve.sig(lambda e: e.tensor_copy(sel[:].rearrange("p a b -> p (a b)"), selr))
    for k in range(8):
        w0 = dve.sig(lambda e, k=k: e.tensor_scalar(dg[:, k, :], idn, cD[:, k:k + 1], None, ALU.mult))
    act.do(lambda e: e.preload_act_table_set("natural_log_exp_and_others"))

    rE, rL, rU, rX, rZ = Ring(tE, 4, w0), Ring(tL, 3, w0), Ring(tU, 3), Ring(psX, 2), Ring(tZ, 2)
    df, bf, cf = [None] * 2, [None] * 2, [None] * 2
    lz = [P.load("z0"), P.load("z1")]
    lo = [P.load("o0"), P.load("o1")]
    ready, stored, gated = {}, {}, {}
    units = [(n, h, a4, c) for n in range(NI) for h in range(2) for a4 in range(4) for c in range(8)]
    S = [{} for _ in units]
    as2 = lambda t, d: t if d < 2 else t.rearrange("p (w h) -> p w h", h=64)
    added = {}

    def step_a(m):
        n, h, a4, c = units[m]
        s, i, k = S[m], m % 2, 2 * a4 + h
        rows = slice(32 * n, 32 * n + 28)
        t = pe.sig(lambda e: e.matmul(psd[:, i, :], dtw[rows, 128 * h:128 * h + 128], part(D[rows, :], a4, c), start=True, stop=True), w, w0, df[i])
        s["e"], E, f1 = rE.take()
        s["l"], L, f2 = rL.take()
        s["E"], s["L"] = E, L
        s["x"] = act.sig(lambda e: e.activation(E, psd[:, i, :], ACT.Abs, bias=cB[:, k:k + 1]), t, f1)
        df[i] = act.sig(lambda e: e.activation(L, psd[:, i, :], ACT.Relu, bias=cB[:, k:k + 1]), f2)

    def step_a2(m):
        s = S[m]
        E = s["E"]
        s["x"] = act.sig(lambda e: e.activation(E, E, ACT.Exp, scale=-1.0), s["x"])

    def step_b(m):
        s = S[m]
        E, L = s["E"], s["L"]
        a = act.sig(lambda e: e.activation(E, E, ACT.Ln, bias=1.0), s["x"])
        s["d"] = dve.sig(lambda e: e.tensor_tensor(L, L, E, ALU.add), a)

    def step_c(m):
        n, h, a4, c = units[m]
        s, k, j = S[m], 2 * a4 + h, m % 2
        E, L = s["E"], s["L"]
        s["a"] = act.sig(lambda e: e.activation(E, L, ACT.Exp, scale=cA[:, k:k + 1]), s["d"], wA)
        s["u"], G, f = rU.take()
        s["U"] = G
        u = part(U[:, 2 * a4 + h, :], n, c)
        s["p"] = pool.sig(lambda e: e.tensor_tensor(as2(G, n), as2(L, n), u, ALU.mult), s["d"], f)
        rL.free[s["l"]] = [s["p"], s["a"]]
        rows = slice(32 * a4, 32 * a4 + 28)
        s["tb"] = pe.sig(lambda e: e.matmul(psB[:, j, :], sel[rows, 0, :], part(D[rows, :], n, c), start=True, stop=True), bf[j])
        s["tc"] = pe.sig(lambda e: e.matmul(psC[:, j, :], sel[rows, 1, :], part(D[rows, :], n, c), start=True, stop=True), cf[j])

    def step_d(m):
        s, j = S[m], m % 2
        G = s["U"]
        s["b"] = bf[j] = dve.sig(lambda e: e.tensor_tensor(G, psB[:, j, :], G, ALU.mult), s["p"], s["tb"])

    def step_e(m):
        n, h, a4, c = units[m]
        s, j = S[m], m % 2
        E, G = s["E"], s["U"]
        init = 0.0 if c == 0 else S[m - 1]["U"][:, 511:512]
        q = dve.sig(lambda e: e.tensor_tensor_scan(G, E, G, init, ALU.mult, ALU.add), s["a"], s["b"], S[m - 1]["q"] if c else None)
        s["q"] = q
        if m:
            rU.free[S[m - 1]["u"]] = q

    def step_f(m):
        n, h, a4, c = units[m]
        s, j, z = S[m], m % 2, (2 * n + h) % 2
        E, G = s["E"], s["U"]
        y = cf[j] = dve.sig(lambda e: e.tensor_tensor(E, psC[:, j, :], G, ALU.mult), s["q"], s["tc"])
        o = part(acc[:, z, :], a4, c)
        need = ready[n, h, c] if a4 == 0 else None
        if m + 1 < len(units) and units[m + 1][3] == 0 or m + 1 == len(units):
            rU.free[s["u"]] = y
        rE.free[s["e"]] = added[n, h] = pool.sig(lambda e: e.tensor_tensor(o, o, as2(E, a4), ALU.add), y, need, added.get((n, h)))

    def start(n, h, c):
        z = (2 * n + h) % 2
        i, X, f = rX.take()
        for a4 in range(4):
            g = lambda e, a4=a4: e.matmul(X, dg[:, 2 * a4 + h, :], part(U[:, 2 * a4 + h, :], n ^ a4, c), start=(a4 == 0), stop=(a4 == 3))
            if a4 < 3:
                pe.do(g, f, w0)
            else:
                t = pe.sig(g)
        ready[n, h, c] = rX.free[i] = act.sig(lambda e: e.activation(acc[:, z, 512 * c:512 * c + 512], X, ACT.Copy), t, stored.get((2 * n + h - 2, c)))

    def fetch(n, h, c):
        i, V, f = rZ.take()
        gated[n, h, c] = (i, V, lz[i].dma(sp, V, zs[n, h, :, 512 * c:512 * c + 512], f))

    def gate(n, h, c):
        i, V, t = gated[n, h, c]
        v = acc[:, (2 * n + h) % 2, 512 * c:512 * c + 512]
        y = rZ.free[i] = dve.sig(lambda e: e.tensor_tensor(v, v, V, ALU.mult), t, added[n, h])
        stored[2 * n + h, c] = lo[c % 2].dma(sp, yz[n, h, :, 512 * c:512 * c + 512], v, y)

    sched = {}
    steps = ((3, 0, step_d), (1, 1, step_b), (2, 2, step_c), (3, 3, step_e), (0, 4, step_a), (0, 5, step_a2), (3, 6, step_f))
    for k in range(2 * NI + 1):
        n, h, t0 = k // 2, k % 2, 32 * k
        for c in range(8):
            if k < 2 * NI:
                sched.setdefault(t0 - 8 + c, []).append((-1, start, n, h, c))
            if k >= 1:
                sched.setdefault(t0 + 3 + 2 * c, []).append((20, fetch, (k - 1) // 2, (k - 1) % 2, c))
                sched.setdefault(t0 + 5 + 2 * c, []).append((21, gate, (k - 1) // 2, (k - 1) % 2, c))
    for m in range(len(units)):
        for lag, order, f in steps:
            sched.setdefault(m + lag, []).append((order, f, m))
    for at in sorted(sched):
        for _, f, *args in sorted(sched[at], key=lambda x: x[0]):
            f(*args)
    sp.wait(*((x.sem, x.n) for x in lo))
    P.run()


def finish3(nc, P, io, yz, out):
    pe, act, dve, pool, sp = P.pe, P.act, P.dve, P.pool, P.sp
    wo, gw, ob = P.sb("wo", [128, 2, 128]), P.sb("gw", [128, 2, 128]), P.sb("ob", [128, 2, 128])
    bw, mean, one = P.sb("bw", [128, 128]), P.sb("mean", [128, 128]), P.sb("one", [128, 128])
    cg = P.sb("cg", [128, 4])
    y = P.sb("y", [128, 3, 2, TOK])
    sq = P.sb("sq", [128, 3, 2, 512])
    rs = P.sb("rs", [128, 2, 3, 32])
    os = P.sb("os", [128, 3, 512])
    psM = P.ps("M", [128, 3, 512])
    psV = P.ps("V", [128, 2, 512])
    psO = P.ps("O", [128, 3, 512])
    lw = P.load("w")
    for dst, src in ((cg[:, 0:2], io["L3_conv_gamma"].rearrange("(h p) -> p h", p=128)), (cg[:, 2:4], io["L3_conv_beta"].rearrange("(h p) -> p h", p=128)),
                     (wo[:], io["L3_conv_Wout"].rearrange("(h p) d -> p h d", p=128))):
        w = lw.dma(sp, dst, src, slow=True)
    ly = [[P.load("y") for _ in range(4)] for _ in range(3)]
    lo = [P.load("o") for _ in range(3)]
    m = dve.sig(lambda e: e.memset(one[:], 1.0))
    wm = dve.sig(lambda e: e.memset(mean[:], 1.0 / 256))
    for h in range(2):
        dve.sig(lambda e, h=h: e.tensor_scalar(gw[:, h, :], wo[:, h, :], cg[:, h:h + 1], None, ALU.mult), w)
        g = dve.sig(lambda e, h=h: e.tensor_scalar(ob[:, h, :], one[:], cg[:, 2 + h:3 + h], None, ALU.mult), m)
    pe.do(lambda e: e.matmul(psV[:, 0, 0:128], ob[:, 0, :], wo[:, 0, :], start=True, stop=False), g, w)
    t = pe.sig(lambda e: e.matmul(psV[:, 0, 0:128], ob[:, 1, :], wo[:, 1, :], start=False, stop=True))
    g = dve.sig(lambda e: e.tensor_copy(bw[:], psV[:, 0, 0:128]), t)
    rM, rO, rQ = Ring(psM, 3), Ring(psO, 3), Ring(sq[:].rearrange("p s h n -> p s (h n)"), 3)
    vf, of = [g, None], [None] * 3
    loaded, mu, cen, doneb, rst, sqr = {}, {}, {}, {}, {}, {}

    def load(b):
        for q in range(4):
            s = slice(1024 * q, 1024 * q + 1024)
            loaded[b, q] = ly[b % 3][q].dma(sp, y[:, b % 3, :, s], yz[b, :, :, s].rearrange("h p n -> p h n"), doneb.get(b - 3))

    def stage1(b, c):
        sl = slice(512 * c, 512 * c + 512)
        i, X, f = rM.take()
        pe.do(lambda e: e.matmul(X, mean[:], y[:, b % 3, 0, sl], start=True, stop=False), loaded[b, c // 2], wm, f)
        mu[b, c] = (i, X, pe.sig(lambda e: e.matmul(X, mean[:], y[:, b % 3, 1, sl], start=False, stop=True)))

    def stage2(b, c):
        sl = slice(512 * c, 512 * c + 512)
        i, X, t = mu[b, c]
        v = y[:, b % 3, :, sl]
        d = rM.free[i] = cen[b, c] = dve.sig(lambda e: e.tensor_tensor(v, v, X.rearrange("p (a n) -> p a n", a=1).broadcast_to([128, 2, 512]), ALU.subtract), t)
        k, Q, f = rQ.take()
        a = act.sig(lambda e: e.activation(Q.rearrange("p (h n) -> p h n", h=2), v, ACT.Square), d, f)
        sqr[b, c] = (k, Q, a)

    def stage2b(b, c):
        k, Q, a = sqr[b, c]
        for j in range(4):
            for h in range(2):
                g = lambda e, j=j, h=h: e.matmul(psV[:, b % 2, 4 * c + j:4 * c + j + 1], Q[:, 512 * h + 128 * j:512 * h + 128 * j + 128], mean[:, 0:1], start=(h == 0), stop=(h == 1))
                if h:
                    t = pe.sig(g)
                else:
                    pe.do(g, a, vf[b % 2])
        rQ.free[k] = t
        if c == 7:
            r = rs[:, b % 2]
            v2 = vf[b % 2] = dve.sig(lambda e: e.tensor_scalar(r[:, 0, :], psV[:, b % 2, 0:32], 1.0e-5, None, ALU.add), t)
            v2 = act.sig(lambda e: e.activation(r[:, 1, :], r[:, 0, :], ACT.Sqrt), v2)
            rst[b] = dve.sig(lambda e: e.reciprocal(r[:, 2, :], r[:, 1, :]), v2)

    def stage3(b, c):
        r = rs[:, b % 2]
        i, X, f = rO.take()
        for j in range(4):
            tk = slice(512 * c + 128 * j, 512 * c + 128 * j + 128)
            for h in range(2):
                g = lambda e, j=j, h=h, tk=tk: e.matmul(X[:, 128 * j:128 * j + 128], y[:, b % 3, h, tk], gw[:, h, :], start=(h == 0), stop=(h == 1))
                if h:
                    t = pe.sig(g)
                else:
                    pe.do(g, f, cen[b, c])
        if c == 7:
            doneb[b] = t
        o = (8 * b + c) % 3
        for j in range(4):
            d = dve.sig(lambda e, j=j: e.scalar_tensor_tensor(os[:, o, 128 * j:128 * j + 128], X[:, 128 * j:128 * j + 128], r[:, 2, 4 * c + j:4 * c + j + 1], bw[:],
                                                             ALU.mult, ALU.add), t, rst[b], of[o])
        rO.free[i] = d
        of[o] = lo[o].dma(sp, out[b, 8 * c:8 * c + 8].rearrange("(t r) c d -> (r c) t d", r=2), os[:, o, :].rearrange("p (t c) -> p t c", t=4), d)

    load(0)
    load(1)
    load(2)
    for g in range(8 * NI + 11):
        if g < 8 * NI:
            stage1(g // 8, g % 8)
        if 1 <= g <= 8 * NI:
            stage2((g - 1) // 8, (g - 1) % 8)
        if 2 <= g < 8 * NI + 2:
            stage2b((g - 2) // 8, (g - 2) % 8)
        if g >= 11:
            stage3((g - 11) // 8, (g - 11) % 8)
            if (g - 11) % 8 == 7 and (g - 11) // 8 + 3 < NI:
                load((g - 11) // 8 + 3)
    sp.wait(*of)
    P.run()


USED = ["x", "xT", "xqT", "ident", "rpbx", "mask", "group", "taps", "dtw", "sel", "wx28", "low"]
USED += ["L0_conv_" + k for k in ("qkv_w", "qkv_b", "proj_w", "proj_b", "g1_w", "g1_b", "g2_w", "g2_b")]
USED += ["L1_conv_" + k for k in ("gn_scale", "gn_bias", "wq", "bq", "wk", "bk", "wv", "bv", "wo", "bo")]
USED += ["L2_conv_" + k for k in ("W_left", "b_left", "W_right", "b_right", "W_gate", "b_gate", "W_eq", "b_eq", "W_out", "b_out", "ln_scale", "ln_bias")]
USED += ["L3_conv_" + k for k in ("Win", "conv_b", "Wxproj", "A_log", "D_param", "dt_bias", "gamma", "beta", "Wout")]


def layout3(a):
    o = {}
    o["taps"] = np.ascontiguousarray(a["L3_conv_conv_w"].reshape(256, 9).T)
    o["wx28"] = np.ascontiguousarray(a["L3_conv_Wxproj"][:, list(range(8)) * 3 + [8, 8, 9, 9]])
    dtw = np.zeros((NI, 32, 256), np.float32)
    for k in range(3):
        dtw[:, 8 * k:8 * k + 8] = a["L3_conv_dt_weight"].transpose(0, 2, 1)
    o["dtw"] = dtw.reshape(128, 256)
    sel = np.zeros((NI, 32, 2, 128), np.float32)
    sel[:, 24:26, 0] = 1.0
    sel[:, 26:28, 1] = 1.0
    o["sel"] = sel.reshape(128, 2, 128)
    low = np.zeros((128, 4), np.float32)
    low[[*range(8, 16), 25, 27], 0] = 1.0
    low.reshape(NI, 32, 4)[:, 16:24, 2] = 1.0
    low[:, 1::2] = 1.0 - low[:, 0::2]
    o["low"] = low
    o["ident"] = np.eye(128, dtype=np.float32)
    return o


def layout(inputs):
    a = {k: np.asarray(v) for k, v in inputs.items()}
    a["xT"] = np.ascontiguousarray(a["x"].reshape(NI, TOK, C).transpose(0, 2, 1))
    a["xqT"] = np.ascontiguousarray(a["x"].reshape(NI, 8, 8, 4, 16, C).transpose(0, 5, 1, 3, 2, 4).reshape(NI, C, TOK))
    rpb = a["L0_conv_rpb"]
    q = np.arange(128)
    key = np.arange(308)
    rp, mask = [], []
    for dr in (0, 3, 6):
        for dc in (0, 3, 6):
            def axis(d, n, size):
                i = np.arange(n) + d
                start = {0: np.maximum(i - 3, 0), 3: i - 3, 6: np.minimum(i - 3, size - 7)}[d]
                return i, start
            ri, rs = axis(dr, 8, 14)
            ci, cs = axis(dc, 16, 22)
            qi, qs, pi, ps = ri[q // 16], rs[q // 16], ci[q % 16], cs[q % 16]
            kr, kc = key // 22, key % 22
            inside = ((kr >= qs[:, None]) & (kr < qs[:, None] + 7) & (kc >= ps[:, None]) & (kc < ps[:, None] + 7))
            br = np.clip(kr[None] - qi[:, None] + 6, 0, 12)
            bc = np.clip(kc[None] - pi[:, None] + 6, 0, 12)
            mask.append(np.where(inside, 0.0, -1.0e30).astype(np.float32))
            rp.append(rpb[:, br, bc])
    a["rpbx"] = np.ascontiguousarray(np.concatenate(rp))
    a["mask"] = np.stack(mask)
    a["group"] = (np.kron(np.eye(32), np.ones((4, 4))) / 4).astype(np.float32)
    a.update(layout3(a))
    a["ident"] = np.eye(128, dtype=np.float32)
    return a


def program(nc, io, out):
    global SEMS
    x1 = nc.dram_tensor("x1", [NI, HW, HW, C], F32).ap()
    x1t = nc.dram_tensor("x1t", [NI, C, TOK], F32).ap()
    x2 = nc.dram_tensor("x2", [NI, HW, HW, C], F32).ap()
    x3t = nc.dram_tensor("x3t", [NI, C, TOK], F32).ap()
    vs = nc.dram_tensor("vs", [NI, HW, HW, C], F32).ap()
    hls = nc.dram_tensor("hls", [8, 2, C, 512], F32).ap()
    dbl = nc.dram_tensor("dbl", [NI, 28, TOK], F32).ap()
    zs = nc.dram_tensor("zs", [NI, 2, C, TOK], F32).ap()
    yz = nc.dram_tensor("yz", [NI, 2, C, TOK], F32).ap()
    with ExitStack() as SEMS:
        with ExitStack() as ctx:
            layer0(nc, Phase(nc, ctx, "l0"), io, vs, hls, x1)
        with ExitStack() as ctx:
            layer1(nc, Phase(nc, ctx, "l1"), io, x1, x1t, x2)
        with ExitStack() as ctx:
            layer2(nc, Phase(nc, ctx, "l2"), io, x2, x3t)
        with ExitStack() as ctx:
            layer3(nc, ctx, io, x3t, dbl, zs, yz)
        with ExitStack() as ctx:
            finish3(nc, Phase(nc, ctx, "l3c"), io, yz, out)


def kernel(**inputs):
    import concourse.bacc as bacc
    from concourse.bass_utils import run_bass_kernel_spmd

    a = layout(inputs)
    nc = bacc.Bacc("TRN2", target_bir_lowering=False, num_devices=1)
    arrays, io = {}, {}
    for name in USED:
        v = np.ascontiguousarray(a[name])
        arrays[f"in_{name}"] = v
        io[name] = nc.dram_tensor(f"in_{name}", v.shape, mybir.dt.from_np(v.dtype), kind="ExternalInput").ap()
    out = nc.dram_tensor("out_0", (NI, HW, HW, C), F32, kind="ExternalOutput").ap()
    program(nc, io, out)
    r = run_bass_kernel_spmd(nc, [arrays], core_ids=[0])
    return r.results[0]["out_0"]
```

```python
from contextlib import ExitStack

import numpy as np
import concourse.bass as bass
from concourse import mybir

F32 = mybir.dt.float32
F32R = mybir.dt.float32r
ALU = mybir.AluOpType
ACT = mybir.ActivationFunctionType
AX = mybir.AxisListType

NI = 4
HW = 64
TOK = HW * HW
C = 128
SEMS = None


class Lane:

    def __init__(self, sem):
        self.sem, self.n, self.ops, self.seen = sem, 0, [], {}

    def wait(self, *tokens):
        for token in tokens:
            if token is None:
                continue
            if isinstance(token, list):
                self.wait(*token)
                continue
            sem, value = token
            if self.seen.get(id(sem), 0) < value:
                self.seen[id(sem)] = value
                self.ops.append(lambda e, s=sem, v=value: e.wait_ge(s, v))

    def do(self, f, *tokens):
        self.wait(*tokens)
        self.ops.append(f)

    def sig(self, f, *tokens):
        self.wait(*tokens)
        self.n += 1
        self.ops.append(lambda e: f(e).then_inc(self.sem, 1))
        return self.sem, self.n

    def play(self, e):
        for f in self.ops:
            f(e)


class Load:

    def __init__(self, sem):
        self.sem, self.n = sem, 0

    def dma(self, lane, dst, src, *tokens, slow=False):
        lane.wait(*tokens)
        self.n += 16
        lane.ops.append(lambda e: e.dma_start(dst, src, allow_slow_non_contiguous=slow).then_inc(self.sem, 16))
        return self.sem, self.n


class Phase:

    def __init__(self, nc, ctx, name):
        self.nc, self.ctx, self.name, self.k = nc, ctx, name, 0
        self.pe, self.act, self.dve, self.pool, self.sp = (Lane(self.sem(x)) for x in ("pe", "act", "dve", "pool", "sp"))

    def sem(self, what):
        self.k += 1
        return SEMS.enter_context(self.nc.semaphore(f"{self.name}_{what}_{self.k}"))

    def load(self, what):
        return Load(self.sem(what))

    def sb(self, name, shape, dt=F32):
        return self.ctx.enter_context(self.nc.sbuf_tensor(f"{self.name}_{name}", shape, dt))

    def ps(self, name, shape, dt=F32):
        return self.ctx.enter_context(self.nc.psum_tensor(f"{self.name}_{name}", shape, dt))

    def run(self):
        with self.nc.Block() as block:
            block.sync(lambda e: self.sp.play(e))
            block.tensor(lambda e: self.pe.play(e))
            block.scalar(lambda e: self.act.play(e))
            block.vector(lambda e: self.dve.play(e))
            block.gpsimd(lambda e: self.pool.play(e))


class Ring:

    def __init__(self, tile, n, first=None):
        self.tile, self.n, self.k, self.free = tile, n, 0, [first] * n

    def take(self):
        i = self.k % self.n
        self.k += 1
        return i, self.tile[:, i], self.free[i]


def layer0(nc, P, io, vs, hls, x1):
    pe, act, dve, pool, sp = P.pe, P.act, P.dve, P.pool, P.sp
    R = lambda t: t.bitcast(F32)
    S32 = 32.0 ** -0.5
    NB = NI * 8
    N = NB * 4

    ident = P.sb("ident", [128, 128])
    wqkv = P.sb("wqkv", [128, 384])
    wp = P.sb("wp", [128, 128])
    g1w = P.sb("g1w", [128, 64])
    g2w = P.sb("g2w", [64, 1])
    cols = P.sb("cols", [128, 8])
    bvb = P.sb("bvb", [128, 128])
    pbb = P.sb("pbb", [128, 128])
    bm = P.sb("bm", [128, 36, 308])
    ks = P.sb("ks", [96, 4, TOK], F32R)
    qs = P.sb("qs", [96, 3, 4, 512], F32R)
    hl = P.sb("hl", [128, 2, 2, 512], F32R)
    xn = P.sb("xn", [128, 2, 512])
    xq = P.sb("xq", [128, 2, 512])
    vst = P.sb("vst", [128, 2, 512])
    gt = P.sb("gt", [64, 512])
    gate = P.sb("gate", [128, 3, 4 * NB])
    pr = P.sb("pr", [128, 3, 4, 308])
    vg = P.sb("vg", [128, 5, 3, 128])
    st = P.sb("st", [128, 4, 16])
    ptb = P.sb("ptb", [128, 2, 4, 384])
    on = P.sb("on", [128, 2, 128])
    ot = P.sb("ot", [128, 2, 128])
    tm = P.sb("tm", [128, 128])
    xs = P.sb("xs", [128, 7, 128])
    ys = P.sb("ys", [128, 3, 128])

    psS = P.ps("S", [128, 3, 512])
    psT = P.ps("T", [128, 2, 512])
    psO = P.ps("O", [128, 512])
    psF = P.ps("F", [128, 512])
    psP = P.ps("P", [128, 512])

    lw = P.load("w")
    lb = [P.load("b") for _ in range(3)]
    biases = {}

    def bias(i):
        for k in range(3 * i, 3 * i + 3):
            biases[i] = lb[i].dma(sp, bm[:, 4 * k:4 * k + 4, :], io["rpbx"][4 * k:4 * k + 4].rearrange("k p n -> p k n"))

    for dst, src in ((wqkv[:], io["L0_conv_qkv_w"]), (ident[:], io["ident"]), (wp[:], io["L0_conv_proj_w"]),
                     (g1w[:], io["L0_conv_g1_w"]), (g2w[:], io["L0_conv_g2_w"]),
                     (cols[:, 0:3], io["L0_conv_qkv_b"].rearrange("(t p) -> p t", p=128)),
                     (cols[0:64, 3:4], io["L0_conv_g1_b"].rearrange("(p a) -> p a", a=1)),
                     (cols[:, 4:5], io["L0_conv_g2_b"].rearrange("(a p) -> a p", a=1).broadcast_to([128, 1])),
                     (bvb[:], io["L0_conv_qkv_b"].rearrange("(a p) -> a p", a=1)[:, 256:384].broadcast_to([128, 128])),
                     (pbb[:], io["L0_conv_proj_b"].rearrange("(a p) -> a p", a=1).broadcast_to([128, 128]))):
        w = lw.dma(sp, dst, src, slow=True)
    ln, lq = [P.load("xn") for _ in range(2)], [P.load("xq") for _ in range(2)]
    lh = [[P.load("h") for _ in range(2)] for _ in range(4)]
    lk, lqs, lv = [P.load("k") for _ in range(4)], [P.load("q") for _ in range(3)], [P.load("v") for _ in range(4)]
    lg, lt, lo = [P.load("g") for _ in range(5)], [P.load("t") for _ in range(7)], [P.load("o") for _ in range(3)]

    z1 = dve.sig(lambda e: e.memset(psT[:], 0.0))
    dve.sig(lambda e: e.tensor_scalar(cols[:, 0:1], cols[:, 0:1], S32, None, ALU.mult), w)
    dve.sig(lambda e: e.tensor_scalar(wqkv[:, 0:128], wqkv[:, 0:128], S32, None, ALU.mult), w)
    d0 = dve.sig(lambda e: e.tensor_scalar(cols[:, 4:5], cols[:, 4:5], -1.0, None, ALU.mult), w)

    xin, xnf, xqf = {}, [None] * 2, [None] * 2
    hif = [None, None]
    vstf = [None, None]
    scored, stack, vdone = {}, {}, {}
    qsf = [None] * 3
    pfree = [None]
    gtf = [None]
    gates, hidden = {}, {}

    def fetch(G):
        b, rb = divmod(G, 8)
        s = G % 2
        sl = slice(512 * rb, 512 * rb + 512)
        xin[G] = (ln[s].dma(sp, xn[:, s, :], io["xT"][b, :, sl], xnf[s]), lq[s].dma(sp, xq[:, s, :], io["xqT"][b, :, sl], xqf[s]))

    def split(G, which):
        b, rb = divmod(G, 8)
        s = G % 2
        X, t = (xq, xin[G][1]) if which == 0 else (xn, xin[G][0])
        t = pe.sig(lambda e: e.matmul(psP[:], wqkv[:, 128 * which:128 * which + 128], X[:, s, :], start=True, stop=True), t, d0, pfree[0])
        u = which
        a = act.sig(lambda e: e.activation(hl[:, u, 0, :], psP[:], ACT.Identity, bias=cols[:, which:which + 1]), t, hif[u])
        d = pfree[0] = dve.sig(lambda e: e.scalar_tensor_tensor(hl[:, u, 1, :], psP[:], cols[:, which:which + 1], R(hl[:, u, 0, :]), ALU.add, ALU.subtract), a)
        if which == 0:
            dst, ld, wait = qs[:, G % 3], lqs[G % 3], qsf[G % 3]
            order = (0, 1, 0)
        else:
            dst, ld, wait = ks[:, :, 512 * rb:512 * rb + 512], lk[G % 4], scored.get(min(G - 7, 8 * b - 1))
            order = (0, 0, 1)
        slot = hls[2 * (G % 4) + which]
        d2 = hif[u] = lh[G % 4][which].dma(sp, slot.rearrange("s c n -> c s n"), R(hl[:, u]), a, d)
        for k, j in enumerate(order):
            d3 = ld.dma(sp, R(dst[32 * k:32 * k + 32]), slot[j].rearrange("(h p) n -> p h n", h=4), d2, wait)
        stack[G, which] = d3

    def values(G):
        b, rb = divmod(G, 8)
        s = G % 2
        for k in range(4):
            t = pe.sig(lambda e, k=k: e.matmul(psP[:, 128 * k:128 * k + 128], xn[:, s, 128 * k:128 * k + 128], wqkv[:, 256:384], start=True, stop=True), xin[G][0], pfree[0], w)
        xnf[s] = t
        d = pfree[0] = dve.sig(lambda e: e.tensor_tensor(vst[:, s, :].rearrange("p (k c) -> p k c", k=4), psP[:].rearrange("p (k c) -> p k c", k=4),
                                                         bvb[:].rearrange("p (a c) -> p a c", a=1).broadcast_to([128, 4, 128]), ALU.add), t, w, vstf[s])
        vdone[G] = vstf[s] = lv[G % 4].dma(sp, vs[b, 8 * rb:8 * rb + 8].rearrange("(t r) c d -> (r c) t d", r=2), vst[:, s, :].rearrange("p (t c) -> p t c", t=4), d)

    def gating(G):
        s = G % 2
        t = pe.sig(lambda e: e.matmul(psP[0:64, :], g1w[:], xq[:, s, :], start=True, stop=True), xin[G][1], pfree[0], w)
        xqf[s] = t
        a = act.sig(lambda e: e.activation(gt[:], psP[0:64, :], ACT.Relu, bias=cols[0:64, 3:4]), t, gtf[0], d0)
        hidden[G] = pfree[0] = a

    def opening(G):
        a = hidden[G]
        for k in range(4):
            t = pe.sig(lambda e, k=k: e.matmul(psP[:, k:k + 1], gt[:, 128 * k:128 * k + 128], g2w[:], start=True, stop=True), a, pfree[0])
        gtf[0] = t
        sl = slice(4 * G, 4 * G + 4)
        a = pfree[0] = act.sig(lambda e: e.activation(gate[:, 0, sl], psP[:, 0:4], ACT.Exp, bias=cols[:, 4:5], scale=-1.0), t)
        a = dve.sig(lambda e: e.tensor_scalar(gate[:, 1, sl], gate[:, 0, sl], 1.0, None, ALU.add), a)
        gates[G] = dve.sig(lambda e: e.reciprocal(gate[:, 2, sl], gate[:, 1, sl]), a)

    for G in range(2):
        fetch(G)
    bias(0)
    for G in range(2):
        split(G, 0)
        split(G, 1)
        values(G)
        gating(G)
        opening(G)
        fetch(G + 2)
    kimg = ks[:].rearrange("p a (h w) -> p a h w", w=HW)
    rS, rT = Ring(psS, 3), Ring(psT, 2, z1)
    prf, ptf, vgf = [None] * 3, [[None] * 4 for _ in range(2)], [None] * 5
    sumd = {}
    onf, otf, xsf = [None] * 2, [None] * 2, [None] * 7
    ofree, ffree, tmf = [None], [None], [None]
    info = {}

    def where(n):
        G, i = divmod(n, 4)
        b, rb = divmod(G, 8)
        r0, c0 = 8 * rb, 16 * i
        return b, r0, c0, min(max(r0 - 3, 0), 50), min(max(c0 - 3, 0), 42)

    def bring(n):
        b, r0, c0, kr, kc = where(n)
        G = n // 4
        for j, (o, m) in enumerate(((0, 5), (5, 5), (10, 4))):
            info["v", n] = lg[n % 5].dma(sp, vg[0:22 * m, n % 5, j, :], vs[b, kr + o:kr + o + m, kc:kc + 22, :],
                                         *[vdone[x] for x in (G - 1, G, G + 1) if x // 8 == b and x in vdone], vgf[n % 5])
        info["x", n] = lt[n % 7].dma(pool, xs[:, n % 7, :], io["x"][b, r0:r0 + 8, c0:c0 + 16, :], xsf[n % 7])

    def score(n, h):
        b, r0, c0, kr, kc = where(n)
        G, i4 = divmod(n, 4)
        cls = 3 * {0: 0, 3: 1, 6: 2}[r0 - kr] + {0: 0, 3: 1, 6: 2}[c0 - kc]
        s = n % 3
        i, X, f = rS.take()
        need = [stack[x, 1] for x in (G - 1, G, G + 1) if x // 8 == b and (x, 1) in stack] + [stack[G, 0]]
        t = pe.sig(lambda e: e.matmul(X[:, 0:308], qs[:, G % 3, h, 128 * i4:128 * i4 + 128], kimg[:, h, kr:kr + 14, kc:kc + 22],
                                      start=True, stop=True), f, *need)
        if h == 3 and i4 == 3:
            scored[G] = qsf[G % 3] = t
        rS.free[i] = d = dve.sig(lambda e: e.tensor_tensor_reduce(pr[:, s, h, :], X[:, 0:308], bm[:, 4 * cls + h, :], 1.0, -3.0e38,
                                                                  ALU.add, ALU.max, st[:, n % 4, h:h + 1]), t, biases[cls // 3], prf[s], sumd.get(n - 4))
        if h == 3:
            info["m", n] = dve.sig(lambda e: e.tensor_scalar(st[:, n % 4, 4:8], st[:, n % 4, 0:4], -1.0, None, ALU.mult), d)

    def expo(n, h):
        s = n % 3
        info["e", n, h] = act.sig(lambda e: e.activation(pr[:, s, h, :], pr[:, s, h, :], ACT.Exp, bias=st[:, n % 4, 4 + h:5 + h],
                                                         accum_out=st[:, n % 4, 8 + h:9 + h]), info["m", n])

    def turn(n, h):
        i, X, f = rT.take()
        s = n % 3
        for j, (o, m) in enumerate(((0, 110), (110, 110), (220, 88))):
            t = pe.sig(lambda e, j=j, o=o, m=m: e.transpose(X[0:m, 128 * j:128 * j + 128], pr[:, s, h, o:o + m], ident[:]), f, info["e", n, h], w)
        if h == 3:
            prf[s] = t
        v = ptb[0:110, n % 2, h, :]
        if h % 2 == 0:
            rT.free[i] = act.sig(lambda e: e.activation(v, X[0:110, 0:384], ACT.Copy), t, ptf[n % 2][h])
        else:
            rT.free[i] = dve.sig(lambda e: e.tensor_copy(v, X[0:110, 0:384]), t, ptf[n % 2][h])
        info["p", n, h] = rT.free[i]

    def attend(n, h):
        for j, m in enumerate((110, 110, 88)):
            t = pe.sig(lambda e, j=j, m=m: e.matmul(psO[:, 32 * h:32 * h + 32], ptb[0:m, n % 2, h, 128 * j:128 * j + 128], vg[0:m, n % 5, j, 32 * h:32 * h + 32],
                                                    start=(j == 0), stop=(j == 2)), info["p", n, h], info["v", n], ofree[0])
        ptf[n % 2][h] = t
        if h == 3:
            vgf[n % 5] = t
            s = n % 4
            d = sumd[n] = dve.sig(lambda e: e.reciprocal(st[:, s, 12:16], st[:, s, 8:12]), info["e", n, 3])
            ofree[0] = info["n", n] = sumd[n] = dve.sig(lambda e: e.tensor_tensor(on[:, n % 2, :].rearrange("p (h d) -> p h d", h=4), psO[:, 0:128].rearrange("p (h d) -> p h d", h=4),
                                                                st[:, s, 12:16].rearrange("p (h a) -> p h a", a=1).broadcast_to([128, 4, 32]), ALU.mult), t, d, onf[n % 2])

    def flip(n):
        s = n % 2
        t = onf[s] = pe.sig(lambda e: e.transpose(psF[:, 0:128], on[:, s, :], ident[:]), info["n", n], ffree[0])
        ffree[0] = info["f", n] = act.sig(lambda e: e.activation(ot[:, s, :], psF[:, 0:128], ACT.Copy), t, otf[s])

    def finish(n):
        b, r0, c0, _, _ = where(n)
        s = n % 2
        t = otf[s] = pe.sig(lambda e: e.matmul(psF[:, 128:256], ot[:, s, :], wp[:], start=True, stop=True), info["f", n], ffree[0])
        ffree[0] = d = dve.sig(lambda e: e.tensor_tensor(tm[:], psF[:, 128:256], pbb[:], ALU.add), t, w, tmf[0])
        xsf[n % 7] = tmf[0] = d = dve.sig(lambda e: e.scalar_tensor_tensor(ys[:, n % 3, :], tm[:], gate[:, 2, n:n + 1], xs[:, n % 7, :], ALU.mult, ALU.add),
                                          d, info["x", n], gates[n // 4], info.get(("s", n - 3)))
        info["s", n] = lo[n % 3].dma(pool, x1[b, r0:r0 + 8, c0:c0 + 16, :], ys[:, n % 3, :], d)

    bring(0)
    for n in range(N + 6):
        G = n // 4 + 2
        if n == 2:
            bias(1)
        elif n == 12:
            bias(2)
        if n % 4 == 0:
            if 2 < G <= NB:
                opening(G - 1)
            if G < NB:
                split(G, 1)
        elif G < NB and n % 4 == 1:
            split(G, 0)
        elif G < NB and n % 4 == 2:
            values(G)
        elif G < NB:
            gating(G)
            if G + 2 < NB:
                fetch(G + 2)
        if 0 <= n - 4 < N:
            flip(n - 4)
        for h in range(4):
            if n < N:
                score(n, h)
            if 0 <= n - 1 < N:
                expo(n - 1, h)
            if 0 <= n - 2 < N:
                turn(n - 2, h)
            if 0 <= n - 3 < N:
                attend(n - 3, h)
            if h == 1 and 0 <= n - 5 < N:
                finish(n - 5)
        if n + 1 < N:
            bring(n + 1)
    pool.wait(*[info["s", N - 1 - i] for i in range(3)])
    P.run()


def layer1(nc, P, io, x1, x1t, x2):
    pe, act, dve, pool, sp = P.pe, P.act, P.dve, P.pool, P.sp
    SC = float(C) ** -0.5
    R = lambda t: t.bitcast(F32)

    ident = P.sb("ident", [128, 128])
    wraw = P.sb("wraw", [128, 4, 128])
    wh = P.sb("wh", [128, 3, 128], F32R)
    wl = P.sb("wl", [128, 3, 128], F32R)
    cols = P.sb("cols", [128, 8])
    bob = P.sb("bob", [128, 128])
    grp = P.sb("grp", [128, 128])
    zero = P.sb("zero", [128, 1])
    pr = P.sb("pr", [128, 5, TOK])
    qh, ql = P.sb("qh", [128, TOK], F32R), P.sb("ql", [128, TOK], F32R)
    kh, kl = P.sb("kh", [128, TOK], F32R), P.sb("kl", [128, TOK], F32R)
    vh, vl = P.sb("vh", [128, 32, 128], F32R), P.sb("vl", [128, 32, 128], F32R)
    ph, pl = P.sb("ph", [128, 2, 512], F32R), P.sb("pl", [128, 2, 512], F32R)
    xc = P.sb("xc", [128, 2, 512])
    nh, nl = P.sb("nh", [128, 2, 512], F32R), P.sb("nl", [128, 2, 512], F32R)
    st = P.sb("st", [128, 5, 20])
    bn = P.sb("bn", [128, 8, 6])
    gs = P.sb("gs", [128, 2, 16])
    ots = P.sb("ots", [128, 256])
    xs = P.sb("xs", [128, 2, 128])
    ys = P.sb("ys", [128, 2, 128])

    psS = P.ps("S", [128, 3, 512])
    psT = P.ps("T", [128, 2, 512])
    psO = P.ps("O", [128, 2, 512])
    psF = P.ps("F", [128, 512])

    def row(name):
        return io[name].rearrange("(a p) -> a p", a=1).broadcast_to([128, 128])

    def col(name):
        return io[name].rearrange("(p a) -> p a", a=1)

    lw = P.load("w")
    for dst, src in ((ident[:], io["ident"]), (grp[:], io["group"]), (wraw[:, 0, :], io["L1_conv_wq"]), (wraw[:, 1, :], io["L1_conv_wk"]),
                     (wraw[:, 2, :], io["L1_conv_wv"]), (wraw[:, 3, :], io["L1_conv_wo"]),
                     (cols[:, 0:1], col("L1_conv_bq")), (cols[:, 1:2], col("L1_conv_bk")), (cols[:, 2:3], col("L1_conv_gn_scale")),
                     (cols[:, 3:4], col("L1_conv_gn_bias")), (cols[:, 4:5], col("L1_conv_bv")), (bob[:], row("L1_conv_bo"))):
        w = lw.dma(sp, dst, src, slow=True)
    li = [P.load("i0"), P.load("i1")]
    lx = [P.load("x0"), P.load("x1")]
    lt = [P.load("t0"), P.load("t1")]
    lo = [P.load("o0"), P.load("o1")]

    dve.sig(lambda e: e.memset(zero[:], 0.0))
    a = dve.sig(lambda e: e.tensor_copy(wh[:], wraw[:, 0:3, :]), w)
    wt = dve.sig(lambda e: e.tensor_tensor(wl[:], wraw[:, 0:3, :], R(wh[:]), ALU.subtract), a)
    t = pe.sig(lambda e: e.matmul(psF[:, 0:128], cols[:, 4:5].broadcast_to([128, 128]), wraw[:, 3, :], start=True, stop=True), w)
    wb = dve.sig(lambda e: e.tensor_tensor(bob[:], bob[:], psF[:, 0:128], ALU.add), t)

    sfree, sn = [None] * 3, [0]
    tfree, pfree = [None] * 2, [None] * 2
    ofree, ffree = [None, None], None
    slot = [None] * 5
    xsfree, ysfree = [None, None], [None, None]
    otsfree = None
    info = {}

    def bank():
        i = sn[0] % 3
        sn[0] += 1
        return i

    def three(out, lh, ll, rh, rl, *waits):
        pe.do(lambda e: e.matmul(out, lh, rh, start=True, stop=False), *waits)
        pe.do(lambda e: e.matmul(out, ll, rh, start=False, stop=False))
        return pe.sig(lambda e: e.matmul(out, lh, rl, start=False, stop=True))

    xr = Ring(xc, 2)
    nfree, nn = [None] * 2, [0]
    ready = {}

    def fetch_raw(b, ch):
        i, x, f = xr.take()
        ready["raw"] = i, x, li[i].dma(sp, x.rearrange("p (t c) -> p t c", c=128), x1[b, 8 * ch:8 * ch + 8].rearrange("(t r) c d -> (r c) t d", r=2), f)

    def channels(b, ch):
        i0, raw, ld = ready.pop("raw")
        i = bank()
        for k in range(4):
            t = pe.sig(lambda e, k=k: e.transpose(psS[:, i, 128 * k:128 * k + 128], raw[:, 128 * k:128 * k + 128], ident[:]), ld, sfree[i], w)
        if i0 is None:
            slot[4] = t
        else:
            xr.free[i0] = t
        i1, x, f = xr.take()
        a = sfree[i] = act.sig(lambda e: e.activation(x, psS[:, i, :], ACT.Copy), t, f)
        d = ready["bn"] = dve.sig(lambda e: e.bn_stats(bn[:, ch, :], x), a)
        ready["t", b, ch] = lx[i1].dma(sp, x1t[b, :, 512 * ch:512 * ch + 512], x, a)
        xr.free[i1] = [d, ready["t", b, ch]]

    def moments(b, part_):
        g = gs[:, b % 2]
        if part_ == 0:
            ready["m"] = dve.sig(lambda e: e.bn_aggr(g[:, 0:2], bn[:].rearrange("p a b -> p (a b)")), ready["bn"], ready.get(("last", b - 2)))
        elif part_ == 1:
            i = bank()
            t = pe.sig(lambda e: e.matmul(psS[:, i, 0:2], grp[:], g[:, 0:2], start=True, stop=True), ready["m"], sfree[i])
            s = sfree[i] = dve.sig(lambda e: e.tensor_copy(g[:, 2:4], psS[:, i, 0:2]), t)
            s = dve.sig(lambda e: e.tensor_tensor(g[:, 4:5], g[:, 0:1], g[:, 2:3], ALU.subtract), s)
            ready["m"] = dve.sig(lambda e: e.tensor_tensor(g[:, 5:6], g[:, 4:5], g[:, 4:5], ALU.mult), s)
        else:
            i = bank()
            t = pe.sig(lambda e: e.matmul(psS[:, i, 0:1], grp[:], g[:, 5:6], start=True, stop=True), ready["m"], sfree[i])
            s = sfree[i] = dve.sig(lambda e: e.tensor_tensor(g[:, 6:7], psS[:, i, 0:1], g[:, 3:4], ALU.add), t)
            s = dve.sig(lambda e: e.tensor_scalar(g[:, 11:12], g[:, 6:7], 1.0e-6, None, ALU.add), s)
            s = act.sig(lambda e: e.activation(g[:, 12:13], g[:, 11:12], ACT.Sqrt), s)
            s = dve.sig(lambda e: e.reciprocal(g[:, 9:10], g[:, 12:13]), s)
            s = dve.sig(lambda e: e.tensor_tensor(g[:, 7:8], g[:, 9:10], cols[:, 2:3], ALU.mult), s, w)
            s = dve.sig(lambda e: e.tensor_tensor(g[:, 10:11], g[:, 2:3], g[:, 7:8], ALU.mult), s)
            ready["g", b] = dve.sig(lambda e: e.tensor_tensor(g[:, 8:9], cols[:, 3:4], g[:, 10:11], ALU.subtract), s)

    def fetch_norm(b, ch, kind):
        i, x, f = xr.take()
        ready["x", b, ch, kind] = i, x, li[i].dma(sp, x, x1t[b, :, 512 * ch:512 * ch + 512], ready["t", b, ch], f)

    def normal(b, ch, kind):
        i, x, ld = ready.pop(("x", b, ch, kind))
        g = gs[:, b % 2]
        z = nn[0] % 2
        nn[0] += 1
        a = act.sig(lambda e: e.activation(nh[:, z, :], x, ACT.Identity, bias=g[:, 8:9], scale=g[:, 7:8]), ld, ready["g", b], nfree[z])
        d = ready["last", b] = dve.sig(lambda e: e.tensor_scalar(x, x, g[:, 7:8], g[:, 8:9], ALU.mult, ALU.add), a)
        p = xr.free[i] = pool.sig(lambda e: e.tensor_tensor(nl[:, z, :], x, R(nh[:, z, :]), ALU.subtract), d)
        ready["n", b, ch, kind] = z, p

    def product(b, ch, kind):
        z, p = ready.pop(("n", b, ch, kind))
        sl = slice(512 * ch, 512 * ch + 512)
        if kind == 0:
            for k, (dh, dl) in enumerate(((kh, kl), (qh, ql))):
                k = 1 - k
                i = bank()
                t = three(psS[:, i, :], wh[:, k, :], wl[:, k, :], nh[:, z, :], nl[:, z, :], p, wt, sfree[i])
                u = act.sig(lambda e, i=i, dh=dh, k=k: e.activation(dh[:, sl], psS[:, i, :], ACT.Identity, bias=cols[:, k:k + 1]), t, ready.get(("qk", b - 1)), w)
                sfree[i] = dve.sig(lambda e, i=i, dh=dh, dl=dl, k=k: e.scalar_tensor_tensor(dl[:, sl], psS[:, i, :], cols[:, k:k + 1], R(dh[:, sl]),
                                                                                         ALU.add, ALU.subtract), u)
            ready["kq", b, ch] = sfree[i]
        else:
            i = bank()
            pe.wait(sfree[i], p)
            for k in range(4):
                tk = slice(128 * k, 128 * k + 128)
                t = three(psS[:, i, tk], nh[:, z, tk], nl[:, z, tk], wh[:, 2, :], wl[:, 2, :])
            v = psS[:, i, :].rearrange("p (t c) -> p t c", c=128)
            sl4 = slice(4 * ch, 4 * ch + 4)
            u = act.sig(lambda e: e.activation(vh[:, sl4, :], v, ACT.Copy), t, ready.get(("pv", b - 1, 2 * ch + 1)))
            sfree[i] = ready["v", b, ch] = dve.sig(lambda e: e.tensor_tensor(vl[:, sl4, :], v, R(vh[:, sl4, :]), ALU.subtract), u)
        nfree[z] = t

    pending = []

    def qk(b, u):
        q, kc = divmod(u, 8)
        s = (32 * b + q) % 5
        i = bank()
        qs, ks = slice(128 * q, 128 * q + 128), slice(512 * kc, 512 * kc + 512)
        t = ready["qk", b] = three(psS[:, i, :], qh[:, qs], ql[:, qs], kh[:, ks], kl[:, ks], ready["kq", b, kc], ready["kq", b, q // 4], sfree[i])
        d = sfree[i] = dve.sig(lambda e: e.tensor_tensor_reduce(pr[:, s, ks], psS[:, i, :], zero[:].broadcast_to([128, 512]), 1.0, -3.0e38,
                                                                ALU.add, ALU.max, st[:, s, kc:kc + 1]), t, slot[s])
        if kc == 7:
            d = dve.sig(lambda e: e.tensor_reduce(st[:, s, 8:9], st[:, s, 0:8], AX.X, ALU.max), d)
            d = dve.sig(lambda e: e.tensor_scalar(st[:, s, 9:10], st[:, s, 8:9], -SC, None, ALU.mult), d)
            for k in range(8):
                pending.append((32 * b + q, s, k, d, 256 * b + u - 24 + 1))

    def exps(step):
        if pending and pending[0][4] <= step:
            q, s, k, d, _ = pending.pop(0)
            es = slice(512 * k, 512 * k + 512)
            info["e", q, k] = act.sig(lambda e: e.activation(pr[:, s, es], pr[:, s, es], ACT.Exp, bias=st[:, s, 9:10], scale=SC,
                                                         accum_out=st[:, s, 10 + k:11 + k]), d)

    def turn(v):
        g, j = divmod(v, 16)
        i = v % 2
        for q in range(2):
            s = (2 * g + q) % 5
            for k in range(2):
                kt = 2 * j + k
                t = pe.sig(lambda e, k=k, q=q, s=s, kt=kt: e.transpose(psT[:, i, 256 * k + 128 * q:256 * k + 128 * q + 128], pr[:, s, 128 * kt:128 * kt + 128], ident[:]),
                           info["e", 2 * g + q, j // 2], tfree[i])
        if j == 15:
            slot[2 * g % 5] = slot[(2 * g + 1) % 5] = t
        a = act.sig(lambda e: e.activation(ph[:, i, :], psT[:, i, :], ACT.Copy), t, pfree[i])
        tfree[i] = info["p", v] = dve.sig(lambda e: e.tensor_tensor(pl[:, i, :], psT[:, i, :], R(ph[:, i, :]), ALU.subtract), a)

    def pv(b, v):
        g, j = divmod(v, 16)
        i, o = v % 2, g % 2
        out = psO[:, o, 0:256]
        for k in range(2):
            kt = 2 * j + k
            ks = slice(256 * k, 256 * k + 256)
            pe.do(lambda e, kt=kt, ks=ks, f=(j == 0 and k == 0): e.matmul(out, vh[:, kt, :], ph[:, i, ks], start=f, stop=False), info["p", 256 * b + v], ofree[o], ready["v", b, j // 2])
            pe.do(lambda e, kt=kt, ks=ks: e.matmul(out, vl[:, kt, :], ph[:, i, ks], start=False, stop=False))
            t = pe.sig(lambda e, kt=kt, ks=ks, f=(j == 15 and k == 1): e.matmul(out, vh[:, kt, :], pl[:, i, ks], start=False, stop=f))
        pfree[i] = t
        if v >= 240:
            ready["pv", b, j] = t
        if j == 15:
            for q in range(2):
                n = 2 * g + q
                info["x", n] = lt[q].dma(sp, xs[:, q, :], x1[b, 2 * n:2 * n + 2].rearrange("r c d -> (r c) d"), xsfree[q])
            info["o"] = (b, g, t)

    def out1():
        nonlocal otsfree
        b, g, t = info["o"]
        o = g % 2
        a = ofree[o] = act.sig(lambda e: e.activation(ots[:], psO[:, o, 0:256], ACT.Copy), t, otsfree)
        info["a"] = a

    def out2():
        nonlocal ffree, otsfree
        b, g, _ = info.pop("o")
        for q in range(2):
            n = 2 * g + q
            t = pe.sig(lambda e, q=q: e.matmul(psF[:, 128 * q:128 * q + 128], ots[:, 128 * q:128 * q + 128], wraw[:, 3, :], start=True, stop=True), info["a"], ffree)
        otsfree = t
        for q in range(2):
            n = 2 * g + q
            s = (32 * b + n) % 5
            r = dve.sig(lambda e, s=s: e.tensor_reduce(st[:, s, 18:19], st[:, s, 10:18], AX.X, ALU.add), info["e", 32 * b + n, 7])
            r = dve.sig(lambda e, s=s: e.reciprocal(st[:, s, 19:20], st[:, s, 18:19]), r)
            x = pool.sig(lambda e, q=q: e.tensor_tensor(xs[:, q, :], xs[:, q, :], bob[:], ALU.add), info["x", n], wb)
            d = xsfree[q] = ffree = dve.sig(lambda e, q=q, s=s: e.scalar_tensor_tensor(ys[:, q, :], psF[:, 128 * q:128 * q + 128], st[:, s, 19:20], xs[:, q, :],
                                                                           ALU.mult, ALU.add), t, r, x, ysfree[q])
            ysfree[q] = lo[q].dma(sp, x2[b, 2 * n:2 * n + 2].rearrange("r c d -> (r c) d"), ys[:, q, :], d)

    at = {}

    def plan(step, f, *args):
        at.setdefault(step, []).append((f, args))

    first = pr[:, 4, :]
    halves = []
    for hf in range(2):
        halves.append(li[hf].dma(sp, first[:, 2048 * hf:2048 * hf + 2048].rearrange("p (t c) -> p t c", c=128), x1[0, 32 * hf:32 * hf + 32].rearrange("(t r) c d -> (r c) t d", r=2)))
    for hf, ld in enumerate(halves):
        for ch in range(4 * hf, 4 * hf + 4):
            ready["raw"] = None, first[:, 512 * ch:512 * ch + 512], ld
            channels(0, ch)
    for k in range(3):
        moments(0, k)
    for b in range(NI):
        base = 256 * b
        if b + 1 < NI:
            for ch in range(8):
                plan(base + 12 + 22 * ch, fetch_raw, b + 1, ch)
                plan(base + 18 + 22 * ch, channels, b + 1, ch)
            for k in range(3):
                plan(base + 190 + 2 * k, moments, b + 1, k)
        for kind, first, every in ((0, -26, 1), (1, -14, 2)):
            for ch in range(8):
                t = base + first + every * ch
                plan(t, product, b, ch, kind)
                plan(t - 2, normal, b, ch, kind)
                plan(t - 4, fetch_norm, b, ch, kind)
    for jobs in at.values():
        jobs.sort(key=lambda j: (product, normal, channels, moments, fetch_norm, fetch_raw).index(j[0]))
    for step in range(-30, 256 * NI + 4):
        for f, args in at.get(step, ()):
            f(*args)
        if 0 <= step + 24 < 256 * NI:
            qk(*divmod(step + 24, 256))
        if 0 <= step + 1 < 256 * NI:
            turn(step + 1)
        exps(step)
        if 0 <= step < 256 * NI:
            pv(*divmod(step, 256))
        if "o" in info and step % 16 == 1:
            out1()
        elif "o" in info and step % 16 == 3:
            out2()
    sp.wait(*ysfree)
    P.run()


def layer2(nc, P, io, x2, x3t):
    pe, act, dve, pool, sp = P.pe, P.act, P.dve, P.pool, P.sp
    ident = P.sb("ident", [128, 128])
    wts = P.sb("wts", [128, 5, 128])
    cols = P.sb("cols", [128, 8])
    bob = P.sb("bob", [128, 128])
    x = P.sb("x", [128, 3, 32, 128])
    xt = P.sb("xt", [128, 3, 512])
    rs = P.sb("rs", [128, 2, 3, 8])
    ee = P.sb("ee", [128, 2, 512])
    ll = P.sb("ll", [128, 2, 512])
    bn = P.sb("bn", [128, 32, 6])
    mv = P.sb("mv", [128, 2, 32, 2])
    rstd = P.sb("rstd", [128, 2, 3, 32])
    o3 = P.sb("o3", [128, 2, 512])
    psA = P.ps("A", [128, 2, 512])
    psG = P.ps("G", [128, 1, 512])
    psR = P.ps("R", [128, 8])
    psO = P.ps("O", [128, 2, 512])
    psX = P.ps("X", [128, 2, 512])

    def col(name):
        return io[name].rearrange("(p a) -> p a", a=1)

    lw = P.load("w")
    for dst, src in ((ident[:], io["ident"]), (wts[:, 0, :], io["L2_conv_W_left"]), (wts[:, 1, :], io["L2_conv_W_eq"]),
                     (wts[:, 2, :], io["L2_conv_W_right"]), (wts[:, 3, :], io["L2_conv_W_gate"]), (wts[:, 4, :], io["L2_conv_W_out"]),
                     (cols[:, 0:1], col("L2_conv_b_left")), (cols[:, 1:2], col("L2_conv_b_eq")), (cols[:, 2:3], col("L2_conv_b_right")),
                     (cols[:, 3:4], col("L2_conv_b_gate")), (cols[:, 4:5], col("L2_conv_ln_scale")), (cols[:, 5:6], col("L2_conv_ln_bias")),
                     (bob[:], io["L2_conv_b_out"].rearrange("(a p) -> a p", a=1).broadcast_to([128, 128]))):
        w = lw.dma(sp, dst, src, slow=True)
    li = [[P.load("i") for _ in range(2)] for _ in range(3)]
    lo = [P.load("o0"), P.load("o1")]
    dve.sig(lambda e: e.tensor_tensor(wts[:, 0, :], wts[:, 0, :], wts[:, 1, :], ALU.add), w)
    dve.sig(lambda e: e.tensor_tensor(cols[:, 0:1], cols[:, 0:1], cols[:, 1:2], ALU.add), w)
    wk = dve.sig(lambda e: e.tensor_scalar(cols[:, 2:3], cols[:, 2:3], 64.0, None, ALU.mult), w)

    bx, nx = [None] * 2, [0]
    bo, no = [None] * 2, [0]
    ba, bg = [None] * 2, [None] * 2
    eef, llf, o3f = [None] * 2, [None] * 2, [None] * 2
    xfree, xtf = [None] * 3, [None] * 3

    def chunk(g):
        b, ch = divmod(g, 8)
        s = ch % 2
        X = xt[:, g % 3, :]
        xtok, rsok = got[g]
        xok = ld[b, ch // 4]
        t1 = pe.sig(lambda e: e.matmul(psG[:, 0, :], wts[:, 3, :], X, start=True, stop=True), xtok, bg[0])
        t2 = pe.sig(lambda e: e.matmul(psA[:, s, :], wts[:, 0, :], X, start=True, stop=True), ba[s], wk)
        xtf[g % 3] = t2
        a = bg[0] = act.sig(lambda e: e.activation(ee[:, s, :], psG[:, 0, :], ACT.Sigmoid, bias=cols[:, 3:4]), t1, wk, eef[s])
        d2 = ba[s] = dve.sig(lambda e: e.scalar_tensor_tensor(ll[:, s, :].rearrange("p (r c) -> p r c", c=64), psA[:, s, :].rearrange("p (r c) -> p r c", c=64),
                                                             cols[:, 0:1], rs[:, 1, g % 3, :].rearrange("p (r a) -> p r a", a=1).broadcast_to([128, 8, 64]),
                                                             ALU.add, ALU.mult), t2, rsok, llf[s])
        d2 = eef[s] = dve.sig(lambda e: e.tensor_tensor(ll[:, s, :], ll[:, s, :], ee[:, s, :], ALU.mult), d2, a)
        v = x[:, b % 3, 4 * ch:4 * ch + 4, :]
        xb = pool.sig(lambda e: e.tensor_tensor(v, v, bob[:].rearrange("p (a c) -> p a c", a=1).broadcast_to([128, 4, 128]), ALU.add), xok, xtok, w)
        return lambda: tail(b, ch, s, d2, xb)

    def tail(b, ch, s, d2, xb):
        i = ch % 2
        v = x[:, b % 3, 4 * ch:4 * ch + 4, :]
        for k in range(4):
            t = pe.sig(lambda e, k=k: e.matmul(psO[:, i, 128 * k:128 * k + 128], ll[:, s, 128 * k:128 * k + 128], wts[:, 4, :], start=True, stop=True), d2, bo[i], w)
        llf[s] = t
        y = bo[i] = dve.sig(lambda e: e.tensor_tensor(v, psO[:, i, :].rearrange("p (k c) -> p k c", k=4), v, ALU.add), t, xb)
        for k in range(4):
            q = dve.sig(lambda e, k=k: e.bn_stats(bn[:, 4 * ch + k, :], v[:, k, :]), y)
        for k in range(4):
            q = dve.sig(lambda e, k=k: e.bn_aggr(mv[:, b % 2, 4 * ch + k, :], bn[:, 4 * ch + k, :]), q)
        return q

    def front(g):
        b, ch = divmod(g, 8)
        i = nx[0] % 2
        nx[0] += 1
        for k in range(4):
            t = pe.sig(lambda e, k=k: e.transpose(psX[:, i, 128 * k:128 * k + 128], x[:, b % 3, 4 * ch + k, :], ident[:]), bx[i], ld[b, ch // 4], w)
        a = act.sig(lambda e: e.activation(xt[:, g % 3, :], psX[:, i, :], ACT.Copy), t, xtf[g % 3])
        r = dve.sig(lambda e: e.tensor_reduce(rs[:, 0, g % 3, :], xt[:, g % 3, :].rearrange("p (r c) -> p r c", c=64), AX.X, ALU.add), a)
        bx[i] = a
        got[g] = a, r

    def sums(g):
        a, r = got[g]
        t = pe.sig(lambda e: e.matmul(psR[:], wts[:, 2, :], rs[:, 0, g % 3, :], start=True, stop=True), r, bg[1], w)
        bg[1] = dve.sig(lambda e: e.tensor_scalar(rs[:, 1, g % 3, :], psR[:], cols[:, 2:3], None, ALU.add), t, wk)
        got[g] = a, bg[1]

    def roots(b, q):
        q = dve.sig(lambda e: e.tensor_scalar(rstd[:, b % 2, 0, :], mv[:, b % 2, :, 1], 1.0e-5, None, ALU.add), q)
        q = act.sig(lambda e: e.activation(rstd[:, b % 2, 1, :], rstd[:, b % 2, 0, :], ACT.Sqrt), q)
        done[b] = dve.sig(lambda e: e.reciprocal(rstd[:, b % 2, 2, :], rstd[:, b % 2, 1, :]), q)

    def norm(g):
        b, ch = divmod(g, 8)
        for k in range(4):
            n = 4 * ch + k
            z = dve.sig(lambda e, n=n: e.tensor_scalar(x[:, b % 3, n, :], x[:, b % 3, n, :], mv[:, b % 2, n, 0:1], rstd[:, b % 2, 2, n:n + 1],
                                                       ALU.subtract, ALU.mult), done[b])
        normed[g] = z

    def turn(g):
        b, ch = divmod(g, 8)
        i = nx[0] % 2
        nx[0] += 1
        for k in range(4):
            t = pe.sig(lambda e, k=k: e.transpose(psX[:, i, 128 * k:128 * k + 128], x[:, b % 3, 4 * ch + k, :], ident[:]), bx[i], normed[g])
        s = ch % 2
        bx[i] = a = act.sig(lambda e: e.activation(o3[:, s, :], psX[:, i, :], ACT.Identity, bias=cols[:, 5:6], scale=cols[:, 4:5]), t, o3f[s])
        o3f[s] = lo[s].dma(sp, x3t[b, :, 512 * ch:512 * ch + 512], o3[:, s, :], a)
        if ch == 7:
            xfree[b % 3] = t

    def fetch(b):
        for hf in range(2):
            ld[b, hf] = li[b % 3][hf].dma(sp, x[:, b % 3, 16 * hf:16 * hf + 16, :], x2[b, 32 * hf:32 * hf + 32].rearrange("(t r) c d -> (r c) t d", r=2), xfree[b % 3])

    ld, got, done, normed, tails = {}, {}, {}, {}, {}
    fetch(0)
    fetch(1)
    fetch(2)
    for g in range(8 * NI + 14):
        if 0 <= g - 1 < 8 * NI:
            sums(g - 1)
        if g < 8 * NI:
            front(g)
        if 0 <= g - 3 < 8 * NI:
            q = tails.pop(g - 3)()
            if (g - 3) % 8 == 7:
                roots((g - 3) // 8, q)
        if 0 <= g - 2 < 8 * NI:
            tails[g - 2] = chunk(g - 2)
        if 0 <= g - 12 < 8 * NI:
            turn(g - 12)
            if (g - 12) % 8 == 7 and (g - 12) // 8 + 3 < NI:
                fetch((g - 12) // 8 + 3)
        if 0 <= g - 11 < 8 * NI:
            norm(g - 11)
    sp.wait(*o3f)
    P.run()


def directed(t, d):
    if d == 0:
        return t.rearrange("p (k l) -> p k l", k=8)
    if d == 1:
        return t[:, ::-1].rearrange("p (k l) -> p k l", k=8)
    v = t.rearrange("p (h w) -> p h w", w=HW)
    if d == 3:
        v = v[:, ::-1, ::-1]
    return v.rearrange("p h (k w) -> p k w h", k=8)


def part(t, d, c):
    v = directed(t, d)
    return v[:, c] if d >= 2 else v[:, c, :]


def layer3(nc, ctx, io, x3t, dbl, zs, yz):
    U = ctx.enter_context(nc.sbuf_tensor("l3_u", [128, 2 * NI, TOK], F32))
    with ExitStack() as inner:
        convolve(nc, Phase(nc, inner, "l3a"), io, x3t, dbl, zs, U)
    with ExitStack() as inner:
        scan(nc, Phase(nc, inner, "l3b"), io, dbl, zs, yz, U)


def convolve(nc, P, io, x3t, dbl, zs, U):
    pe, act, dve, pool, sp = P.pe, P.act, P.dve, P.pool, P.sp
    R = lambda t: t.bitcast(F32)
    win = P.sb("win", [128, 512])
    tmp = P.sb("tmp", [128, 6, 256])
    zst = tmp[:].rearrange("p a b -> p (a b)").rearrange("p (s n) -> p s n", s=3)
    th, tl = P.sb("th", [128, 6, 256], F32R), P.sb("tl", [128, 6, 256], F32R)
    wh, wl = P.sb("wh", [128, 512], F32R), P.sb("wl", [128, 512], F32R)
    xb = P.sb("xb", [128, 4, 8, 66])
    ct = P.sb("ct", [128, 2, 3])
    xh, xl = P.sb("xh", [128, 66, 66], F32R), P.sb("xl", [128, 66, 66], F32R)
    xr = P.sb("xr", [128, 2, 512])
    wx = P.sb("wx", [128, 2, 28])
    cb = P.sb("cb", [128, 2])
    mk = P.sb("mk", [28, 2])
    dh, dm = P.sb("dh", [28, 2, 512], F32R), P.sb("dm", [28, 2, 512])
    ps = P.ps("c", [128, 5, 512])
    psD = P.ps("d", [128, 2, 512])
    lw = P.load("w")
    for dst, src in ((win[:], io["L3_conv_Win"]), (tmp[:, 0:3, :], io["taps"][0:3].rearrange("(a t) c -> a t c", a=1).broadcast_to([128, 3, 256])),
                     (tmp[:, 3:6, :], io["taps"][6:9].rearrange("(a t) c -> a t c", a=1).broadcast_to([128, 3, 256])),
                     (ct[:, 0, :], io["taps"][3:6, 0:128].rearrange("t p -> p t")), (ct[:, 1, :], io["taps"][3:6, 128:256].rearrange("t p -> p t")),
                     (wx[:], io["wx28"].rearrange("(h p) d -> p h d", p=128)), (cb[:], io["L3_conv_conv_b"].rearrange("(h p) -> p h", p=128)),
                     (mk[:], io["low"][0:28, 0:2])):
        w = lw.dma(sp, dst, src, slow=True)
    lx = [P.load("x0"), P.load("x1")]
    ld = [P.load("d0"), P.load("d1")]
    lz = [P.load("z") for _ in range(3)]
    zb = pool.sig(lambda e: e.memset(xb[:], 0.0))
    dve.sig(lambda e: e.memset(R(xh[:]), 0.0))
    z = dve.sig(lambda e: e.memset(R(xl[:]), 0.0))
    a = dve.sig(lambda e: e.tensor_tensor(tmp[:], tmp[:], win[:, 0:256].rearrange("p (a c) -> p a c", a=1).broadcast_to([128, 6, 256]), ALU.mult), w)
    a = dve.sig(lambda e: e.tensor_copy(th[:], tmp[:]), a)
    dve.sig(lambda e: e.tensor_tensor(tl[:], tmp[:], R(th[:]), ALU.subtract), a)
    a = dve.sig(lambda e: e.tensor_copy(wh[:], win[:]), w)
    wt = dve.sig(lambda e: e.tensor_tensor(wl[:], win[:], R(wh[:]), ALU.subtract), a)
    rP = Ring(ps, 5)
    rZ, rX = Ring(zst, 3, wt), Ring(xb, 4, zb)
    df, xrf, dsf = [None, None], [None, None], [None, None]
    conv, pad, mid, row = {}, {}, {}, {}
    stores = [None] * 3

    def load(b, ch):
        s = ch % 2
        t = lx[s].dma(sp, xr[:, s, :], x3t[b, :, 512 * ch:512 * ch + 512], xrf[s])
        r = slice(8 * ch + 1, 8 * ch + 9)
        v = xr[:, s, :].rearrange("p (r c) -> p r c", c=64)
        before = conv.get((b - 1, min(ch + 1, 7)))
        a = act.sig(lambda e: e.activation(xh[:, r, 1:65], v, ACT.Copy), t, z, before)
        xrf[s] = pad[b, ch] = dve.sig(lambda e: e.tensor_tensor(xl[:, r, 1:65], v, R(xh[:, r, 1:65]), ALU.subtract), a)

    def products(o, pairs):
        n = len(pairs)
        for j, (weights, pixels) in enumerate(pairs):
            f = lambda e, j=j, weights=weights, pixels=pixels: e.matmul(o, weights, pixels, start=(j == 0), stop=(j == n - 1))
            if j == n - 1:
                return pe.sig(f)
            pe.do(f)

    def centre(b, ch):
        pe.wait(pad[b, min(ch + 1, 7)], wt)
        rr = slice(8 * ch + 1, 8 * ch + 9)
        for h in range(4):
            i, X, f = rP.take()
            pe.wait(f)
            hs = slice(128 * h, 128 * h + 128)
            t = products(X, [(wh[:, hs], xh[:, rr, 1:65]), (wl[:, hs], xh[:, rr, 1:65]), (wh[:, hs], xl[:, rr, 1:65])])
            if h < 2:
                q, V, f = rX.take()
                a = rP.free[i] = act.sig(lambda e, X=X, V=V: e.activation(V[:, :, 1:65], X.rearrange("p (r c) -> p r c", c=64), ACT.Copy), t, f)
                mid[h] = q, V, a
            else:
                q, V, f = rZ.take()
                a = rP.free[i] = act.sig(lambda e, X=X, V=V: e.activation(V, X, ACT.Silu), t, f)
                rZ.free[q] = stores[q] = lz[q].dma(sp, zs[b, h - 2, :, 512 * ch:512 * ch + 512], V, a)

    def outer(b, ch, h):
        i, X, f = rP.take()
        pe.wait(f)
        hs = slice(128 * h, 128 * h + 128)
        pairs = []
        for j in range(6):
            rr, cc = slice(8 * ch + 2 * (j // 3), 8 * ch + 2 * (j // 3) + 8), slice(j % 3, j % 3 + 64)
            pairs += [(th[:, j, hs], xh[:, rr, cc]), (tl[:, j, hs], xh[:, rr, cc]), (th[:, j, hs], xl[:, rr, cc])]
        t = conv[b, ch] = products(X, pairs)
        q, V, a = mid[h]
        u = U[:, 2 * b + h, 512 * ch:512 * ch + 512].rearrange("p (r c) -> p r c", c=64)
        for j in range(3):
            y = X.rearrange("p (r c) -> p r c", c=64) if j == 0 else u
            t = dve.sig(lambda e, j=j, y=y: e.scalar_tensor_tensor(u, V[:, :, j:j + 64], ct[:, h, j:j + 1], y, ALU.mult, ALU.add), t, a, w)
            if j == 0:
                rP.free[i] = t
        rX.free[q] = t
        row[b, ch, h] = t

    def finish(b, ch):
        sl, j = slice(512 * ch, 512 * ch + 512), ch % 2
        a = [act.sig(lambda e, h=h: e.activation(U[:, 2 * b + h, sl], U[:, 2 * b + h, sl], ACT.Silu, bias=cb[:, h:h + 1]), row[b, ch, h], w) for h in range(2)]
        pe.wait(a, df[j])
        t = products(psD[0:28, j, :], [(wx[:, h, :], U[:, 2 * b + h, sl]) for h in range(2)])
        d = dve.sig(lambda e: e.tensor_copy(dh[:, j, :], psD[0:28, j, :]), t)
        d = df[j] = dve.sig(lambda e: e.tensor_tensor(dm[:, j, :], psD[0:28, j, :], R(dh[:, j, :]), ALU.subtract), d, dsf[j])
        d = dve.sig(lambda e: e.tensor_scalar(dm[:, j, :], dm[:, j, :], mk[:, 0:1], None, ALU.mult), d, w)
        d = dve.sig(lambda e: e.scalar_tensor_tensor(dm[:, j, :], R(dh[:, j, :]), mk[:, 1:2], dm[:, j, :], ALU.mult, ALU.add), d)
        dsf[j] = ld[j].dma(sp, dbl[b, :, sl], dm[:, j, :], d)

    for ch in range(8):
        load(0, ch)
    for g in range(8 * NI + 1):
        b, ch = divmod(g, 8)
        if b < NI:
            centre(b, ch)
            outer(b, ch, 0)
        if g:
            finish(*divmod(g - 1, 8))
        if b < NI:
            outer(b, ch, 1)
            if b + 1 < NI and ch >= 1:
                load(b + 1, ch - 1)
        if ch == 7 and b + 1 < NI:
            load(b + 1, 7)
    sp.wait(*dsf, *stores)
    P.run()


def scan(nc, P, io, dbl, zs, yz, U):
    pe, act, dve, pool, sp = P.pe, P.act, P.dve, P.pool, P.sp
    R = lambda t: t.bitcast(F32)
    D = P.sb("D", [128, TOK], F32R)
    acc = P.sb("acc", [128, 2, TOK])
    dtw = P.sb("dtw", [128, NI * 256], F32R)
    sel = P.sb("sel", [128, 2, 128], F32R)
    dg = P.sb("dg", [128, 8, 128])
    cc = P.sb("cc", [128, 32])
    tE, tL, tU, tZ = P.sb("E", [128, 3, 512]), P.sb("L", [128, 3, 512]), P.sb("du", [128, 3, 512]), P.sb("z", [128, 2, 512])
    psd = P.ps("d", [128, 3, 512])
    psB = P.ps("B", [128, 2, 512])
    psC = P.ps("C", [128, 2, 512])
    psX = P.ps("X", [128, 1, 512])
    cA, cD, cm = cc[:, 0:8], cc[:, 8:16], cc[:, 16:18]

    lw = P.load("w")
    ld = P.load("D")
    z0 = dve.sig(lambda e: e.memset(R(D[:]), 1.0))
    flat = lambda t: t.rearrange("p s n -> p (s n)")
    raw, selr, idn = flat(tE[:])[:, 0:1024], flat(tE[:])[:, 1024:1280], flat(tE[:])[:, 1280:1408]
    loads = [(cA, io["L3_conv_A_log"].rearrange("(k p) a -> p (k a)", p=128)), (cD, io["L3_conv_D_param"].rearrange("(k p) -> p k", p=128)),
             (cm, io["low"][:, 2:4]),
             (raw, io["dtw"]), (selr, io["sel"].rearrange("p a b -> p (a b)")), (idn, io["ident"])]
    for b in range(NI):
        wD = ld.dma(act, R(D[32 * b:32 * b + 28, :]), dbl[b], z0)
    for dst, src in loads:
        w = lw.dma(sp, dst, src, slow=True)
    a = act.sig(lambda e: e.activation(cA, cA, ACT.Exp), w)
    wA = dve.sig(lambda e: e.tensor_scalar(cA, cA, -1.0, None, ALU.mult), a)
    t1, t2 = flat(tL[:])[:, 0:1024], flat(tU[:])[:, 0:1024]
    a = dve.sig(lambda e: e.tensor_copy(dtw[:], raw), w)
    a = dve.sig(lambda e: e.tensor_tensor(t1, raw, R(dtw[:]), ALU.subtract), a)
    a = dve.sig(lambda e: e.tensor_scalar(t1, t1, cm[:, 0:1], None, ALU.mult), a)
    a = dve.sig(lambda e: e.scalar_tensor_tensor(t2, R(dtw[:]), cm[:, 1:2], t1, ALU.mult, ALU.add), a)
    dve.sig(lambda e: e.tensor_copy(dtw[:], t2), a)
    dve.sig(lambda e: e.tensor_copy(sel[:].rearrange("p a b -> p (a b)"), selr))
    for k in range(8):
        w0 = dve.sig(lambda e, k=k: e.tensor_scalar(dg[:, k, :], idn, cD[:, k:k + 1], None, ALU.mult))

    rE, rL, rU, rX, rZ = Ring(tE, 3, w0), Ring(tL, 3, w0), Ring(tU, 3, w0), Ring(psX, 1), Ring(tZ, 2)
    act.do(lambda e: e.preload_act_table_set("natural_log_exp_and_others"))
    df, bf, cf = [None] * 3, [None] * 2, [None] * 2
    lz = [P.load("z0"), P.load("z1")]
    lo = [P.load("o0"), P.load("o1")]
    ready, stored, gated = {}, {}, {}
    units = [(n, h, a4, c) for n in range(NI) for h in range(2) for a4 in range(4) for c in range(8)]
    S = [{} for _ in units]
    as2 = lambda t, d: t if d < 2 else t.rearrange("p (w h) -> p w h", h=64)
    added = {}

    def step_a(m):
        n, h, a4, c = units[m]
        s, i = S[m], m % 3
        rows = slice(32 * n, 32 * n + 32)
        t = pe.sig(lambda e: e.matmul(psd[:, i, :], dtw[rows, 256 * a4 + 128 * h:256 * a4 + 128 * h + 128], part(D[rows, :], a4, c), start=True, stop=True), wD, w0, df[i])
        s["e"], s["E"], f = rE.take()
        s["x"] = act.sig(lambda e: e.activation(s["E"], psd[:, i, :], ACT.Exp), t, f)

    def step_b(m):
        s, i = S[m], m % 3
        E = s["E"]
        a = act.sig(lambda e: e.activation(E, E, ACT.Ln, bias=1.0), s["x"])
        s["d"] = df[i] = dve.sig(lambda e: e.scalar_tensor_tensor(E, E, 20.0, psd[:, i, :], ALU.min, ALU.max), a)

    def step_c(m):
        n, h, a4, c = units[m]
        s, k, j = S[m], 2 * a4 + h, m % 2
        E = s["E"]
        s["l"], L, f = rL.take()
        s["L"] = L
        s["a"] = act.sig(lambda e: e.activation(L, E, ACT.Exp, scale=cA[:, k:k + 1]), s["d"], wA, f)
        s["u"], G, f = rU.take()
        s["U"] = G
        u = part(U[:, 2 * a4 + h, :], n, c)
        s["p"] = pool.sig(lambda e: e.tensor_tensor(as2(G, n), as2(E, n), u, ALU.mult), s["d"], f)
        rE.free[s["e"]] = [s["p"], s["a"]]
        rows = slice(32 * a4, 32 * a4 + 32)
        s["tb"] = pe.sig(lambda e: e.matmul(psB[:, j, :], sel[rows, 0, :], part(D[rows, :], n, c), start=True, stop=True), bf[j])
        s["tc"] = pe.sig(lambda e: e.matmul(psC[:, j, :], sel[rows, 1, :], part(D[rows, :], n, c), start=True, stop=True), cf[j])

    def step_d(m):
        s, j = S[m], m % 2
        G = s["U"]
        s["b"] = bf[j] = dve.sig(lambda e: e.tensor_tensor(G, psB[:, j, :], G, ALU.mult), s["p"], s["tb"])

    def step_e(m):
        n, h, a4, c = units[m]
        s, j = S[m], m % 2
        L, G = s["L"], s["U"]
        init = 0.0 if c == 0 else S[m - 1]["U"][:, 511:512]
        q = dve.sig(lambda e: e.tensor_tensor_scan(G, L, G, init, ALU.mult, ALU.add), s["a"], s["b"], S[m - 1]["q"] if c else None)
        s["q"] = q
        if m:
            rU.free[S[m - 1]["u"]] = q

    def step_f(m):
        n, h, a4, c = units[m]
        s, j, z = S[m], m % 2, (2 * n + h) % 2
        L, G = s["L"], s["U"]
        y = cf[j] = dve.sig(lambda e: e.tensor_tensor(L, psC[:, j, :], G, ALU.mult), s["q"], s["tc"])
        s["y"] = y
        if m + 1 < len(units) and units[m + 1][3] == 0 or m + 1 == len(units):
            rU.free[s["u"]] = y

    def step_g(m):
        n, h, a4, c = units[m]
        s, z, L = S[m], (2 * n + h) % 2, S[m]["L"]
        o = part(acc[:, z, :], a4, c)
        need = ready[n, h, c] if a4 == 0 else None
        rL.free[s["l"]] = added[n, h] = pool.sig(lambda e: e.tensor_tensor(o, o, as2(L, a4), ALU.add), s["y"], need, added.get((n, h)))

    def start(n, h, c, a4):
        if a4 == 0:
            i, X, f = rX.take()
            ready["X"] = i, X
            pe.wait(f, w0)
        i, X = ready["X"]
        ready["t"] = pe.sig(lambda e: e.matmul(X, dg[:, 2 * a4 + h, :], part(U[:, 2 * a4 + h, :], n ^ a4, c), start=(a4 == 0), stop=(a4 == 3)))

    def keep(n, h, c):
        z = (2 * n + h) % 2
        i, X = ready["X"]
        ready[n, h, c] = rX.free[i] = act.sig(lambda e: e.activation(acc[:, z, 512 * c:512 * c + 512], X, ACT.Copy), ready["t"], stored.get((2 * n + h - 2, c)))

    def fetch(n, h, c):
        i, V, f = rZ.take()
        gated[n, h, c] = (i, V, lz[i].dma(sp, V, zs[n, h, :, 512 * c:512 * c + 512], f))

    def gate(n, h, c):
        i, V, t = gated[n, h, c]
        v = acc[:, (2 * n + h) % 2, 512 * c:512 * c + 512]
        y = rZ.free[i] = dve.sig(lambda e: e.tensor_tensor(v, v, V, ALU.mult), t, added[n, h])
        stored[2 * n + h, c] = lo[c % 2].dma(sp, yz[n, h, :, 512 * c:512 * c + 512], v, y)

    sched = {}
    steps = ((4, 0, step_g), (3, 0, step_d), (1, 1, step_b), (2, 2, step_c), (3, 3, step_e), (0, 4, step_a), (3, 6, step_f))
    for k in range(2 * NI + 1):
        n, h, t0 = k // 2, k % 2, 32 * k
        for c in range(8):
            if k < 2 * NI:
                t = c + 1 if k == 0 else t0 - 22 + 2 * c
                for a4 in range(4):
                    sched.setdefault(t - 1 if k == 0 else t - 2 + a4 // 2, []).append((30, start, n, h, c, a4))
                sched.setdefault(t, []).append((3.5, keep, n, h, c))
            if k >= 1:
                sched.setdefault(t0 + 3 + 2 * c, []).append((20, fetch, (k - 1) // 2, (k - 1) % 2, c))
                sched.setdefault(t0 + 5 + 2 * c, []).append((21, gate, (k - 1) // 2, (k - 1) % 2, c))
    for m in range(len(units)):
        for lag, order, f in steps:
            sched.setdefault(m + lag, []).append((order, f, m))
    for at in sorted(sched):
        for _, f, *args in sorted(sched[at], key=lambda x: x[0]):
            f(*args)
    sp.wait(*((x.sem, x.n) for x in lo))
    P.run()


def finish3(nc, P, io, yz, out):
    pe, act, dve, pool, sp = P.pe, P.act, P.dve, P.pool, P.sp
    wo, gw, ob = P.sb("wo", [128, 2, 128]), P.sb("gw", [128, 2, 128]), P.sb("ob", [128, 2, 128])
    bw, mean, one = P.sb("bw", [128, 128]), P.sb("mean", [128, 128]), P.sb("one", [128, 128])
    cg = P.sb("cg", [128, 4])
    y = P.sb("y", [128, 3, 2, TOK])
    sq = P.sb("sq", [128, 3, 2, 512])
    rs = P.sb("rs", [128, 2, 3, 32])
    os = P.sb("os", [128, 3, 512])
    psM = P.ps("M", [128, 3, 512])
    psV = P.ps("V", [128, 2, 512])
    psO = P.ps("O", [128, 3, 512])
    lw = P.load("w")
    for dst, src in ((cg[:, 0:2], io["L3_conv_gamma"].rearrange("(h p) -> p h", p=128)), (cg[:, 2:4], io["L3_conv_beta"].rearrange("(h p) -> p h", p=128)),
                     (wo[:], io["L3_conv_Wout"].rearrange("(h p) d -> p h d", p=128))):
        w = lw.dma(sp, dst, src, slow=True)
    ly = [[P.load("y") for _ in range(4)] for _ in range(3)]
    lo = [P.load("o") for _ in range(3)]
    m = dve.sig(lambda e: e.memset(one[:], 1.0))
    wm = dve.sig(lambda e: e.memset(mean[:], 1.0 / 256))
    for h in range(2):
        dve.sig(lambda e, h=h: e.tensor_scalar(gw[:, h, :], wo[:, h, :], cg[:, h:h + 1], None, ALU.mult), w)
        g = dve.sig(lambda e, h=h: e.tensor_scalar(ob[:, h, :], one[:], cg[:, 2 + h:3 + h], None, ALU.mult), m)
    pe.do(lambda e: e.matmul(psV[:, 0, 0:128], ob[:, 0, :], wo[:, 0, :], start=True, stop=False), g, w)
    t = pe.sig(lambda e: e.matmul(psV[:, 0, 0:128], ob[:, 1, :], wo[:, 1, :], start=False, stop=True))
    g = dve.sig(lambda e: e.tensor_copy(bw[:], psV[:, 0, 0:128]), t)
    rM, rO, rQ = Ring(psM, 3), Ring(psO, 3), Ring(sq[:].rearrange("p s h n -> p s (h n)"), 3)
    vf, of = [g, None], [None] * 3
    loaded, mu, cen, doneb, rst, sqr = {}, {}, {}, {}, {}, {}

    def load(b):
        for q in range(4):
            s = slice(1024 * q, 1024 * q + 1024)
            loaded[b, q] = ly[b % 3][q].dma(sp, y[:, b % 3, :, s], yz[b, :, :, s].rearrange("h p n -> p h n"), doneb.get(b - 3))

    def stage1(b, c):
        sl = slice(512 * c, 512 * c + 512)
        i, X, f = rM.take()
        pe.do(lambda e: e.matmul(X, mean[:], y[:, b % 3, 0, sl], start=True, stop=False), loaded[b, c // 2], wm, f)
        mu[b, c] = (i, X, pe.sig(lambda e: e.matmul(X, mean[:], y[:, b % 3, 1, sl], start=False, stop=True)))

    def stage2(b, c):
        sl = slice(512 * c, 512 * c + 512)
        i, X, t = mu[b, c]
        v = y[:, b % 3, :, sl]
        d = rM.free[i] = cen[b, c] = dve.sig(lambda e: e.tensor_tensor(v, v, X.rearrange("p (a n) -> p a n", a=1).broadcast_to([128, 2, 512]), ALU.subtract), t)
        k, Q, f = rQ.take()
        a = act.sig(lambda e: e.activation(Q.rearrange("p (h n) -> p h n", h=2), v, ACT.Square), d, f)
        sqr[b, c] = (k, Q, a)

    def stage2b(b, c):
        k, Q, a = sqr[b, c]
        for j in range(4):
            for h in range(2):
                g = lambda e, j=j, h=h: e.matmul(psV[:, b % 2, 4 * c + j:4 * c + j + 1], Q[:, 512 * h + 128 * j:512 * h + 128 * j + 128], mean[:, 0:1], start=(h == 0), stop=(h == 1))
                if h:
                    t = pe.sig(g)
                else:
                    pe.do(g, a, vf[b % 2])
        rQ.free[k] = t
        if c == 7:
            r = rs[:, b % 2]
            v2 = vf[b % 2] = dve.sig(lambda e: e.tensor_scalar(r[:, 0, :], psV[:, b % 2, 0:32], 1.0e-5, None, ALU.add), t)
            v2 = act.sig(lambda e: e.activation(r[:, 1, :], r[:, 0, :], ACT.Sqrt), v2)
            rst[b] = dve.sig(lambda e: e.reciprocal(r[:, 2, :], r[:, 1, :]), v2)

    def stage3(b, c):
        r = rs[:, b % 2]
        i, X, f = rO.take()
        for j in range(4):
            tk = slice(512 * c + 128 * j, 512 * c + 128 * j + 128)
            for h in range(2):
                g = lambda e, j=j, h=h, tk=tk: e.matmul(X[:, 128 * j:128 * j + 128], y[:, b % 3, h, tk], gw[:, h, :], start=(h == 0), stop=(h == 1))
                if h:
                    t = pe.sig(g)
                else:
                    pe.do(g, f, cen[b, c])
        if c == 7:
            doneb[b] = t
        o = (8 * b + c) % 3
        for j in range(4):
            d = dve.sig(lambda e, j=j: e.scalar_tensor_tensor(os[:, o, 128 * j:128 * j + 128], X[:, 128 * j:128 * j + 128], r[:, 2, 4 * c + j:4 * c + j + 1], bw[:],
                                                             ALU.mult, ALU.add), t, rst[b], of[o])
        rO.free[i] = d
        of[o] = lo[o].dma(sp, out[b, 8 * c:8 * c + 8].rearrange("(t r) c d -> (r c) t d", r=2), os[:, o, :].rearrange("p (t c) -> p t c", t=4), d)

    load(0)
    load(1)
    load(2)
    for g in range(8 * NI + 11):
        if g < 8 * NI:
            stage1(g // 8, g % 8)
        if 1 <= g <= 8 * NI:
            stage2((g - 1) // 8, (g - 1) % 8)
        if 2 <= g < 8 * NI + 2:
            stage2b((g - 2) // 8, (g - 2) % 8)
        if g >= 11:
            stage3((g - 11) // 8, (g - 11) % 8)
            if (g - 11) % 8 == 7 and (g - 11) // 8 + 3 < NI:
                load((g - 11) // 8 + 3)
    sp.wait(*of)
    P.run()


USED = ["x", "xT", "xqT", "ident", "rpbx", "group", "taps", "dtw", "sel", "wx28", "low"]
USED += ["L0_conv_" + k for k in ("qkv_w", "qkv_b", "proj_w", "proj_b", "g1_w", "g1_b", "g2_w", "g2_b")]
USED += ["L1_conv_" + k for k in ("gn_scale", "gn_bias", "wq", "bq", "wk", "bk", "wv", "bv", "wo", "bo")]
USED += ["L2_conv_" + k for k in ("W_left", "b_left", "W_right", "b_right", "W_gate", "b_gate", "W_eq", "b_eq", "W_out", "b_out", "ln_scale", "ln_bias")]
USED += ["L3_conv_" + k for k in ("Win", "conv_b", "Wxproj", "A_log", "D_param", "dt_bias", "gamma", "beta", "Wout")]


def layout3(a):
    o = {}
    o["taps"] = np.ascontiguousarray(a["L3_conv_conv_w"].reshape(256, 9).T)
    o["wx28"] = np.ascontiguousarray(a["L3_conv_Wxproj"][:, list(range(8)) * 3 + [8, 8, 9, 9]])
    dtw = np.zeros((NI, 32, NI, 256), np.float32)
    for k in range(3):
        dtw[:, 8 * k:8 * k + 8] = a["L3_conv_dt_weight"].transpose(0, 2, 1)[:, :, None]
    dtw[:, 28:30] = a["L3_conv_dt_bias"].reshape(NI, 256)
    o["dtw"] = dtw.reshape(128, NI * 256)
    sel = np.zeros((NI, 32, 2, 128), np.float32)
    sel[:, 24:26, 0] = 1.0
    sel[:, 26:28, 1] = 1.0
    o["sel"] = sel.reshape(128, 2, 128)
    low = np.zeros((128, 4), np.float32)
    low[[*range(8, 16), 25, 27], 0] = 1.0
    low.reshape(NI, 32, 4)[:, 16:24, 2] = 1.0
    low[29::32, 2] = 1.0
    low[:, 1::2] = 1.0 - low[:, 0::2]
    o["low"] = low
    o["ident"] = np.eye(128, dtype=np.float32)
    return o


def layout(inputs):
    a = {k: np.asarray(v) for k, v in inputs.items()}
    a["xT"] = np.ascontiguousarray(a["x"].reshape(NI, TOK, C).transpose(0, 2, 1))
    a["xqT"] = np.ascontiguousarray(a["x"].reshape(NI, 8, 8, 4, 16, C).transpose(0, 5, 1, 3, 2, 4).reshape(NI, C, TOK))
    rpb = np.pad(a["L0_conv_rpb"].reshape(4, 169), ((0, 0), (0, 1)), constant_values=-1.0e30)
    q = np.arange(128)
    key = np.arange(308)
    rp = []
    for dr in (0, 3, 6):
        for dc in (0, 3, 6):
            def axis(d, n, size):
                i = np.arange(n) + d
                start = {0: np.maximum(i - 3, 0), 3: i - 3, 6: np.minimum(i - 3, size - 7)}[d]
                return i, start
            ri, rs = axis(dr, 8, 14)
            ci, cs = axis(dc, 16, 22)
            qi, qs, pi, ps = ri[q // 16], rs[q // 16], ci[q % 16], cs[q % 16]
            kr, kc = key // 22, key % 22
            inside = ((kr >= qs[:, None]) & (kr < qs[:, None] + 7) & (kc >= ps[:, None]) & (kc < ps[:, None] + 7))
            br = np.clip(kr[None] - qi[:, None] + 6, 0, 12)
            bc = np.clip(kc[None] - pi[:, None] + 6, 0, 12)
            rp.append(rpb[:, np.where(inside, 13 * br + bc, 169)])
    a["rpbx"] = np.ascontiguousarray(np.concatenate(rp))
    a["group"] = (np.kron(np.eye(32), np.ones((4, 4))) / 4).astype(np.float32)
    a.update(layout3(a))
    a["ident"] = np.eye(128, dtype=np.float32)
    return a


def program(nc, io, out):
    global SEMS
    x1 = nc.dram_tensor("x1", [NI, HW, HW, C], F32).ap()
    x1t = nc.dram_tensor("x1t", [NI, C, TOK], F32).ap()
    x2 = nc.dram_tensor("x2", [NI, HW, HW, C], F32).ap()
    x3t = nc.dram_tensor("x3t", [NI, C, TOK], F32).ap()
    vs = nc.dram_tensor("vs", [NI, HW, HW, C], F32).ap()
    hls = nc.dram_tensor("hls", [8, 2, C, 512], F32).ap()
    dbl = nc.dram_tensor("dbl", [NI, 28, TOK], F32).ap()
    zs = nc.dram_tensor("zs", [NI, 2, C, TOK], F32).ap()
    yz = nc.dram_tensor("yz", [NI, 2, C, TOK], F32).ap()
    with ExitStack() as SEMS:
        with ExitStack() as ctx:
            layer0(nc, Phase(nc, ctx, "l0"), io, vs, hls, x1)
        with ExitStack() as ctx:
            layer1(nc, Phase(nc, ctx, "l1"), io, x1, x1t, x2)
        with ExitStack() as ctx:
            layer2(nc, Phase(nc, ctx, "l2"), io, x2, x3t)
        with ExitStack() as ctx:
            layer3(nc, ctx, io, x3t, dbl, zs, yz)
        with ExitStack() as ctx:
            finish3(nc, Phase(nc, ctx, "l3c"), io, yz, out)


def kernel(**inputs):
    import concourse.bacc as bacc
    from concourse.bass_utils import run_bass_kernel_spmd

    a = layout(inputs)
    nc = bacc.Bacc("TRN2", target_bir_lowering=False, num_devices=1)
    arrays, io = {}, {}
    for name in USED:
        v = np.ascontiguousarray(a[name])
        arrays[f"in_{name}"] = v
        io[name] = nc.dram_tensor(f"in_{name}", v.shape, mybir.dt.from_np(v.dtype), kind="ExternalInput").ap()
    out = nc.dram_tensor("out_0", (NI, HW, HW, C), F32, kind="ExternalOutput").ap()
    program(nc, io, out)
    r = run_bass_kernel_spmd(nc, [arrays], core_ids=[0])
    return r.results[0]["out_0"]
```
